# Optimizing a Trainium2 kernel written in Bass

```python
import numpy as np
import jax
import jax.numpy as jnp

def _softmax(x, axis=-1):
    return jax.nn.softmax(x, axis=axis)

def _gelu(x):
    return jax.nn.gelu(x, approximate=True)

def _silu(x):
    return jax.nn.silu(x)

def _sigmoid(x):
    return jax.nn.sigmoid(x)

def _layernorm(x, axis=-1, eps=1e-05):
    m = jnp.mean(x, axis=axis, keepdims=True)
    v = jnp.var(x, axis=axis, keepdims=True)
    return (x - m) / jnp.sqrt(v + eps)

def _scatter_add(tgt, idx, src, axis=0):
    return tgt.at[idx].add(src)

def _segment_sum(src, seg, n):
    return jax.ops.segment_sum(src, seg, n)
kernel_name = 'mk_early_fusion_d1_tok_img1024_r4_b0065a'

def setup_inputs(seed: int=0):
    np.random.seed(seed)
    _w = jnp.asarray

    def _rec_inputs():
        import jax
        import jax.numpy as jnp
        _rk = jax.random.key(seed)
        x = -0.00016672 + 0.999947 * jax.random.normal(jax.random.fold_in(_rk, 1), (16, 3, 112, 112), jnp.float32)
        txt = 8.24161e-11 + 0.999995 * jax.random.normal(jax.random.fold_in(_rk, 2), (16, 32, 256), jnp.float32)
        return (x, txt)
    x, txt = _rec_inputs()

    def _L0_tok_setup():
        import jax, jax.numpy as jnp
        import numpy as np
        P = 16
        EPS = 1e-05

        def _layernorm(x, g, b):
            mu = jnp.mean(x, axis=-1, keepdims=True)
            var = jnp.mean(jnp.square(x - mu), axis=-1, keepdims=True)
            return (x - mu) * jax.lax.rsqrt(var + EPS) * g + b
        key = jax.random.key(seed)
        ks = jax.random.split(key, 7)
        B, C, H, W = (64, 3, 96, 96)
        patch_dim = C * P * P
        out_dim = 256
        x = jax.random.normal(ks[0], (B, C, H, W), dtype=jnp.float32)
        Wp = jax.random.normal(ks[1], (patch_dim, out_dim), dtype=jnp.float32) * (1.0 / np.sqrt(patch_dim))
        bp = jax.random.normal(ks[2], (out_dim,), dtype=jnp.float32) * 0.01
        ln1_g = jnp.ones((patch_dim,), dtype=jnp.float32)
        ln1_b = jnp.zeros((patch_dim,), dtype=jnp.float32)
        ln2_g = jnp.ones((out_dim,), dtype=jnp.float32)
        ln2_b = jnp.zeros((out_dim,), dtype=jnp.float32)
        return {'x': x, 'Wp': Wp, 'bp': bp, 'ln1_g': ln1_g, 'ln1_b': ln1_b, 'ln2_g': ln2_g, 'ln2_b': ln2_b}
    _L0_tok_all = _L0_tok_setup()
    _L0_tok_in = {k: v for k, v in _L0_tok_all.items() if k in ('Wp', 'bp', 'ln1_g', 'ln1_b', 'ln2_g', 'ln2_b')}
    del _L0_tok_all

    def _L0_attn_setup():
        import jax, jax.numpy as jnp
        import numpy as np
        B, S, D_MODEL, H, D = (2, 512, 256, 16, 64)
        SCALE = 1.0 / float(np.sqrt(D))

        def _rope(t, c, s):
            d2 = t.shape[-1] // 2
            t1, t2 = (t[..., :d2], t[..., d2:])
            return jnp.concatenate([t1 * c - t2 * s, t1 * s + t2 * c], axis=-1)
        key = jax.random.key(seed)
        ks = jax.random.split(key, 5)
        x = jax.random.normal(ks[0], (B, S, D_MODEL), jnp.float32)
        qkv_w = jax.random.normal(ks[1], (3 * H * D, D_MODEL), jnp.float32) * 0.02
        out_w = jax.random.normal(ks[2], (D_MODEL, H * D), jnp.float32) * 0.02
        bias_p = jax.random.uniform(ks[3], (H, 1, 1), jnp.float32) * 2.0
        bias_a = jax.random.uniform(ks[4], (H, 1, 1), jnp.float32)
        rope_freqs = 10000.0 ** (-jnp.arange(D // 2, dtype=jnp.float32) / (D // 2))
        return {'x': x, 'qkv_w': qkv_w, 'out_w': out_w, 'bias_p': bias_p, 'bias_a': bias_a, 'rope_freqs': rope_freqs}
    _L0_attn_all = _L0_attn_setup()
    _L0_attn_in = {k: v for k, v in _L0_attn_all.items() if k in ('qkv_w', 'out_w', 'bias_p', 'bias_a', 'rope_freqs')}
    del _L0_attn_all

    def _L0_ffn_setup():
        import jax, jax.numpy as jnp
        import numpy as np
        BLOCK = 32
        W_BITS = 4
        ACT_BITS = 16

        def act_qdq(x):
            qmax = 2.0 ** (ACT_BITS - 1) - 1.0
            scale = jnp.maximum(jnp.max(jnp.abs(x)) / qmax, 1e-12)
            return jnp.clip(jnp.round(x / scale), -qmax - 1.0, qmax) * scale

        def fixed_qdq_u16(x):
            scale = 1.0 / 65536.0
            return jnp.clip(jnp.round(x / scale), 0.0, 65535.0) * scale

        def lpbq_dequant(w):
            O, I = w.shape
            qmax = 2.0 ** (W_BITS - 1) - 1.0
            wb = w.reshape(O, I // BLOCK, BLOCK)
            s = jnp.maximum(jnp.max(jnp.abs(wb), axis=-1, keepdims=True) / qmax, 1e-12)
            wq = jnp.clip(jnp.round(wb / s), -qmax - 1.0, qmax) * s
            return wq.reshape(O, I)
        key = jax.random.key(seed)
        k1, k2, k3, k4 = jax.random.split(key, 4)
        B, S, H, I = (2, 1024, 256, 768)
        x = jax.random.normal(k1, (B, S, H), jnp.float32)
        w_gate = jax.random.normal(k2, (I, H), jnp.float32) * 0.02
        w_up = jax.random.normal(k3, (I, H), jnp.float32) * 0.02
        w_down = jax.random.normal(k4, (H, I), jnp.float32) * 0.02
        return {'x': x, 'w_gate': w_gate, 'w_up': w_up, 'w_down': w_down}
    _L0_ffn_all = _L0_ffn_setup()
    _L0_ffn_in = {k: v for k, v in _L0_ffn_all.items() if k in ('w_gate', 'w_up', 'w_down')}
    del _L0_ffn_all
    return {'x': x, 'txt': txt, 'L0_tok_Wp': _L0_tok_in['Wp'], 'L0_tok_bp': _L0_tok_in['bp'], 'L0_tok_ln1_g': _L0_tok_in['ln1_g'], 'L0_tok_ln1_b': _L0_tok_in['ln1_b'], 'L0_tok_ln2_g': _L0_tok_in['ln2_g'], 'L0_tok_ln2_b': _L0_tok_in['ln2_b'], 'L0_attn_qkv_w': _L0_attn_in['qkv_w'], 'L0_attn_out_w': _L0_attn_in['out_w'], 'L0_attn_bias_p': _L0_attn_in['bias_p'], 'L0_attn_bias_a': _L0_attn_in['bias_a'], 'L0_attn_rope_freqs': _L0_attn_in['rope_freqs'], 'L0_ffn_w_gate': _L0_ffn_in['w_gate'], 'L0_ffn_w_up': _L0_ffn_in['w_up'], 'L0_ffn_w_down': _L0_ffn_in['w_down']}

def reference(x, txt, L0_tok_Wp, L0_tok_bp, L0_tok_ln1_g, L0_tok_ln1_b, L0_tok_ln2_g, L0_tok_ln2_b, L0_attn_qkv_w, L0_attn_out_w, L0_attn_bias_p, L0_attn_bias_a, L0_attn_rope_freqs, L0_ffn_w_gate, L0_ffn_w_up, L0_ffn_w_down):
    import jax
    import jax.numpy as jnp

    def _L0_tok_ref(x, Wp, bp, ln1_g, ln1_b, ln2_g, ln2_b):
        import jax, jax.numpy as jnp
        import numpy as np
        P = 16
        EPS = 1e-05

        def _layernorm(x, g, b):
            mu = jnp.mean(x, axis=-1, keepdims=True)
            var = jnp.mean(jnp.square(x - mu), axis=-1, keepdims=True)
            return (x - mu) * jax.lax.rsqrt(var + EPS) * g + b
        B, C, H, W = x.shape
        h, w = (H // P, W // P)
        patches = x.reshape(B, C, h, P, w, P)
        patches = jnp.transpose(patches, (0, 2, 4, 3, 5, 1))
        patches = patches.reshape(B, h * w, P * P * C)
        y = _layernorm(patches, ln1_g, ln1_b)
        y = jnp.einsum('bnd,de->bne', y, Wp) + bp
        y = _layernorm(y, ln2_g, ln2_b)
        return y

    def _L0_attn_ref(x, qkv_w, out_w, bias_p, bias_a, rope_freqs):
        import jax, jax.numpy as jnp
        import numpy as np
        B, S, D_MODEL, H, D = (2, 512, 256, 16, 64)
        SCALE = 1.0 / float(np.sqrt(D))

        def _rope(t, c, s):
            d2 = t.shape[-1] // 2
            t1, t2 = (t[..., :d2], t[..., d2:])
            return jnp.concatenate([t1 * c - t2 * s, t1 * s + t2 * c], axis=-1)
        Bb, Ss, _ = x.shape
        qkv = (x @ qkv_w.T).reshape(Bb, Ss, 3, H, D)
        q = qkv[:, :, 0].transpose(0, 2, 1, 3)
        k = qkv[:, :, 1].transpose(0, 2, 1, 3)
        v = qkv[:, :, 2].transpose(0, 2, 1, 3)
        pos = jnp.arange(Ss, dtype=jnp.float32)
        ang = pos[:, None] * rope_freqs[None, :]
        c = jnp.cos(ang)[None, None]
        s = jnp.sin(ang)[None, None]
        q = _rope(q, c, s)
        k = _rope(k, c, s)
        scores = jnp.einsum('bhqd,bhkd->bhqk', q, k) * SCALE
        p = jnp.maximum(bias_p, 0.01)
        a = jnp.maximum(bias_a, 0.01)
        dist = jnp.abs(pos[None, :] - pos[:, None])
        kb = -p * jnp.log1p(a * dist)
        attn = jax.nn.softmax(scores + kb[None], axis=-1)
        out = jnp.einsum('bhqk,bhkd->bhqd', attn, v)
        out = out.transpose(0, 2, 1, 3).reshape(Bb, Ss, H * D)
        return out @ out_w.T

    def _L0_ffn_ref(x, w_gate, w_up, w_down):
        import jax, jax.numpy as jnp
        import numpy as np
        BLOCK = 32
        W_BITS = 4
        ACT_BITS = 16

        def act_qdq(x):
            qmax = 2.0 ** (ACT_BITS - 1) - 1.0
            scale = jnp.maximum(jnp.max(jnp.abs(x)) / qmax, 1e-12)
            return jnp.clip(jnp.round(x / scale), -qmax - 1.0, qmax) * scale

        def fixed_qdq_u16(x):
            scale = 1.0 / 65536.0
            return jnp.clip(jnp.round(x / scale), 0.0, 65535.0) * scale

        def lpbq_dequant(w):
            O, I = w.shape
            qmax = 2.0 ** (W_BITS - 1) - 1.0
            wb = w.reshape(O, I // BLOCK, BLOCK)
            s = jnp.maximum(jnp.max(jnp.abs(wb), axis=-1, keepdims=True) / qmax, 1e-12)
            wq = jnp.clip(jnp.round(wb / s), -qmax - 1.0, qmax) * s
            return wq.reshape(O, I)
        x = act_qdq(x)
        up = act_qdq(x @ lpbq_dequant(w_up).T)
        gate = act_qdq(x @ lpbq_dequant(w_gate).T)
        sig = fixed_qdq_u16(jax.nn.sigmoid(gate))
        gate = act_qdq(gate * sig)
        o = act_qdq(gate * up)
        return o @ lpbq_dequant(w_down).T
    h = _L0_tok_ref(x, L0_tok_Wp, L0_tok_bp, L0_tok_ln1_g, L0_tok_ln1_b, L0_tok_ln2_g, L0_tok_ln2_b)
    h = jnp.concatenate([h, txt], axis=1)
    h = h + _L0_attn_ref(_layernorm(h, axis=-1), L0_attn_qkv_w, L0_attn_out_w, L0_attn_bias_p, L0_attn_bias_a, L0_attn_rope_freqs)
    h = h + _L0_ffn_ref(_layernorm(h, axis=-1), L0_ffn_w_gate, L0_ffn_w_up, L0_ffn_w_down)
    return h

_drawn_inputs = setup_inputs


def setup_inputs(seed=0):
    import zlib

    import numpy as np

    out = dict(_drawn_inputs(seed))
    spreads = {'L0_tok_ln1_g': (1.0, 0.2),
     'L0_tok_ln1_b': (0.0, 0.1),
     'L0_tok_ln2_g': (1.0, 0.2),
     'L0_tok_ln2_b': (0.0, 0.1)}
    factors = {'L0_tok_bp': 7.214, 'L0_attn_rope_freqs': 8.0}
    for name, (base, spread) in spreads.items():
        noise = np.random.default_rng([zlib.crc32(name.encode()), seed]).standard_normal(out[name].shape)
        drawn = base * np.exp(spread * noise) if base else spread * noise
        out[name] = jnp.asarray(drawn.astype(out[name].dtype))
    for name, factor in factors.items():
        out[name] = (out[name] * factor).astype(out[name].dtype)
    return out
```

```python
from contextlib import ExitStack

import numpy as np
import concourse.bass as bass
from concourse import mybir

F32 = mybir.dt.float32
F32R = mybir.dt.float32r
I32 = mybir.dt.int32
ACT = mybir.ActivationFunctionType
ALU = mybir.AluOpType
AXX = mybir.AxisListType.X

P = 128
BATCHES, CHANNELS, IMG, PATCH = 16, 3, 112, 16
SIDE = IMG // PATCH
IMG_TOK = SIDE * SIDE
TXT_TOK = 32
TOK = IMG_TOK + TXT_TOK
FEAT = PATCH * PATCH * CHANNELS
FEAT_T = FEAT // P
DM = 256
DM_T = DM // P
HEADS, HD = 16, 64
HALF = HD // 2
INNER = HEADS * HD
INNER_T = INNER // P
FFN = 768
FFN_T = FFN // P
GROUP = 4
GROUPS = BATCHES // GROUP
GTOK = GROUP * TOK
UNITS = 4
UHEADS = HEADS // UNITS
STEPS = 2 * UNITS
SLOTS = STEPS + 2
ITEMS = 8
TOK_TILES = BATCHES // 2
SEAT = 64
TILE_ROWS = SEAT + IMG_TOK
QBLOCK = 32
QT = 2 * FFN_T
QBLOCKS = (QT * DM + DM_T * FFN) // QBLOCK

EPS = 1e-5
SCORE_SCALE = 1.0 / float(np.sqrt(HD))
WMAX = 7.0
ACTMAX = 32767.0
SIGLEVELS = 65536.0
TINY = 1e-12
RINT = 12582912.0
PI = 3.1415925
TWO_PI = 2.0 * float(np.pi)
PI_A = 6.28125
PI_B = float(np.float32(np.round((TWO_PI - PI_A) * 2.0**21) / 2.0**21))
PI_C = float(np.float32(TWO_PI - PI_A - PI_B))

BANK_S = 0
BANK_PT = 2
BANK_O = 4
BANK_PJ = 6


def build(nc, patches, txt, wp, bp, g1, b1, g2, b2, wqkv, wo, bias_p, bias_a, freqs, wgu, wdn, out):
    ctx = ExitStack()
    with ctx:
        def sb(name, shape, dt=F32, where=ctx):
            return where.enter_context(nc.sbuf_tensor(name, shape, dt))

        ident = sb("ident", [P, P])
        ones = sb("ones", [P, P])
        neg_half = sb("neg_half", [P, BATCHES])
        h = sb("h", [P, BATCHES, DM])
        ffn_x = sb("ffn_x", [P, DM_T, BATCHES * TOK])
        wq = sb("wq", [P, QT * DM + DM_T * FFN])
        xmax = sb("xmax", [P, GROUPS])
        gred = sb("gred", [P, 5])
        gall = sb("gall", [P, 5])
        scal = sb("scal", [P, 16])

        wq_gu = wq[:, 0:QT * DM].rearrange("p (t i) -> p t i", t=QT)
        wq_dn = wq[:, QT * DM:].rearrange("p (t i) -> p t i", t=DM_T)

        att = ExitStack()
        wqkv_h = sb("wqkv_h", [P, DM_T, 3 * INNER], F32R, att)
        wqkv_l = sb("wqkv_l", [P, DM_T, 3 * INNER], F32R, att)
        wo_h = sb("wo_h", [P, INNER_T, DM], F32R, att)
        wo_l = sb("wo_l", [P, INNER_T, DM], F32R, att)
        rope_c = sb("rope_c", [P, 2, TOK], where=att)
        rope_s = sb("rope_s", [P, 2, TOK], where=att)
        kbias = sb("kbias", [P, HEADS, TOK], where=att)







        v = sb("v", [P, 2, GROUP, UHEADS, HD + 1], where=att)

        pro = ExitStack()
        xin = sb("xin", [P, TOK_TILES, FEAT], where=pro)
        xnt = sb("xnt", [P, 2, FEAT_T, P], where=pro)
        xnorm = sb("xnorm", [P, 2, FEAT], where=pro)
        ytok = sb("ytok", [P, TOK_TILES, DM], where=pro)
        wp_sb = sb("wp_sb", [P, FEAT_T, DM], where=pro)
        bp_sb = sb("bp_sb", [1, DM], where=pro)
        bias_tok = sb("bias_tok", [1, DM], where=pro)
        g1_sb = sb("g1_sb", [P, FEAT_T], where=pro)
        b1_sb = sb("b1_sb", [P, FEAT_T], where=pro)
        g2_sb = sb("g2_sb", [P, DM], where=pro)
        b2_sb = sb("b2_sb", [P, DM], where=pro)
        stat1 = sb("stat1", [P, TOK_TILES, 2, 6], where=pro)
        mv1 = sb("mv1", [P, TOK_TILES, 2], where=pro)
        rstd1 = sb("rstd1", [P, TOK_TILES], where=pro)
        stat2 = sb("stat2", [P, TOK_TILES, 6], where=pro)
        mv2 = sb("mv2", [P, TOK_TILES, 2], where=pro)
        rstd2 = sb("rstd2", [P, TOK_TILES], where=pro)
        wraw = sb("wraw", [P, 3 * INNER], where=pro)
        qmax = sb("qmax", [P, QBLOCKS], where=pro)
        qinv = sb("qinv", [P, QBLOCKS], where=pro)
        freq = sb("freq", [P, 1], where=pro)
        sign = sb("sign", [P, 1], where=pro)
        pos_i = sb("pos_i", [P, TOK], I32, pro)
        dist_i = sb("dist_i", [P, TOK], I32, pro)
        dist = sb("dist", [P, TOK], where=pro)
        ang = sb("ang", [P, 4, TOK], where=pro)
        bias_ps = sb("bias_ps", [P, HEADS], where=pro)
        bias_as = sb("bias_as", [P, HEADS], where=pro)
        pro.close()

        xh = sb("xh", [P, DM_T, GTOK], F32R, att)
        xl = sb("xl", [P, DM_T, GTOK], F32R, att)
        xn = sb("xn", [P, GROUP, DM], where=att)
        xn2 = sb("xn2", [P, GROUP, DM], where=att)
        stat = sb("stat", [P, GROUP, 6], where=att)
        mv = sb("mv", [P, GROUP, 2], where=att)
        rstd = sb("rstd", [P, GROUP], where=att)
        stat_f = sb("stat_f", [P, GROUP, 6], where=att)
        mv_f = sb("mv_f", [P, GROUP, 2], where=att)
        rstd_f = sb("rstd_f", [P, GROUP], where=att)
        rs = sb("rs", [P, 2, UHEADS, GTOK], where=att)
        rsx = sb("rsx", [P, 2, UHEADS, GTOK], where=att)
        qk = sb("qk", [P, 2, UHEADS, GTOK], where=att)
        s = sb("s", [P, 2, 2 * UHEADS, TOK], where=att)
        nmax = sb("nmax", [P, 2, 2 * UHEADS], where=att)
        pr = sb("pr", [P, 2, 2 * UHEADS, TOK], where=att)
        pt = sb("pt", [P, 2, UHEADS, TOK], where=att)
        rsum = sb("rsum", [P, 2, UHEADS], where=att)
        on = sb("on", [P, 2, UHEADS * HD], where=att)
        oth = sb("oth", [P, INNER_T, GTOK], F32R, att)
        otl = sb("otl", [P, INNER_T, GTOK], F32R, att)
        att.close()

        wgu_h = sb("wgu_h", [P, DM_T, QT * P], F32R)
        wgu_l = sb("wgu_l", [P, DM_T, QT * P], F32R)
        wdn_h = sb("wdn_h", [P, FFN_T, DM], F32R)
        wdn_l = sb("wdn_l", [P, FFN_T, DM], F32R)
        yt = sb("yt", [P, DM_T, GTOK])
        maxes = sb("maxes", [P, 4, 2 * GROUPS])
        gate = sb("gate", [P, GROUPS, FFN_T * GTOK])
        fx = ExitStack()
        fxh = sb("fxh", [P, DM_T, BATCHES * TOK], F32R, fx)
        fxl = sb("fxl", [P, DM_T, BATCHES * TOK], F32R, fx)
        up = sb("up", [P, GROUPS, FFN_T * GTOK], where=fx)
        sig = sb("sig", [P, GROUPS, FFN_T * GTOK], where=fx)
        fx.close()
        fy = ExitStack()
        fo_h = sb("fo_h", [P, GROUPS, FFN_T * GTOK], F32R, fy)
        fo_l = sb("fo_l", [P, GROUPS, FFN_T * GTOK], F32R, fy)
        fy.close()

        ps = ctx.enter_context(nc.psum_tensor("ps", [P, 8, 512], F32))

        names = (
            "txt_in wp_in small_in wqkv_in ffnw_in out_stored "
            "consts iotas ident_ready tok_stats tok_rstd tok_normed tok_transposed tok_evac tok_product "
            "tok_y tok_stats2 tok_rstd2 tok_placed bias_product angles_ready sines_ready logs_ready "
            "tables_ready high_ready low_ready vstep prologue_v prologue_a "
            "ln_stats ln_rstd x_normed x_transposed xh_ready xl_ready proj_done roped swapped0 swapped1 "
            "qk_ready v_ready scores_done biased maxed exped p_transposed pt_ready_v pt_ready_a pv_done "
            "o_summed o_normed o_transposed oth_ready otl_ready ao_done h_added ln2_stats ln2_rstd x2_normed "
            "x2_transposed x2_copied xmax_ready "
            "fstep fw_transposed fw_high fw_low max_ready max_shared scales_ready fx_t fx_ready gu_done gu_maxed "
            "gu_copied gate_t gate_q sig_done sig_t sig_q g2_ready g2_maxed up_t up_q g2_t o_ready o_maxed o_t "
            "fo_ready down_done yt_ready yt_transposed y_added"
        ).split()
        S = {n: ctx.enter_context(nc.semaphore(n)) for n in names}
        patches_in = [ctx.enter_context(nc.semaphore(f"patches_in{t}")) for t in range(TOK_TILES)]
        block = ctx.enter_context(nc.Block())

        PER = dict(
            ln_stats=2 * GROUP + 1, ln_rstd=1, x_normed=GROUP, x_transposed=1, xh_ready=1, xl_ready=1,
            proj_done=UNITS * ITEMS, roped=UNITS * UHEADS, swapped0=UNITS // 2 * 64, swapped1=UNITS // 2 * 64,
            qk_ready=UNITS * UHEADS, v_ready=UNITS * GROUP, scores_done=STEPS, biased=STEPS, maxed=STEPS,
            exped=STEPS, p_transposed=2 * STEPS, pt_ready_v=STEPS, pt_ready_a=STEPS, pv_done=2 * STEPS,
            o_summed=2 * STEPS, o_normed=2 * STEPS, o_transposed=2 * STEPS, oth_ready=2 * STEPS,
            otl_ready=2 * STEPS, ao_done=GROUP, h_added=GROUP, ln2_stats=2 * GROUP + 1, ln2_rstd=1,
            x2_normed=GROUP, x2_transposed=1, x2_copied=1, xmax_ready=1,
            tok_normed=2, tok_transposed=2, tok_evac=2, tok_product=2, tok_y=2, tok_stats2=2)
        SEEDS = dict(tok_transposed=2, tok_product=2, tok_evac=2, tok_y=2, biased=1, exped=2, p_transposed=4,
                     pt_ready_v=1, pt_ready_a=1, pv_done=6, o_transposed=2, otl_ready=2, qk_ready=8,
                     scores_done=4, swapped0=16, swapped1=16, x2_copied=1, gu_copied=2, yt_transposed=1,
                     y_added=1)

        def at(i, name, n):
            return i * PER.get(name, 1) + (SEEDS.get(name, 0) + n)

        def apart(eng):
            eng.wait_ge(S["prologue_v"], 1)

        def items_of(n, half):
            unit = n // 2 + 1
            if n >= STEPS or unit >= UNITS:
                return []
            first = 4 * (n % 2) + 2 * half
            return [(unit, first), (unit, first + 1)]

        def item_bank(u, k):
            return BANK_PJ + k % 2

        def steps_view(ap, cols):
            return ap.rearrange("p (j x) -> p j x", j=cols)

        def o_t_view(jj):
            return ps[:, BANK_O + jj, OT_AT:OT_AT + 2 * TOK].rearrange("p (c x) -> p c x", c=2)

        def fill_view(r):
            return ps[:, r % 8, :]

        def weight_fill(gu, dn, r):
            if r < 2 * QT // 4:
                c, q = r // (QT // 4), r % (QT // 4)
                return gu[:, c, 512 * q:512 * q + 512]
            m = 2 * (r - 2 * QT // 4)
            return dn[:, m:m + 2, :].rearrange("p m d -> p (m d)")

        def over(ap, n, rows=slice(0, P)):
            return ap[rows, :].unsqueeze(1).broadcast_to([rows.stop - rows.start, n, DM])

        @block.sync
        def _(sp):
            flat = patches.rearrange("b t f -> (b t) f")
            for b in range(BATCHES):
                rows = min(SEAT, (BATCHES - b) * IMG_TOK)
                seat = SEAT * (b % 2)
                sp.dma_start(xin[seat:seat + rows, b // 2, :],
                             flat[b * IMG_TOK:b * IMG_TOK + rows, :]).then_inc(patches_in[b // 2], 16)
                if rows < SEAT:
                    sp.dma_start(xin[seat + rows:seat + SEAT, b // 2, :],
                                 flat[0:SEAT - rows, :]).then_inc(patches_in[b // 2], 16)
            sp.dma_start(h[IMG_TOK:TOK, :, :], txt.rearrange("b t d -> t b d")).then_inc(S["txt_in"], 16)

            sp.wait_ge(S["prologue_v"], 1)
            sp.wait_ge(S["prologue_a"], 1)
            with sp.Fori(0, GROUPS, 1) as g:
                for u in range(UNITS):
                    swapped = f"swapped{u % 2}"
                    sp.wait_ge(S["roped"], at(g, "roped", UHEADS * (u + 1)))
                    sp.wait_ge(S["qk_ready"], at(g, "qk_ready", UHEADS * (u - 1)))
                    for q in range(4):
                        sp.dma_start(rsx[32 * q:32 * q + 32, u % 2], rs[32 * (q ^ 1):32 * (q ^ 1) + 32, u % 2]) \
                            .then_inc(S[swapped], 16)

            out_g = out.rearrange("(g j) t d -> g t j d", g=GROUPS)
            with sp.Fori(0, GROUPS, 1) as g:
                sp.wait_ge(S["y_added"], at(g, "y_added", 1))
                sp.dma_start(out_g[g], h[0:TOK, bass.ts(g, GROUP), :]).then_inc(S["out_stored"], 16)
            sp.wait_ge(S["out_stored"], 16 * GROUPS)

        @block.gpsimd
        def _(pool):
            for name, n in SEEDS.items():
                pool.sem_inc(S[name], n)
            nc.gpsimd.memset(neg_half[:, :], -0.5).then_inc(S["consts"], 1)
            nc.gpsimd.memset(ones[:, :], 1.0).then_inc(S["consts"], 1)
            nc.gpsimd.memset(v[:, :, :, :, HD:HD + 1].rearrange("p a j h c -> p (a j h) c"), 1.0) \
                .then_inc(S["consts"], 1)
            nc.gpsimd.iota(pos_i[:, :], [[1, TOK]], base=0, channel_multiplier=0).then_inc(S["iotas"], 1)
            nc.gpsimd.iota(dist_i[:, :], [[1, TOK]], base=0, channel_multiplier=-1).then_inc(S["iotas"], 1)
            pool.wait_ge(S["consts"], 3)
            nc.gpsimd.affine_select(out=ident[:, :], in_=ones[:, :], compare_op=ALU.is_equal, fill=0.0, base=0,
                                    pattern=[[-1, P]], channel_multiplier=1).then_inc(S["ident_ready"], 1)
            small = [(g1_sb[:, :], g1), (b1_sb[:, :], b1), (bp_sb[:, :], bp), (g2_sb[:, :], g2.broadcast_to([P, DM])),
                     (b2_sb[:, :], b2.broadcast_to([P, DM])), (bias_ps[:, :], bias_p.broadcast_to([P, HEADS])),
                     (bias_as[:, :], bias_a.broadcast_to([P, HEADS]))]
            small += [(freq[32 * q:32 * q + 32, :], freqs) for q in range(4)]
            assert len(small) == SMALLS
            for dst, src in small:
                pool.dma_start(dst, src).then_inc(S["small_in"], 16)
            pool.wait_ge(S["tok_stats"], 1)
            nc.gpsimd.tensor_tensor(rstd1[:, :], mv1[:, :, 1], neg_half[:, 0:TOK_TILES], ALU.pow) \
                .then_inc(S["tok_rstd"], 1)
            pool.wait_ge(S["tok_stats2"], 2 * TOK_TILES // 2 + 1)
            nc.gpsimd.tensor_tensor(rstd2[:, :], mv2[:, :, 1], neg_half[:, 0:TOK_TILES], ALU.pow) \
                .then_inc(S["tok_rstd2"], 1)

            with nc.gpsimd.Fori(0, GROUPS, 1) as g:
                pool.wait_ge(S["ln_stats"], at(g, "ln_stats", PER["ln_stats"]))
                nc.gpsimd.tensor_tensor(rstd[0:TOK, :], mv[0:TOK, :, 1], neg_half[0:TOK, 0:GROUP], ALU.pow) \
                    .then_inc(S["ln_rstd"], 1)
                for u in range(UNITS):
                    swapped = f"swapped{u % 2}"
                    pool.wait_ge(S[swapped], at(g, swapped, 64 * (u // 2 + 1)))
                    for i in range(UHEADS):
                        nc.gpsimd.tensor_tensor(qk[:, u % 2, i, :], qk[:, u % 2, i, :], rsx[:, u % 2, i, :],
                                                ALU.add).then_inc(S["qk_ready"], 1)
                pool.wait_ge(S["ln2_stats"], at(g, "ln2_stats", PER["ln2_stats"]))
                nc.gpsimd.tensor_tensor(rstd_f[0:TOK, :], mv_f[0:TOK, :, 1], neg_half[0:TOK, 0:GROUP], ALU.pow) \
                    .then_inc(S["ln2_rstd"], 1)

            for n in range(5):
                pool.wait_ge(S["max_ready"], n + 1)
                nc.gpsimd.partition_all_reduce(gall[:, n:n + 1], gred[:, n:n + 1], P, bass.bass_isa.ReduceOp.max) \
                    .then_inc(S["max_shared"], 1)

        @block.scalar
        def _(act):
            act.dma_start(wp_sb[:, :, :], wp.rearrange("(c p) d -> p c d", p=P)).then_inc(S["wp_in"], 16)
            act.dma_start(wq_gu, wgu.rearrange("(t p) i -> p t i", p=P)).then_inc(S["ffnw_in"], 16)
            act.dma_start(wq_dn, wdn.rearrange("(t p) i -> p t i", p=P)).then_inc(S["ffnw_in"], 16)
            act.dma_start(wraw[:, :], wqkv[0:P, :]).then_inc(S["wqkv_in"], 16)

            act.wait_ge(S["angles_ready"], 1)
            nc.scalar.activation(ang[:, 2:4, :], ang[:, 2:4, :], ACT.Sin).then_inc(S["sines_ready"], 1)
            act.wait_ge(S["angles_ready"], 2)
            for i in range(HEADS):
                last = nc.scalar.activation(kbias[0:TOK, i, :], dist[0:TOK, :], ACT.Ln, bias=1.0,
                                            scale=bias_as[0:TOK, i:i + 1])
            last.then_inc(S["logs_ready"], 1)

            def high_part(n):
                act.wait_ge(S["wqkv_in"], 16 * (n + 1))
                dst = (wqkv_h[:, 0, :], wqkv_h[:, 1, :], wo_h[:, :, :].rearrange("p c d -> p (c d)"))[n]
                nc.scalar.activation(dst, wraw[:, 0:dst.shape[1]], ACT.Copy).then_inc(S["high_ready"], 1)

            def next_third(n):
                act.wait_ge(S["low_ready"], n)
                src = (None, wqkv[P:2 * P, :], wo.rearrange("(c p) d -> p c d", p=P))[n]
                dst = wraw[:, :] if n == 1 else wraw[:, 0:INNER_T * DM].rearrange("p (c d) -> p c d", c=INNER_T)
                act.dma_start(dst, src).then_inc(S["wqkv_in"], 16)

            high_part(0)

            with nc.scalar.Fori(0, TOK_TILES // 2, 1) as i:
                for t in range(2):
                    act.wait_ge(S["tok_transposed"], at(i, "tok_transposed", t + 1))
                    act.wait_ge(S["tok_product"], at(i, "tok_product", t - 1))
                    nc.scalar.activation(xnt[:, t, 0:4, :], ps[:, 2 * t, 0:4 * P].rearrange("p (c x) -> p c x", c=4),
                                         ACT.Copy)
                    nc.scalar.activation(xnt[:, t, 4:6, :],
                                         ps[:, 2 * t + 1, 0:2 * P].rearrange("p (c x) -> p c x", c=2), ACT.Copy) \
                        .then_inc(S["tok_evac"], 1)
                for t in range(2):
                    act.wait_ge(S["tok_product"], at(i, "tok_product", t + 1))
                    nc.scalar.activation(ytok[:, 2 * i + t, :], ps[:, 4 + t, 0:DM], ACT.Copy).then_inc(S["tok_y"], 1)
            next_third(1)
            high_part(1)
            next_third(2)
            high_part(2)
            act.wait_ge(S["prologue_v"], 1)
            nc.scalar.activation(scal[:, 15:16], ones[:, 0:1], ACT.Copy).then_inc(S["prologue_a"], 1)

            with nc.scalar.Fori(0, GROUPS, 1) as g:
                def v_item(u, k):
                    j = k - UHEADS
                    act.wait_ge(S["proj_done"], at(g, "proj_done", ITEMS * u + k + 1))
                    act.wait_ge(S["pv_done"], at(g, "pv_done", 4 * (u - 1)))
                    nc.scalar.activation(v[0:TOK, u % 2, j, :, 0:HD],
                                         ps[0:TOK, item_bank(u, k), 0:UHEADS * HD].rearrange("p (h d) -> p h d", h=UHEADS),
                                         ACT.Copy).then_inc(S["v_ready"], 1)

                def o_high(n):
                    for jj in range(2):
                        j = 2 * (n % 2) + jj
                        act.wait_ge(S["o_transposed"], at(g, "o_transposed", 2 * n + jj + 1))
                        nc.scalar.activation(oth[:, 2 * (n // 2):2 * (n // 2) + 2, j * TOK:(j + 1) * TOK],
                                             o_t_view(jj), ACT.Copy).then_inc(S["oth_ready"], 1)

                def p_evac(n):
                    act.wait_ge(S["p_transposed"], at(g, "p_transposed", 2 * n + 2))
                    act.wait_ge(S["pv_done"], at(g, "pv_done", 2 * n))
                    nc.scalar.activation(pt[0:TOK, 1, :, :],
                                         ps[0:TOK, BANK_PT + 1, 0:UHEADS * TOK].rearrange("p (h x) -> p h x", h=UHEADS),
                                         ACT.Copy).then_inc(S["pt_ready_a"], 1)

                def exps(n):
                    act.wait_ge(S["maxed"], at(g, "maxed", n + 1))
                    act.wait_ge(S["p_transposed"], at(g, "p_transposed", 2 * (n - 1)))
                    for i in range(2 * UHEADS):
                        last = nc.scalar.activation(pr[0:TOK, n % 2, i, :], s[0:TOK, n % 2, i, :], ACT.Exp,
                                                    bias=nmax[0:TOK, n % 2, i:i + 1], scale=1.0)
                    last.then_inc(S["exped"], 1)

                act.wait_ge(S["x_transposed"], at(g, "x_transposed", 1))
                nc.scalar.activation(xh[:, :, :], ps[:, BANK_PJ:BANK_PJ + 2, 0:GTOK], ACT.Copy).then_inc(S["xh_ready"], 1)
                for k in range(UHEADS, ITEMS):
                    v_item(0, k)
                for n in range(SLOTS):
                    if n >= 2:
                        o_high(n - 2)
                    for u, k in items_of(n, 0):
                        if k >= UHEADS:
                            v_item(u, k)
                    if 1 <= n <= STEPS:
                        p_evac(n - 1)
                    for u, k in items_of(n, 1):
                        if k >= UHEADS:
                            v_item(u, k)
                    if n < STEPS:
                        exps(n)
                act.wait_ge(S["x2_transposed"], at(g, "x2_transposed", 1))
                nc.scalar.activation(ffn_x[:, :, bass.ts(g, GTOK)], ps[:, BANK_PJ:BANK_PJ + 2, 0:GTOK], ACT.Copy) \
                    .then_inc(S["x2_copied"], 1)

            for r in range(WFILLS):
                act.wait_ge(S["fw_transposed"], r + 1)
                nc.scalar.activation(weight_fill(wgu_h, wdn_h, r), fill_view(r), ACT.Copy).then_inc(S["fw_high"], 1)
            act.wait_ge(S["scales_ready"], 1)
            for c in range(DM_T):
                nc.scalar.activation(ffn_x[:, c, :], ffn_x[:, c, :], ACT.Copy, bias=RINT, scale=scal[:, I_X:I_X + 1]) \
                    .then_inc(S["fx_t"], 1)

            def gu_copy(which, g, half):
                dst = (gate, up)[which][:, g, half * (FFN_T // 2) * GTOK:(half + 1) * (FFN_T // 2) * GTOK]
                act.wait_ge(S["gu_maxed"], 2 * g + (2 * GROUPS * which + half + 1))
                nc.scalar.activation(dst.rearrange("p (m x) -> p m x", m=FFN_T // 2),
                                     ps[:, 3 * half:3 * half + 3, 0:GTOK], ACT.Copy).then_inc(S["gu_copied"], 1)

            with nc.scalar.Fori(0, GROUPS, 1) as g:
                gu_copy(0, g, 0)
                gu_copy(0, g, 1)
            act.wait_ge(S["scales_ready"], 2)
            with nc.scalar.Fori(0, GROUPS, 1) as g:
                gu_copy(1, g, 0)
                nc.scalar.activation(gate[:, g, :], gate[:, g, :], ACT.Copy, bias=RINT, scale=scal[:, K_GATE:K_GATE + 1]) \
                    .then_inc(S["gate_t"], 1)
                gu_copy(1, g, 1)
            with nc.scalar.Fori(0, GROUPS, 1) as g:
                act.wait_ge(S["gate_q"], g + 1)
                nc.scalar.activation(sig[:, g, :], gate[:, g, :], ACT.Sigmoid, scale=scal[:, S_GATE:S_GATE + 1]) \
                    .then_inc(S["sig_done"], 1)
                apart(act)
                act.wait_ge(S["sig_done"], g + 1)
                nc.scalar.activation(sig[:, g, :], sig[:, g, :], ACT.Copy, bias=RINT, scale=SIGLEVELS) \
                    .then_inc(S["sig_t"], 1)
            act.wait_ge(S["scales_ready"], 3)
            with nc.scalar.Fori(0, GROUPS, 1) as g:
                nc.scalar.activation(up[:, g, :], up[:, g, :], ACT.Copy, bias=RINT, scale=scal[:, K_UP:K_UP + 1]) \
                    .then_inc(S["up_t"], 1)
            act.wait_ge(S["scales_ready"], 4)
            with nc.scalar.Fori(0, GROUPS, 1) as g:
                nc.scalar.activation(gate[:, g, :], gate[:, g, :], ACT.Copy, bias=RINT, scale=scal[:, K_G2:K_G2 + 1]) \
                    .then_inc(S["g2_t"], 1)
            act.wait_ge(S["scales_ready"], 5)
            with nc.scalar.Fori(0, GROUPS, 1) as g:
                nc.scalar.activation(gate[:, g, :], gate[:, g, :], ACT.Copy, bias=RINT, scale=scal[:, K_O:K_O + 1]) \
                    .then_inc(S["o_t"], 1)
            with nc.scalar.Fori(0, GROUPS, 1) as g:
                act.wait_ge(S["down_done"], g + 1)
                act.wait_ge(S["yt_transposed"], at(g, "yt_transposed", 0))
                nc.scalar.activation(yt[:, :, :], ps[:, 0:2, 0:GTOK], ACT.Copy, scale=scal[:, S_O:S_O + 1]) \
                    .then_inc(S["yt_ready"], 1)

        @block.tensor
        def _(pe):
            def mm(o, lhsT, rhs, start=True, stop=True):
                return nc.tensor.matmul(o, lhsT, rhs, start=start, stop=stop)

            def three_pass(o, parts, first=True):
                n = 0
                for lh, ll, rh, rl in parts:
                    for a, b in ((lh, rl), (ll, rh), (lh, rh)):
                        n += 1
                        last = mm(o, a, b, start=(n == 1), stop=(n == 3 * len(parts)))
                return last

            pe.wait_ge(S["wp_in"], 16)
            pe.wait_ge(S["small_in"], 16 * SMALLS)
            for c in range(FEAT_T):
                last = mm(ps[0:1, 7, 0:DM], b1_sb[:, c:c + 1], wp_sb[:, c, :], start=(c == 0), stop=(c == FEAT_T - 1))
            last.then_inc(S["bias_product"], 1)

            pe.wait_ge(S["ident_ready"], 1)
            pe.wait_ge(S["tables_ready"], 1)
            with nc.tensor.Fori(0, TOK_TILES // 2, 1) as i:
                for t in range(2):
                    pe.wait_ge(S["tok_normed"], at(i, "tok_normed", t + 1))
                    pe.wait_ge(S["tok_evac"], at(i, "tok_evac", t - 1))
                    for c in range(FEAT_T):
                        o = ps[:, 2 * t + c // 4, (c % 4) * P:(c % 4 + 1) * P]
                        last = nc.tensor.transpose(o, xnorm[:, t, c * P:(c + 1) * P], ident[:, :])
                    last.then_inc(S["tok_transposed"], 1)
                for t in range(2):
                    pe.wait_ge(S["tok_evac"], at(i, "tok_evac", t + 1))
                    pe.wait_ge(S["tok_y"], at(i, "tok_y", t - 1))
                    o = ps[:, 4 + t, 0:DM]
                    for c in range(FEAT_T):
                        mm(o, xnt[:, t, c, :], wp_sb[:, c, :], start=(c == 0), stop=False)
                    mm(o, ones[0:1, :], bias_tok[:, :], start=False, stop=True).then_inc(S["tok_product"], 1)
            pe.wait_ge(S["low_ready"], 3)
            pe.wait_ge(S["prologue_a"], 1)

            with nc.tensor.Fori(0, GROUPS, 1) as g:
                def item(u, k):
                    m = ITEMS * u + k - 2
                    if m >= 0:
                        pu, pk = m // ITEMS, m % ITEMS
                        if pk < UHEADS:
                            pe.wait_ge(S["roped"], at(g, "roped", UHEADS * pu + pk + 1))
                        else:
                            pe.wait_ge(S["v_ready"], at(g, "v_ready", GROUP * pu + pk - UHEADS + 1))
                    if k < UHEADS:
                        col = (k // 2) * INNER + (2 * u + k % 2) * P
                        last = three_pass(ps[:, item_bank(u, k), 0:GTOK], [
                            (wqkv_h[:, c, col:col + P], wqkv_l[:, c, col:col + P], xh[:, c, :], xl[:, c, :])
                            for c in range(DM_T)])
                    else:
                        j = k - UHEADS
                        t0, col = j * TOK, 2 * INNER + u * UHEADS * HD
                        last = three_pass(ps[0:TOK, item_bank(u, k), 0:UHEADS * HD], [
                            (xh[:, c, t0:t0 + TOK], xl[:, c, t0:t0 + TOK],
                             wqkv_h[:, c, col:col + UHEADS * HD], wqkv_l[:, c, col:col + UHEADS * HD])
                            for c in range(DM_T)])
                    last.then_inc(S["proj_done"], 1)

                def scores(n):
                    u = n // 2
                    pe.wait_ge(S["qk_ready"], at(g, "qk_ready", UHEADS * (u + 1)))
                    pe.wait_ge(S["biased"], at(g, "biased", n))
                    for jj in range(2):
                        t0 = (2 * (n % 2) + jj) * TOK
                        for pair in range(2):
                            for e in range(2):
                                rows = slice(HD * e, HD * e + HD)
                                c0 = (2 * jj + pair) * TOK
                                last = mm(ps[0:TOK, BANK_S + e, c0:c0 + TOK], qk[rows, u % 2, pair, t0:t0 + TOK],
                                          qk[rows, u % 2, 2 + pair, t0:t0 + TOK])
                    last.then_inc(S["scores_done"], 1)

                def p_transpose(n):
                    pe.wait_ge(S["exped"], at(g, "exped", n + 1))
                    for jj in range(2):
                        name = ("pt_ready_v", "pt_ready_a")[jj]
                        pe.wait_ge(S[name], at(g, name, n))
                        for hh in range(UHEADS):
                            i = 4 * (hh % 2) + 2 * jj + hh // 2
                            last = nc.tensor.transpose(ps[0:TOK, BANK_PT + jj, hh * TOK:(hh + 1) * TOK],
                                                       pr[0:TOK, n % 2, i, :], ident[0:TOK, 0:TOK])
                        last.then_inc(S["p_transposed"], 1)

                def values(n):
                    u = n // 2
                    pe.wait_ge(S["v_ready"], at(g, "v_ready", GROUP * (u + 1)))
                    for jj in range(2):
                        j = 2 * (n % 2) + jj
                        name = ("pt_ready_v", "pt_ready_a")[jj]
                        pe.wait_ge(S[name], at(g, name, n + 1))
                        pe.wait_ge(S["otl_ready"], at(g, "otl_ready", 2 * n + jj - 1))
                        for hh in range(UHEADS):
                            last = mm(ps[0:TOK, BANK_O + jj, hh * (HD + 1):(hh + 1) * (HD + 1)], pt[0:TOK, jj, hh, :],
                                      v[0:TOK, u % 2, j, hh, :])
                        last.then_inc(S["pv_done"], 1)

                def o_transpose(n):
                    for jj in range(2):
                        pe.wait_ge(S["o_normed"], at(g, "o_normed", 2 * n + jj + 1))
                        for c in range(2):
                            o = ps[:, BANK_O + jj, OT_AT + c * TOK:OT_AT + (c + 1) * TOK]
                            last = nc.tensor.transpose(o, on[0:TOK, jj, c * P:(c + 1) * P], ident[0:TOK, 0:TOK])
                        last.then_inc(S["o_transposed"], 1)

                def transpose_group(src, ready):
                    for j in range(GROUP):
                        pe.wait_ge(S[ready], at(g, ready, j + 1))
                        for c in range(DM_T):
                            last = nc.tensor.transpose(ps[:, BANK_PJ + c, j * TOK:(j + 1) * TOK],
                                                       src[0:TOK, j, c * P:(c + 1) * P], ident[0:TOK, 0:TOK])
                    return last

                pe.wait_ge(S["x2_copied"], at(g, "x2_copied", 0))
                transpose_group(xn, "x_normed").then_inc(S["x_transposed"], 1)
                pe.wait_ge(S["xl_ready"], at(g, "xl_ready", 1))
                for k in range(ITEMS):
                    item(0, k)
                for n in range(SLOTS):
                    if n < STEPS:
                        scores(n)
                    if n >= 2:
                        o_transpose(n - 2)
                    for u, k in items_of(n, 0):
                        item(u, k)
                    if 1 <= n <= STEPS:
                        p_transpose(n - 1)
                    for u, k in items_of(n, 1):
                        item(u, k)
                    if 1 <= n <= STEPS:
                        values(n - 1)
                pe.wait_ge(S["otl_ready"], at(g, "otl_ready", 2 * STEPS))
                for j in range(GROUP):
                    if j >= 2:
                        pe.wait_ge(S["h_added"], at(g, "h_added", j - 1))
                    t0 = j * TOK
                    three_pass(ps[0:TOK, BANK_PJ + j % 2, 0:DM], [
                        (oth[:, c, t0:t0 + TOK], otl[:, c, t0:t0 + TOK], wo_h[:, c, :], wo_l[:, c, :])
                        for c in range(INNER_T)]).then_inc(S["ao_done"], 1)
                pe.wait_ge(S["h_added"], at(g, "h_added", GROUP))
                transpose_group(xn2, "x2_normed").then_inc(S["x2_transposed"], 1)

            pe.wait_ge(S["x2_copied"], at(GROUPS, "x2_copied", 0))
            for r in range(WFILLS):
                if r >= 8:
                    pe.wait_ge(S["fw_low"], r - 7)
                for i in range(4):
                    if r < 2 * QT // 4:
                        c, t = r // (QT // 4), 4 * (r % (QT // 4)) + i
                        src = wq_gu[:, t, c * P:(c + 1) * P]
                    else:
                        m = 2 * (r - 2 * QT // 4) + i // 2
                        src = wq_dn[:, i % 2, m * P:(m + 1) * P]
                    last = nc.tensor.transpose(ps[:, r % 8, i * P:(i + 1) * P], src, ident[:, :])
                last.then_inc(S["fw_transposed"], 1)
            pe.wait_ge(S["fw_low"], WFILLS)
            pe.wait_ge(S["fx_ready"], DM_T)

            for which in range(2):
                with nc.tensor.Fori(0, GROUPS, 1) as g:
                    for half in range(2):
                        pe.wait_ge(S["gu_copied"], 2 * g + (2 * GROUPS * which + half - 1 + SEEDS["gu_copied"]))
                        for b in range(3):
                            col = (which * FFN_T + 3 * half + b) * P
                            last = three_pass(ps[:, 3 * half + b, 0:GTOK], [
                                (wgu_h[:, c, col:col + P], wgu_l[:, c, col:col + P],
                                 fxh[:, c, bass.ts(g, GTOK)], fxl[:, c, bass.ts(g, GTOK)]) for c in range(DM_T)])
                        last.then_inc(S["gu_done"], 1)
            pe.wait_ge(S["gu_copied"], 4 * GROUPS + SEEDS["gu_copied"])
            with nc.tensor.Fori(0, GROUPS, 1) as g:
                pe.wait_ge(S["fo_ready"], g + 1)
                pe.wait_ge(S["yt_transposed"], at(g, "yt_transposed", 0))
                for mo in range(DM_T):
                    last = three_pass(ps[:, mo, 0:GTOK], [
                        (wdn_h[:, m, mo * P:(mo + 1) * P], wdn_l[:, m, mo * P:(mo + 1) * P],
                         fo_h[:, g, m * GTOK:(m + 1) * GTOK], fo_l[:, g, m * GTOK:(m + 1) * GTOK])
                        for m in range(FFN_T)])
                last.then_inc(S["down_done"], 1)
                pe.wait_ge(S["yt_ready"], g + 1)
                pe.wait_ge(S["y_added"], at(g, "y_added", 0))
                for j in range(GROUP):
                    for mo in range(DM_T):
                        c0 = (j % 2) * DM + mo * P
                        last = nc.tensor.transpose(ps[0:TOK, 2 + j // 2, c0:c0 + P], yt[:, mo, j * TOK:(j + 1) * TOK],
                                                   ident[:, :])
                last.then_inc(S["yt_transposed"], 1)

        @block.vector
        def _(dve):
            V = nc.vector
            count = [0]

            def link(ins):
                count[0] += 1
                ins.then_inc(S["vstep"], 1)
                dve.wait_ge(S["vstep"], count[0])

            dve.wait_ge(S["iotas"], 2)
            dve.wait_ge(S["consts"], 3)
            dve.wait_ge(S["small_in"], 16 * SMALLS)
            for q in range(4):
                V.memset(sign[32 * q:32 * q + 32, :], 1.0 if q % 2 == 0 else -1.0)
            V.memset(gred[:, :], 0.0)
            link(V.tensor_copy(ang[:, 1, :], pos_i[:, :]))
            link(V.tensor_scalar(ang[:, 0, :], ang[:, 1, :], freq[:, 0:1], None, ALU.mult))
            link(V.tensor_scalar(ang[:, 1, :], ang[:, 0, :], 1.0 / TWO_PI, RINT, ALU.mult, ALU.add))
            link(V.tensor_scalar(ang[:, 1, :], ang[:, 1, :], RINT, None, ALU.subtract))
            for part in (PI_A, PI_B, PI_C):
                link(V.scalar_tensor_tensor(out=ang[:, 0, :], in0=ang[:, 1, :], scalar=-part, in1=ang[:, 0, :],
                                            op0=ALU.mult, op1=ALU.add))
            link(V.tensor_scalar(ang[:, 2, :], ang[:, 0, :], PI, -PI, ALU.min, ALU.max))
            link(V.tensor_scalar(ang[:, 3, :], ang[:, 0, :], TWO_PI / 4, None, ALU.add))
            link(V.tensor_scalar(ang[:, 1, :], ang[:, 3, :], PI, -TWO_PI, ALU.is_gt, ALU.mult))
            link(V.tensor_tensor(ang[:, 3, :], ang[:, 3, :], ang[:, 1, :], ALU.add))
            V.tensor_scalar(ang[:, 3, :], ang[:, 3, :], PI, -PI, ALU.min, ALU.max).then_inc(S["angles_ready"], 1)
            V.tensor_scalar(bias_as[:, :], bias_as[:, :], 0.01, None, ALU.max)
            V.tensor_scalar(bias_ps[:, :], bias_ps[:, :], 0.01, -1.0, ALU.max, ALU.mult)
            V.scalar_tensor_tensor(out=dist[:, :], in0=dist_i[:, :], scalar=-1.0, in1=dist_i[:, :], op0=ALU.mult,
                                   op1=ALU.max).then_inc(S["angles_ready"], 1)

            dve.wait_ge(S["bias_product"], 1)
            V.tensor_tensor(bias_tok[:, :], ps[0:1, 7, 0:DM], bp_sb[:, :], ALU.add)
            for c in range(FEAT_T):
                last = V.tensor_scalar(wp_sb[:, c, :], wp_sb[:, c, :], g1_sb[:, c:c + 1], None, ALU.mult)
            last.then_inc(S["tables_ready"], 1)

            for t in range(TOK_TILES):
                dve.wait_ge(patches_in[t], 16 * (2 if t < TOK_TILES - 1 else 3))
                for c in range(2):
                    last = V.bn_stats(stat1[:, t, c, :], xin[:, t, c * FEAT // 2:(c + 1) * FEAT // 2])
            link(last)
            for t in range(TOK_TILES):
                last = V.bn_aggr(mv1[:, t, :], stat1[:, t, :, :].rearrange("p c s -> p (c s)"))
            link(last)
            V.tensor_scalar(mv1[:, :, 1], mv1[:, :, 1], EPS, None, ALU.add).then_inc(S["tok_stats"], 1)

            dve.wait_ge(S["sines_ready"], 1)
            link(V.tensor_scalar(ang[:, 2, :], ang[:, 2, :], sign[:, 0:1], None, ALU.mult))
            V.tensor_scalar(rope_s[:, 0, :], ang[:, 2, :], SCORE_SCALE, None, ALU.mult)
            V.tensor_copy(rope_s[:, 1, :], ang[:, 2, :])
            V.tensor_scalar(rope_c[:, 0, :], ang[:, 3, :], SCORE_SCALE, None, ALU.mult)
            V.tensor_copy(rope_c[:, 1, :], ang[:, 3, :])

            dve.wait_ge(S["tok_rstd"], 1)
            with V.Fori(0, TOK_TILES // 2, 1) as i:
                for t in range(2):
                    dve.wait_ge(S["tok_transposed"], at(i, "tok_transposed", t - 1))
                    V.tensor_scalar(xnorm[:, t, :], xin[:, 2 * i + t, :], mv1[:, 2 * i + t, 0:1],
                                    rstd1[:, bass.ds(2 * i + t, 1)], ALU.subtract, ALU.mult).then_inc(S["tok_normed"], 1)
                for t in range(2):
                    dve.wait_ge(S["tok_y"], at(i, "tok_y", t + 1))
                    V.bn_stats(stat2[:, 2 * i + t, :], ytok[:, 2 * i + t, :]).then_inc(S["tok_stats2"], 1)
            dve.wait_ge(S["tok_stats2"], TOK_TILES)
            for t in range(TOK_TILES):
                last = V.bn_aggr(mv2[:, t, :], stat2[:, t, :])
            link(last)
            V.tensor_scalar(mv2[:, :, 1], mv2[:, :, 1], EPS, None, ALU.add).then_inc(S["tok_stats2"], 1)

            for n in range(3):
                dve.wait_ge(S["high_ready"], n + 1)
                lo = (wqkv_l[:, 0, :], wqkv_l[:, 1, :], wo_l[:, :, :].rearrange("p c d -> p (c d)"))[n]
                hi = (wqkv_h[:, 0, :], wqkv_h[:, 1, :], wo_h[:, :, :].rearrange("p c d -> p (c d)"))[n]
                V.tensor_tensor(lo, wraw[:, 0:lo.shape[1]], hi.bitcast(F32), ALU.subtract).then_inc(S["low_ready"], 1)
                if n == 0:
                    dve.wait_ge(S["tok_rstd2"], 1)
                    for t in range(TOK_TILES):
                        last = V.tensor_scalar(ytok[:, t, :], ytok[:, t, :], mv2[:, t, 0:1], rstd2[:, t:t + 1],
                                               ALU.subtract, ALU.mult)
                    link(last)
                    link(V.tensor_tensor(ytok[:, :, :], ytok[:, :, :], over(g2_sb, TOK_TILES), ALU.mult))
                    for half in range(2):
                        rows = slice(SEAT * half, SEAT * half + IMG_TOK)
                        V.tensor_tensor(h[0:IMG_TOK, half:BATCHES:2, :], ytok[rows, :, :], over(b2_sb, TOK_TILES, rows),
                                        ALU.add).then_inc(S["tok_placed"], 1)

            dve.wait_ge(S["logs_ready"], 1)
            V.tensor_tensor(kbias[0:TOK, :, :], kbias[0:TOK, :, :],
                            bias_ps[0:TOK, :].unsqueeze(2).broadcast_to([TOK, HEADS, TOK]), ALU.mult)

            dve.wait_ge(S["ffnw_in"], 32)
            blocks = wq[:, :].rearrange("p (b i) -> p b i", i=QBLOCK)

            def by_block(ap):
                return ap.unsqueeze(2).broadcast_to([P, QBLOCKS, QBLOCK])

            link(V.tensor_reduce(qmax[:, :], blocks, axis=AXX, op=ALU.max, apply_absolute_value=True))
            link(V.tensor_scalar(qmax[:, :], qmax[:, :], 1.0 / WMAX, TINY, ALU.mult, ALU.max))
            link(V.reciprocal(qinv[:, :], qmax[:, :]))
            link(V.tensor_tensor(blocks, blocks, by_block(qinv[:, :]), ALU.mult))
            link(V.tensor_scalar(wq[:, :], wq[:, :], RINT, RINT, ALU.add, ALU.subtract))
            link(V.tensor_scalar(wq[:, :], wq[:, :], WMAX, -WMAX - 1.0, ALU.min, ALU.max))
            link(V.tensor_tensor(blocks, blocks, by_block(qmax[:, :]), ALU.mult))
            V.memset(xmax[:, :], 0.0).then_inc(S["prologue_v"], 1)
            dve.wait_ge(S["prologue_a"], 1)
            dve.wait_ge(S["tok_placed"], 2)
            dve.wait_ge(S["txt_in"], 16)

            with V.Fori(0, GROUPS, 1) as g:
                def layer_norm(src_of, st, m, r, dst, stats, rooted, normed):
                    for j in range(GROUP):
                        V.bn_stats(st[0:TOK, j, :], src_of(j)).then_inc(S[stats], 1)
                    dve.wait_ge(S[stats], at(g, stats, GROUP))
                    V.memset(scal[:, 14:15], 0.0)
                    for j in range(GROUP):
                        V.bn_aggr(m[0:TOK, j, :], st[0:TOK, j, :]).then_inc(S[stats], 1)
                    dve.wait_ge(S[stats], at(g, stats, 2 * GROUP))
                    V.tensor_scalar(m[0:TOK, :, 1], m[0:TOK, :, 1], EPS, None, ALU.add).then_inc(S[stats], 1)
                    dve.wait_ge(S[rooted], at(g, rooted, 1))
                    for j in range(GROUP):
                        V.tensor_scalar(dst[0:TOK, j, :], src_of(j), m[0:TOK, j, 0:1], r[0:TOK, j:j + 1],
                                        ALU.subtract, ALU.mult).then_inc(S[normed], 1)

                def rope(u, k):
                    dve.wait_ge(S["proj_done"], at(g, "proj_done", ITEMS * u + k + 1))
                    swapped = f"swapped{u % 2}"
                    if k == 0:
                        dve.wait_ge(S[swapped], at(g, swapped, 64 * (u // 2)))
                        dve.wait_ge(S["scores_done"], at(g, "scores_done", 2 * (u - 1)))
                    src = steps_view(ps[:, item_bank(u, k), 0:GTOK], GROUP)
                    for table, dst in ((rope_s, rs), (rope_c, qk)):
                        t = table[:, k // 2, :].unsqueeze(1).broadcast_to([P, GROUP, TOK])
                        last = V.tensor_tensor(steps_view(dst[:, u % 2, k, :], GROUP), src, t, ALU.mult)
                    last.then_inc(S["roped"], 1)

                def bias_and_max(n):
                    dve.wait_ge(S["scores_done"], at(g, "scores_done", n + 1))
                    dve.wait_ge(S["exped"], at(g, "exped", n - 1))
                    u = n // 2
                    kb = kbias[0:TOK, UHEADS * u:UHEADS * (u + 1), :].rearrange("p (e q) x -> p e (q x)", e=2)
                    V.tensor_tensor(s[0:TOK, n % 2, :, :].rearrange("p (e j q) x -> p e j (q x)", e=2, j=2),
                                    ps[0:TOK, BANK_S:BANK_S + 2, 0:UHEADS * TOK].rearrange("p e (j x) -> p e j x", j=2),
                                    kb.unsqueeze(2).broadcast_to([TOK, 2, 2, 2 * TOK]), ALU.add) \
                        .then_inc(S["biased"], 1)
                    dve.wait_ge(S["biased"], at(g, "biased", n + 1))
                    V.tensor_reduce(nmax[0:TOK, n % 2, :], s[0:TOK, n % 2, :, :], axis=AXX, op=ALU.max, negate=True) \
                        .then_inc(S["maxed"], 1)

                def o_low(n):
                    for jj in range(2):
                        j = 2 * (n % 2) + jj
                        dve.wait_ge(S["oth_ready"], at(g, "oth_ready", 2 * n + jj + 1))
                        at_ = (slice(None), slice(2 * (n // 2), 2 * (n // 2) + 2), slice(j * TOK, (j + 1) * TOK))
                        V.tensor_tensor(otl[at_], o_t_view(jj), oth[at_].bitcast(F32), ALU.subtract) \
                            .then_inc(S["otl_ready"], 1)

                def p_evac(n):
                    dve.wait_ge(S["p_transposed"], at(g, "p_transposed", 2 * n + 1))
                    dve.wait_ge(S["pv_done"], at(g, "pv_done", 2 * n - 1))
                    V.tensor_copy(pt[0:TOK, 0, :, :],
                                  ps[0:TOK, BANK_PT, 0:UHEADS * TOK].rearrange("p (h x) -> p h x", h=UHEADS)) \
                        .then_inc(S["pt_ready_v"], 1)

                def normalise(n):
                    for jj in range(2):
                        dve.wait_ge(S["pv_done"], at(g, "pv_done", 2 * n + jj + 1))
                        o = ps[0:TOK, BANK_O + jj, 0:UHEADS * (HD + 1)].rearrange("p (h x) -> p h x", h=UHEADS)
                        V.reciprocal(rsum[0:TOK, jj, :], o[:, :, HD]).then_inc(S["o_summed"], 1)
                        dve.wait_ge(S["o_summed"], at(g, "o_summed", 2 * n + jj + 1))
                        dve.wait_ge(S["o_transposed"], at(g, "o_transposed", 2 * n + jj - 1))
                        V.tensor_tensor(on[0:TOK, jj, :].rearrange("p (h x) -> p h x", h=UHEADS), o[:, :, 0:HD],
                                        rsum[0:TOK, jj, :].unsqueeze(2).broadcast_to([TOK, UHEADS, HD]), ALU.mult) \
                            .then_inc(S["o_normed"], 1)

                layer_norm(lambda j: h[0:TOK, GROUP * g + j, :], stat, mv, rstd, xn, "ln_stats", "ln_rstd", "x_normed")
                dve.wait_ge(S["xh_ready"], at(g, "xh_ready", 1))
                V.tensor_tensor(xl[:, :, :], ps[:, BANK_PJ:BANK_PJ + 2, 0:GTOK], xh[:, :, :].bitcast(F32),
                                ALU.subtract).then_inc(S["xl_ready"], 1)
                for k in range(UHEADS):
                    rope(0, k)
                for n in range(SLOTS):
                    if n < STEPS:
                        bias_and_max(n)
                    if n >= 2:
                        o_low(n - 2)
                    for u, k in items_of(n, 0):
                        if k < UHEADS:
                            rope(u, k)
                    if 1 <= n <= STEPS:
                        p_evac(n - 1)
                    for u, k in items_of(n, 1):
                        if k < UHEADS:
                            rope(u, k)
                    if 1 <= n <= STEPS:
                        normalise(n - 1)
                for j in range(GROUP):
                    dve.wait_ge(S["ao_done"], at(g, "ao_done", j + 1))
                    V.tensor_tensor(h[0:TOK, GROUP * g + j, :], h[0:TOK, GROUP * g + j, :],
                                    ps[0:TOK, BANK_PJ + j % 2, 0:DM], ALU.add).then_inc(S["h_added"], 1)
                apart(dve)
                dve.wait_ge(S["h_added"], at(g, "h_added", GROUP))
                layer_norm(lambda j: h[0:TOK, GROUP * g + j, :], stat_f, mv_f, rstd_f, xn2, "ln2_stats", "ln2_rstd",
                           "x2_normed")
                dve.wait_ge(S["x2_normed"], at(g, "x2_normed", GROUP))
                V.tensor_reduce(xmax[0:TOK, bass.ds(g, 1)], xn2[0:TOK, :, :].rearrange("p j d -> p (j d)"), axis=AXX,
                                op=ALU.max, apply_absolute_value=True).then_inc(S["xmax_ready"], 1)

            def col(n):
                return scal[:, n:n + 1]

            def scale_of(n, unit, s_, k_):
                dve.wait_ge(S["max_shared"], n + 1)
                if unit is None:
                    link(V.tensor_scalar(col(s_), gall[:, n:n + 1], 1.0 / ACTMAX, TINY, ALU.mult, ALU.max))
                    V.reciprocal(col(k_), col(s_)).then_inc(S["scales_ready"], 1)
                else:
                    link(V.tensor_scalar(col(s_), gall[:, n:n + 1], col(unit), 1.0 / ACTMAX, ALU.mult, ALU.mult))
                    link(V.tensor_scalar(col(s_), col(s_), TINY, None, ALU.max))
                    link(V.reciprocal(col(SCRATCH), col(s_)))
                    V.tensor_scalar(col(k_), col(SCRATCH), col(unit), None, ALU.mult).then_inc(S["scales_ready"], 1)

            dve.wait_ge(S["xmax_ready"], GROUPS)
            V.tensor_reduce(gred[:, 0:1], xmax[:, :], axis=AXX, op=ALU.max).then_inc(S["max_ready"], 1)
            scale_of(0, None, S_X, I_X)
            for r in range(WFILLS):
                dve.wait_ge(S["fw_high"], r + 1)
                V.tensor_tensor(weight_fill(wgu_l, wdn_l, r), fill_view(r),
                                weight_fill(wgu_h, wdn_h, r).bitcast(F32), ALU.subtract).then_inc(S["fw_low"], 1)
            for c in range(DM_T):
                dve.wait_ge(S["fx_t"], c + 1)
                link(V.tensor_scalar(fxh[:, c, :], ffn_x[:, c, :], RINT, None, ALU.subtract))
                V.scalar_tensor_tensor(out=fxl[:, c, :], in0=ffn_x[:, c, :], scalar=RINT,
                                       in1=fxh[:, c, :].bitcast(F32), op0=ALU.subtract,
                                       op1=ALU.subtract).then_inc(S["fx_ready"], 1)

            def gu_max(which, g, half):
                dve.wait_ge(S["gu_done"], 2 * g + (2 * GROUPS * which + half + 1))
                V.tensor_reduce(maxes[:, which, bass.ds(2 * g + half, 1)], ps[:, 3 * half:3 * half + 3, 0:GTOK],
                                axis=mybir.AxisListType.XY, op=ALU.max, apply_absolute_value=True) \
                    .then_inc(S["gu_maxed"], 1)

            def all_max(n, cols):
                V.tensor_reduce(gred[:, n:n + 1], maxes[:, n - 1, 0:cols], axis=AXX, op=ALU.max) \
                    .then_inc(S["max_ready"], 1)

            with V.Fori(0, GROUPS, 1) as g:
                gu_max(0, g, 0)
                gu_max(0, g, 1)
            dve.wait_ge(S["gu_maxed"], 2 * GROUPS)
            all_max(1, 2 * GROUPS)
            scale_of(1, S_X, S_GATE, K_GATE)
            with V.Fori(0, GROUPS, 1) as g:
                gu_max(1, g, 0)
                dve.wait_ge(S["gate_t"], g + 1)
                V.tensor_scalar(gate[:, g, :], gate[:, g, :], RINT, None, ALU.subtract).then_inc(S["gate_q"], 1)
                gu_max(1, g, 1)
            dve.wait_ge(S["gu_maxed"], 4 * GROUPS)
            all_max(2, 2 * GROUPS)
            scale_of(2, S_X, S_UP, K_UP)
            dve.wait_ge(S["gate_q"], GROUPS)
            with V.Fori(0, GROUPS, 1) as g:
                dve.wait_ge(S["sig_t"], g + 1)
                V.tensor_scalar(sig[:, g, :], sig[:, g, :], RINT, SIGLEVELS - 1.0, ALU.subtract, ALU.min) \
                    .then_inc(S["sig_q"], 1)
                dve.wait_ge(S["sig_q"], g + 1)
                V.tensor_tensor(gate[:, g, :], gate[:, g, :], sig[:, g, :], ALU.mult).then_inc(S["g2_ready"], 1)
                dve.wait_ge(S["g2_ready"], g + 1)
                V.tensor_reduce(maxes[:, 2, bass.ds(g, 1)], gate[:, g, :], axis=AXX, op=ALU.max,
                                apply_absolute_value=True).then_inc(S["g2_maxed"], 1)
            dve.wait_ge(S["g2_maxed"], GROUPS)
            all_max(3, GROUPS)
            link(V.tensor_scalar(col(U_G2), col(S_GATE), 1.0 / SIGLEVELS, None, ALU.mult))
            scale_of(3, U_G2, S_G2, K_G2)
            with V.Fori(0, GROUPS, 1) as g:
                dve.wait_ge(S["up_t"], g + 1)
                V.tensor_scalar(up[:, g, :], up[:, g, :], RINT, None, ALU.subtract).then_inc(S["up_q"], 1)
            dve.wait_ge(S["up_q"], GROUPS)
            with V.Fori(0, GROUPS, 1) as g:
                dve.wait_ge(S["g2_t"], g + 1)
                V.scalar_tensor_tensor(out=gate[:, g, :], in0=gate[:, g, :], scalar=RINT, in1=up[:, g, :],
                                       op0=ALU.subtract, op1=ALU.mult).then_inc(S["o_ready"], 1)
                dve.wait_ge(S["o_ready"], g + 1)
                V.tensor_reduce(maxes[:, 3, bass.ds(g, 1)], gate[:, g, :], axis=AXX, op=ALU.max,
                                apply_absolute_value=True).then_inc(S["o_maxed"], 1)
            dve.wait_ge(S["o_maxed"], GROUPS)
            all_max(4, GROUPS)
            link(V.tensor_tensor(col(U_O), col(S_G2), col(S_UP), ALU.mult))
            scale_of(4, U_O, S_O, K_O)
            with V.Fori(0, GROUPS, 1) as g:
                dve.wait_ge(S["o_t"], g + 1)
                V.tensor_scalar(fo_h[:, g, :], gate[:, g, :], RINT, None, ALU.subtract).then_inc(S["fstep"], 1)
                dve.wait_ge(S["fstep"], g + 1)
                V.scalar_tensor_tensor(out=fo_l[:, g, :], in0=gate[:, g, :], scalar=RINT,
                                       in1=fo_h[:, g, :].bitcast(F32), op0=ALU.subtract,
                                       op1=ALU.subtract).then_inc(S["fo_ready"], 1)
            with V.Fori(0, GROUPS, 1) as g:
                dve.wait_ge(S["yt_transposed"], at(g, "yt_transposed", 1))
                hg = h[0:TOK, bass.ts(g, GROUP), :].rearrange("p j d -> p (j d)").rearrange("p (b x) -> p b x", b=2)
                V.tensor_tensor(hg, hg, ps[0:TOK, 2:4, :], ALU.add).then_inc(S["y_added"], 1)


S_X, I_X, S_GATE, K_GATE, S_UP, K_UP, U_G2, S_G2, K_G2, U_O, S_O, K_O, SCRATCH = range(13)
SMALLS = 11
OT_AT = 264
WFILLS = 2 * QT // 4 + FFN_T // 2


def kernel(x, txt, L0_tok_Wp, L0_tok_bp, L0_tok_ln1_g, L0_tok_ln1_b, L0_tok_ln2_g, L0_tok_ln2_b, L0_attn_qkv_w,
           L0_attn_out_w, L0_attn_bias_p, L0_attn_bias_a, L0_attn_rope_freqs, L0_ffn_w_gate, L0_ffn_w_up,
           L0_ffn_w_down):
    import concourse.bacc as bacc
    from concourse.bass_utils import run_bass_kernel_spmd

    def lay(a, *shape):
        return np.ascontiguousarray(np.asarray(a).reshape(shape))

    patches = np.asarray(x).reshape(BATCHES, CHANNELS, SIDE, PATCH, SIDE, PATCH).transpose(0, 2, 4, 3, 5, 1)

    def by_unit(a):
        return lay(np.asarray(a).reshape(UNITS, 2, 2).transpose(0, 2, 1), 1, HEADS)

    arrays = dict(
        patches=lay(patches, BATCHES, IMG_TOK, FEAT),
        txt=lay(txt, BATCHES, TXT_TOK, DM),
        wp=lay(L0_tok_Wp, FEAT, DM),
        bp=lay(L0_tok_bp, 1, DM),
        g1=np.ascontiguousarray(np.asarray(L0_tok_ln1_g).reshape(FEAT_T, P).T),
        b1=np.ascontiguousarray(np.asarray(L0_tok_ln1_b).reshape(FEAT_T, P).T),
        g2=lay(L0_tok_ln2_g, 1, DM),
        b2=lay(L0_tok_ln2_b, 1, DM),
        wqkv=np.ascontiguousarray(np.asarray(L0_attn_qkv_w).T),
        wo=np.ascontiguousarray(np.asarray(L0_attn_out_w).T),
        bias_p=by_unit(L0_attn_bias_p),
        bias_a=by_unit(L0_attn_bias_a),
        freqs=lay(L0_attn_rope_freqs, HALF, 1),
        wgu=np.concatenate([np.asarray(L0_ffn_w_gate), np.asarray(L0_ffn_w_up)]),
        wdn=lay(L0_ffn_w_down, DM, FFN),
    )
    nc = bacc.Bacc("TRN2", target_bir_lowering=False, num_devices=1)
    args = [nc.dram_tensor(name, a.shape, mybir.dt.from_np(a.dtype), kind="ExternalInput").ap()
            for name, a in arrays.items()]
    args.append(nc.dram_tensor("out", (BATCHES, TOK, DM), F32, kind="ExternalOutput").ap())
    build(nc, *args)
    r = run_bass_kernel_spmd(nc, [arrays], core_ids=[0])
    return r.results[0]["out"]
```

```python
from contextlib import ExitStack

import numpy as np
import concourse.bass as bass
from concourse import mybir

F32 = mybir.dt.float32
F32R = mybir.dt.float32r
I32 = mybir.dt.int32
ACT = mybir.ActivationFunctionType
ALU = mybir.AluOpType
AXX = mybir.AxisListType.X

P = 128
BATCHES, CHANNELS, IMG, PATCH = 16, 3, 112, 16
SIDE = IMG // PATCH
IMG_TOK = SIDE * SIDE
TXT_TOK = 32
TOK = IMG_TOK + TXT_TOK
FEAT = PATCH * PATCH * CHANNELS
FEAT_T = FEAT // P
DM = 256
DM_T = DM // P
HEADS, HD = 16, 64
HALF = HD // 2
INNER = HEADS * HD
INNER_T = INNER // P
FFN = 768
FFN_T = FFN // P
GROUP = 4
GROUPS = BATCHES // GROUP
GTOK = GROUP * TOK
UNITS = 4
UHEADS = HEADS // UNITS
STEPS = 2 * UNITS
ITEMS = 8
TOK_TILES = BATCHES // 2
SEAT = 64
TILE_ROWS = SEAT + IMG_TOK
QBLOCK = 32
QT = 2 * FFN_T
QPART = (QT * DM + DM_T * FFN) // GROUPS

EPS = 1e-5
SCORE_SCALE = 1.0 / float(np.sqrt(HD))
WPART = DM_T * 3 * INNER // (TOK_TILES // 2)
WMAX = 7.0
ACTMAX = 32767.0
SIGLEVELS = 65536.0
TINY = 1e-12
RINT = 12582912.0
AO_SLOTS = {1: 0, 2: 2}
X2_SLOTS = (3, 4)
X_SLOTS = (4, 5)
EARLY_SLOT, LATE_SLOT = 0, 2
EARLY_FILLS = 4
PI = 3.1415925
TWO_PI = 2.0 * float(np.pi)
PI_A = 6.28125
PI_B = float(np.float32(np.round((TWO_PI - PI_A) * 2.0**21) / 2.0**21))
PI_C = float(np.float32(TWO_PI - PI_A - PI_B))

BANK_S = 0
BANK_PT = 2
BANK_O = 4
BANK_PJ = 6


def build(nc, patches, txt, wp, cols, rows, wqkv, wo, wgu, wdn, out):
    ctx = ExitStack()
    with ctx:
        def sb(name, shape, dt=F32, where=ctx):
            return where.enter_context(nc.sbuf_tensor(name, shape, dt))

        ident = sb("ident", [P, P])
        ones = sb("ones", [P, P])
        neg_half = sb("neg_half", [P, BATCHES])
        h = sb("h", [P, BATCHES, DM])
        ffn_x = sb("ffn_x", [P, DM_T, BATCHES * TOK])
        wq = sb("wq", [P, QT * DM + DM_T * FFN])
        xmax = sb("xmax", [P, GROUPS])
        gred = sb("gred", [P, 5])
        gall = sb("gall", [P, 5])
        idle = sb("idle", [P, 2])
        scal = sb("scal", [P, 16])

        wq_gu = wq[:, 0:QT * DM].rearrange("p (t i) -> p t i", t=QT)
        wq_dn = wq[:, QT * DM:].rearrange("p (t i) -> p t i", t=DM_T)

        att = ExitStack()
        wqkv_h = sb("wqkv_h", [P, DM_T, 3 * INNER], F32R, att)
        wqkv_l = sb("wqkv_l", [P, DM_T, 3 * INNER], F32R, att)
        wo_h = sb("wo_h", [P, INNER_T, DM], F32R, att)
        wo_l = sb("wo_l", [P, INNER_T, DM], F32R, att)
        rope_c = sb("rope_c", [P, 2, TOK], where=att)
        rope_s = sb("rope_s", [P, 2, TOK], where=att)
        kbias = sb("kbias", [P, HEADS, TOK], where=att)







        v = sb("v", [P, 2, GROUP, UHEADS, HD + 1], where=att)

        pro = ExitStack()
        xin = sb("xin", [P, TOK_TILES, FEAT], where=pro)
        xnt = sb("xnt", [P, 2, FEAT_T, P], where=pro)
        xnorm = sb("xnorm", [P, 2, FEAT], where=pro)
        ytok = sb("ytok", [P, TOK_TILES, DM], where=pro)
        wp_sb = sb("wp_sb", [P, FEAT_T, DM], where=pro)
        bias_tok = sb("bias_tok", [1, DM], where=pro)
        cols_sb = sb("cols_sb", [P, 2 * FEAT_T + 1], where=pro)
        rows_sb = sb("rows_sb", [P, 3 * DM + 2 * HEADS], where=pro)
        stat1 = sb("stat1", [P, TOK_TILES, 2, 6], where=pro)
        mv1 = sb("mv1", [P, TOK_TILES, 2], where=pro)
        rstd1 = sb("rstd1", [P, TOK_TILES], where=pro)
        stat2 = sb("stat2", [P, TOK_TILES, 6], where=pro)
        mv2 = sb("mv2", [P, TOK_TILES, 2], where=pro)
        rstd2 = sb("rstd2", [P, TOK_TILES], where=pro)
        wraw = sb("wraw", [P, DM_T * 3 * INNER], where=pro)
        sign = sb("sign", [P, 1], where=pro)
        pos_i = sb("pos_i", [P, TOK], I32, pro)
        dist_i = sb("dist_i", [P, TOK], I32, pro)
        dist = sb("dist", [P, TOK], where=pro)
        ang = sb("ang", [P, 4, TOK], where=pro)
        pro.close()

        g1_sb, b1_sb, freq = cols_sb[:, 0:FEAT_T], cols_sb[:, FEAT_T:2 * FEAT_T], cols_sb[:, 2 * FEAT_T:2 * FEAT_T + 1]
        bp_sb, g2_sb, b2_sb = (rows_sb[:, DM * i:DM * (i + 1)] for i in range(3))
        bias_ps, bias_as = (rows_sb[:, 3 * DM + HEADS * i:3 * DM + HEADS * (i + 1)] for i in range(2))

        xh = sb("xh", [P, DM_T, GTOK], F32R, att)
        xl = sb("xl", [P, DM_T, GTOK], F32R, att)
        xn = sb("xn", [P, GROUP, DM], where=att)
        xn2 = sb("xn2", [P, GROUP, DM], where=att)
        stat = sb("stat", [P, GROUP, 6], where=att)
        mv = sb("mv", [P, GROUP, 2], where=att)
        rstd = sb("rstd", [P, GROUP], where=att)
        qmax = sb("qmax", [P, QPART // QBLOCK], where=att)
        qinv = sb("qinv", [P, QPART // QBLOCK], where=att)
        stat_f = sb("stat_f", [P, GROUP, 6], where=att)
        mv_f = sb("mv_f", [P, GROUP, 2], where=att)
        rstd_f = sb("rstd_f", [P, GROUP], where=att)
        rs = sb("rs", [P, 2, UHEADS, GTOK], where=att)
        rsx = sb("rsx", [P, 2, UHEADS, GTOK], where=att)
        qk = sb("qk", [P, 2, UHEADS, GTOK], where=att)
        s = sb("s", [P, 2, 2 * UHEADS, TOK], where=att)
        nmax = sb("nmax", [P, 2, 2 * UHEADS], where=att)
        pr = sb("pr", [P, 2, 2 * UHEADS, TOK], where=att)
        pt = sb("pt", [P, 2, UHEADS, TOK], where=att)
        rsum = sb("rsum", [P, 2, UHEADS], where=att)
        on = sb("on", [P, 2, UHEADS * HD], where=att)
        oth = sb("oth", [P, INNER_T, GTOK], F32R, att)
        otl = sb("otl", [P, INNER_T, GTOK], F32R, att)
        att.close()

        wgu_h = sb("wgu_h", [P, DM_T, QT * P], F32R)
        wgu_l = sb("wgu_l", [P, DM_T, QT * P], F32R)
        wdn_h = sb("wdn_h", [P, FFN_T, DM], F32R)
        wdn_l = sb("wdn_l", [P, FFN_T, DM], F32R)
        yt = sb("yt", [P, DM_T, GTOK])
        maxes = sb("maxes", [P, 4, 2 * GROUPS])
        gate = sb("gate", [P, GROUPS, FFN_T * GTOK])
        fu = ExitStack()
        up = sb("up", [P, GROUPS, FFN_T * GTOK], where=fu)
        fu.close()
        fo_l = sb("fo_l", [P, GROUPS, FFN_T * GTOK], F32R)
        fx = ExitStack()
        fxh = sb("fxh", [P, DM_T, BATCHES * TOK], F32R, fx)
        fxl = sb("fxl", [P, DM_T, BATCHES * TOK], F32R, fx)
        sig = sb("sig", [P, 2, FFN_T * GTOK], where=fx)
        fx.close()
        fo_h = sb("fo_h", [P, GROUPS, FFN_T * GTOK], F32R)
        gate_i, up_i, sig_i, x_i = (t[:, :, :].bitcast(I32) for t in (gate, up, sig, ffn_x))

        ps = ctx.enter_context(nc.psum_tensor("ps", [P, 8, 512], F32))

        names = (
            "txt_in wp_in small_in wqkv_in wo_in ffnw_in out_stored "
            "consts iotas ident_ready tok_stats tok_rstd tok_normed tok_transposed tok_evac tok_product "
            "tok_y tok_stats2 tok_rstd2 tok_placed bias_product angles_ready sines_ready logs_ready "
            "tables_ready high_ready low_ready wo_ready vstep prologue_v prologue_a "
            "ln_stats ln_rstd x_normed x_transposed xh_ready xl_ready proj_done roped swapped0 swapped1 "
            "qk_ready v_ready scores_done biased maxed exped p_transposed pt_ready pv_done "
            "o_summed o_normed o_transposed oth_ready otl_ready ao_done h_added ln2_stats ln2_rstd x2_normed "
            "x2_transposed x2_copied xmax_ready q_max q_scaled q_rounded q_done "
            "fw_transposed fw_high fw_low max_ready max_shared scales_ready fx_high fx_rounded fx_ready gu_done gu_maxed "
            "gu_copied gate_rounded sig_done sig_rounded g2_ready g2_maxed up_rounded g2_rounded o_ready o_maxed "
            "o_high o_rounded fo_ready down_done yt_ready yt_transposed y_added"
        ).split()
        S = {n: ctx.enter_context(nc.semaphore(n)) for n in names}
        patches_in = [ctx.enter_context(nc.semaphore(f"patches_in{t}")) for t in range(TOK_TILES)]
        block = ctx.enter_context(nc.Block())

        PER = dict(
            ln_stats=2 * GROUP + 1, ln_rstd=1, x_normed=GROUP, x_transposed=1, xh_ready=1, xl_ready=1,
            proj_done=UNITS * ITEMS, roped=UNITS * UHEADS, swapped0=UNITS // 2 * 64, swapped1=UNITS // 2 * 64,
            qk_ready=UNITS * UHEADS, v_ready=UNITS * GROUP, scores_done=STEPS, biased=STEPS, maxed=STEPS,
            exped=STEPS, p_transposed=2 * STEPS, pt_ready=2 * STEPS, pv_done=2 * STEPS,
            o_summed=2 * STEPS, o_normed=2 * STEPS, o_transposed=2 * STEPS, oth_ready=2 * STEPS,
            otl_ready=2 * STEPS, ao_done=GROUP, h_added=GROUP, ln2_stats=2 * GROUP + 1, ln2_rstd=1,
            x2_normed=GROUP, x2_transposed=1, x2_copied=1, xmax_ready=1, q_max=3, q_scaled=1, q_rounded=2, q_done=1,
            down_done=DM_T, yt_ready=DM_T,
            tok_normed=2, tok_transposed=2, tok_evac=2, tok_product=2, tok_y=2, tok_stats2=2)
        SEEDS = dict(tok_transposed=2, tok_product=2, tok_evac=2, tok_y=2, biased=1, exped=2, p_transposed=4,
                     pt_ready=2, pv_done=6, o_transposed=2, otl_ready=2, qk_ready=8,
                     scores_done=4, yt_ready=DM_T, g2_ready=2, swapped0=16, swapped1=16, x2_copied=1, ao_done=4, gu_copied=2, yt_transposed=1,
                     y_added=1)

        def at(i, name, n):
            return i * PER.get(name, 1) + (SEEDS.get(name, 0) + n)

        def apart(eng):
            eng.wait_ge(S["prologue_v"], 1)

        def turns(eng, turn):
            turn(-1, False, False, True)
            turn(0, True, False, True)
            with eng.Fori(1, GROUPS - 1, 1) as g:
                turn(g, True, True, True)
            turn(GROUPS - 1, True, True, False)
            turn(GROUPS, False, True, False)

        def has(n, now, prev):
            return (now if n >= 0 else prev) and n < STEPS

        def items_of(n, half, now, nxt):
            unit = n // 2 + 1
            if not (nxt if unit == UNITS else now):
                return []
            first = 4 * (n % 2) + 2 * half
            return [(unit, first), (unit, first + 1)]

        def tenants(n, now, prev, nxt):
            qa, qb = items_of(n, 0, now, nxt), items_of(n, 1, now, nxt)
            out = [("item", u, k) for u, k in qa]
            if n in AO_SLOTS and prev:
                out.append(("ao", AO_SLOTS[n], 0))
            out += [("item", u, k) for u, k in qb]
            if n in AO_SLOTS and prev:
                out.append(("ao", AO_SLOTS[n] + 1, 0))
            return out

        def item_bank(u, k):
            n = 2 * (u - 1) + k // UHEADS
            return BANK_PJ + (k + (n in AO_SLOTS and k % UHEADS >= 2)) % 2

        def ao_bank(j):
            return BANK_PJ + j % 2

        def steps_view(ap, cols):
            return ap.rearrange("p (j x) -> p j x", j=cols)

        def o_t_view(jj):
            return ps[:, BANK_O + jj, OT_AT:OT_AT + 2 * TOK].rearrange("p (c x) -> p c x", c=2)

        def o_rows(n):
            u = n % STEPS // 2
            return slice(2 * u, 2 * u + 2)

        def fill_view(r):
            return ps[:, r % 4, :]

        def weight_fill(gu, dn, r):
            if r < 2 * QT // 4:
                c, q = r // (QT // 4), r % (QT // 4)
                return gu[:, c, 512 * q:512 * q + 512]
            m = 2 * (r - 2 * QT // 4)
            return dn[:, m:m + 2, :].rearrange("p m d -> p (m d)")

        def of(g):
            return slice(g * GTOK, (g + 1) * GTOK)

        def flat(t):
            return t[:, :, :].rearrange("p c d -> p (c d)")

        def q_blocks(g):
            return wq[:, bass.ts(g, QPART)].rearrange("p (b i) -> p b i", i=QBLOCK)

        def by_block(ap):
            return ap[:, :].unsqueeze(2).broadcast_to([P, QPART // QBLOCK, QBLOCK])

        def over(ap, n, rows=slice(0, P)):
            return ap[rows, :].unsqueeze(1).broadcast_to([rows.stop - rows.start, n, DM])

        @block.sync
        def _(sp):
            flat = patches.rearrange("b t f -> (b t) f")
            for b in range(BATCHES):
                rows = min(SEAT, (BATCHES - b) * IMG_TOK)
                seat = SEAT * (b % 2)
                sp.dma_start(xin[seat:seat + rows, b // 2, :],
                             flat[b * IMG_TOK:b * IMG_TOK + rows, :]).then_inc(patches_in[b // 2], 16)
                if rows < SEAT:
                    sp.dma_start(xin[seat + rows:seat + SEAT, b // 2, :],
                                 flat[0:SEAT - rows, :]).then_inc(patches_in[b // 2], 16)
            sp.dma_start(h[IMG_TOK:TOK, :, :], txt.rearrange("b t d -> t b d")).then_inc(S["txt_in"], 16)

            sp.wait_ge(S["prologue_v"], 1)
            sp.wait_ge(S["prologue_a"], 1)

            def turn(g, now, prev, nxt):
                for n in range(0, STEPS, 2):
                    for u, _ in items_of(n, 0, now, nxt)[:1]:
                        swapped = f"swapped{u % 2}"
                        sp.wait_ge(S["roped"], at(g, "roped", UHEADS * (u + 1)))
                        sp.wait_ge(S["qk_ready"], at(g, "qk_ready", UHEADS * (u - 1)))
                        for q in range(4):
                            sp.dma_start(rsx[32 * q:32 * q + 32, u % 2], rs[32 * (q ^ 1):32 * (q ^ 1) + 32, u % 2]) \
                                .then_inc(S[swapped], 16)

            turns(sp, turn)

            out_g = out.rearrange("(g j) t d -> g t j d", g=GROUPS)
            with sp.Fori(0, GROUPS, 1) as g:
                sp.wait_ge(S["y_added"], at(g, "y_added", 1))
                sp.dma_start(out_g[g], h[0:TOK, bass.ts(g, GROUP), :]).then_inc(S["out_stored"], 16)
            sp.wait_ge(S["out_stored"], 16 * GROUPS)

        @block.gpsimd
        def _(pool):
            for name, n in SEEDS.items():
                pool.sem_inc(S[name], n)
            nc.gpsimd.memset(neg_half[:, :], -0.5).then_inc(S["consts"], 1)
            nc.gpsimd.memset(ones[:, :], 1.0).then_inc(S["consts"], 1)
            nc.gpsimd.memset(v[:, :, :, :, HD:HD + 1].rearrange("p a j h c -> p (a j h) c"), 1.0) \
                .then_inc(S["consts"], 1)
            nc.gpsimd.iota(pos_i[:, :], [[1, TOK]], base=0, channel_multiplier=0).then_inc(S["iotas"], 1)
            nc.gpsimd.iota(dist_i[:, :], [[1, TOK]], base=0, channel_multiplier=-1).then_inc(S["iotas"], 1)
            pool.wait_ge(S["consts"], 3)
            nc.gpsimd.affine_select(out=ident[:, :], in_=ones[:, :], compare_op=ALU.is_equal, fill=0.0, base=0,
                                    pattern=[[-1, P]], channel_multiplier=1).then_inc(S["ident_ready"], 1)
            pool.wait_ge(S["tok_stats"], 1)
            nc.gpsimd.tensor_tensor(rstd1[:, :], mv1[:, :, 1], neg_half[:, 0:TOK_TILES], ALU.pow) \
                .then_inc(S["tok_rstd"], 1)
            pool.wait_ge(S["tok_stats2"], 2 * TOK_TILES // 2 + 1)
            nc.gpsimd.tensor_tensor(rstd2[:, :], mv2[:, :, 1], neg_half[:, 0:TOK_TILES], ALU.pow) \
                .then_inc(S["tok_rstd2"], 1)

            def turn(g, now, prev, nxt):
                def carry(n):
                    nc.gpsimd.tensor_tensor(idle[:, n:n + 1], neg_half[:, 0:1], neg_half[:, 0:1], ALU.mult)

                def root(of, rooted, group, m, r):
                    pool.wait_ge(S[of], at(group, of, PER[of]))
                    nc.gpsimd.tensor_tensor(r[0:TOK, :], m[0:TOK, :, 1], neg_half[0:TOK, 0:GROUP], ALU.pow) \
                        .then_inc(S[rooted], 1)

                for n in range(STEPS):
                    if n == X2_SLOTS[0] and prev:
                        root("ln2_stats", "ln2_rstd", g - 1, mv_f, rstd_f)
                    if n == X_SLOTS[0] and nxt:
                        root("ln_stats", "ln_rstd", g + 1, mv, rstd)
                    for u, k in items_of(n, 1, now, nxt)[1:]:
                        if k < UHEADS:
                            swapped = f"swapped{u % 2}"
                            pool.wait_ge(S[swapped], at(g, swapped, 64 * (u // 2 + 1)))
                            for i in range(UHEADS):
                                nc.gpsimd.tensor_tensor(qk[:, u % 2, i, :], qk[:, u % 2, i, :], rsx[:, u % 2, i, :],
                                                        ALU.add).then_inc(S["qk_ready"], 1)
                    if n == 1 and now:
                        pool.wait_ge(S["q_max"], at(g, "q_max", 3))
                        carry(0)
                        nc.gpsimd.tensor_tensor(q_blocks(g), q_blocks(g), by_block(qinv), ALU.mult) \
                            .then_inc(S["q_scaled"], 1)
                    if n == 3 and now:
                        pool.wait_ge(S["q_rounded"], at(g, "q_rounded", 2))
                        carry(1)
                        nc.gpsimd.tensor_tensor(q_blocks(g), q_blocks(g), by_block(qmax), ALU.mult) \
                            .then_inc(S["q_done"], 1)

            turns(pool, turn)

            def share_max(n):
                pool.wait_ge(S["max_ready"], n + 1)
                nc.gpsimd.partition_all_reduce(gall[:, n:n + 1], gred[:, n:n + 1], P, bass.bass_isa.ReduceOp.max) \
                    .then_inc(S["max_shared"], 1)

            def to_integers(dst, src, factor):
                return nc.gpsimd.tensor_scalar(dst, src, factor, 0.0, ALU.mult, ALU.add)

            share_max(0)
            pool.wait_ge(S["scales_ready"], 1)
            for g in range(GROUPS):
                pool.wait_ge(S["fx_high"], g + 1)
                to_integers(x_i[:, :, of(g)], ffn_x[:, :, of(g)], scal[:, I_X:I_X + 1]).then_inc(S["fx_rounded"], 1)
            share_max(1)

            def round_gate(g):
                to_integers(gate_i[:, g, :], gate[:, g, :], scal[:, K_GATE:K_GATE + 1]).then_inc(S["gate_rounded"], 1)

            pool.wait_ge(S["scales_ready"], 2)
            pool.wait_ge(S["gu_copied"], 2 * GROUPS + SEEDS["gu_copied"])
            round_gate(0)
            for g in range(GROUPS):
                if g + 1 < GROUPS:
                    round_gate(g + 1)
                pool.wait_ge(S["sig_done"], g + 1)
                to_integers(sig_i[:, g % 2, :], sig[:, g % 2, :], SIGLEVELS) \
                    .then_inc(S["sig_rounded"], 1)
            share_max(2)
            share_max(3)
            pool.wait_ge(S["scales_ready"], 3)
            pool.wait_ge(S["gu_copied"], 4 * GROUPS + SEEDS["gu_copied"])
            for g in range(GROUPS):
                to_integers(up_i[:, g, :], up[:, g, :], scal[:, K_UP:K_UP + 1]).then_inc(S["up_rounded"], 1)
            share_max(4)
            pool.wait_ge(S["scales_ready"], 5)
            for g in range(GROUPS):
                to_integers(up_i[:, g, :], gate[:, g, :], scal[:, K_O:K_O + 1]).then_inc(S["o_rounded"], 1)

        @block.scalar
        def _(act):
            act.dma_start(cols_sb[:, :], cols).then_inc(S["small_in"], 16)
            act.dma_start(rows_sb[:, :], rows.broadcast_to([P, 3 * DM + 2 * HEADS])).then_inc(S["small_in"], 16)
            act.dma_start(wp_sb[:, :, :], wp.rearrange("(c p) d -> p c d", p=P)).then_inc(S["wp_in"], 16)
            act.dma_start(wraw[:, :].rearrange("p (c n) -> p c n", c=DM_T), wqkv.rearrange("(c p) n -> p c n", p=P)) \
                .then_inc(S["wqkv_in"], 16)
            act.dma_start(wq_gu, wgu.rearrange("(t p) i -> p t i", p=P)).then_inc(S["ffnw_in"], 16)
            act.dma_start(wq_dn, wdn.rearrange("(t p) i -> p t i", p=P)).then_inc(S["ffnw_in"], 16)

            act.wait_ge(S["angles_ready"], 1)
            nc.scalar.activation(ang[:, 2:4, :], ang[:, 2:4, :], ACT.Sin).then_inc(S["sines_ready"], 1)
            act.wait_ge(S["angles_ready"], 2)
            for i in range(HEADS):
                last = nc.scalar.activation(kbias[0:TOK, i, :], dist[0:TOK, :], ACT.Ln, bias=1.0,
                                            scale=bias_as[0:TOK, i:i + 1])
            last.then_inc(S["logs_ready"], 1)

            act.wait_ge(S["wqkv_in"], 16)
            with nc.scalar.Fori(0, TOK_TILES // 2, 1) as i:
                for t in range(2):
                    act.wait_ge(S["tok_transposed"], at(i, "tok_transposed", t + 1))
                    act.wait_ge(S["tok_product"], at(i, "tok_product", t - 1))
                    nc.scalar.activation(xnt[:, t, 0:4, :], ps[:, 2 * t, 0:4 * P].rearrange("p (c x) -> p c x", c=4),
                                         ACT.Copy)
                    nc.scalar.activation(xnt[:, t, 4:6, :],
                                         ps[:, 2 * t + 1, 0:2 * P].rearrange("p (c x) -> p c x", c=2), ACT.Copy) \
                        .then_inc(S["tok_evac"], 1)
                nc.scalar.activation(flat(wqkv_h)[:, bass.ts(i, WPART)], wraw[:, bass.ts(i, WPART)], ACT.Copy) \
                    .then_inc(S["high_ready"], 1)
                for t in range(2):
                    act.wait_ge(S["tok_product"], at(i, "tok_product", t + 1))
                    nc.scalar.activation(ytok[:, 2 * i + t, :], ps[:, 4 + t, 0:DM], ACT.Copy).then_inc(S["tok_y"], 1)
            act.wait_ge(S["low_ready"], TOK_TILES // 2)
            act.dma_start(wraw[:, 0:INNER_T * DM].rearrange("p (c d) -> p c d", c=INNER_T),
                          wo.rearrange("(c p) d -> p c d", p=P)).then_inc(S["wo_in"], 16)
            act.wait_ge(S["wo_in"], 16)
            nc.scalar.activation(flat(wo_h), wraw[:, 0:INNER_T * DM], ACT.Copy).then_inc(S["wo_ready"], 1)
            act.wait_ge(S["prologue_v"], 1)
            nc.scalar.activation(scal[:, 15:16], ones[:, 0:1], ACT.Copy).then_inc(S["prologue_a"], 1)

            def high_weights(fills):
                for r in fills:
                    act.wait_ge(S["fw_transposed"], r + 1)
                    nc.scalar.activation(weight_fill(wgu_h, wdn_h, r), fill_view(r), ACT.Copy) \
                        .then_inc(S["fw_high"], 1)

            def turn(g, now, prev, nxt):
                def v_item(u, k):
                    j = k - UHEADS
                    act.wait_ge(S["proj_done"], at(g, "proj_done", ITEMS * u + k + 1))
                    act.wait_ge(S["pv_done"], at(g, "pv_done", 4 * (u - 1)))
                    nc.scalar.activation(v[0:TOK, u % 2, j, :, 0:HD],
                                         ps[0:TOK, item_bank(u, k), 0:UHEADS * HD].rearrange("p (h d) -> p h d", h=UHEADS),
                                         ACT.Copy).then_inc(S["v_ready"], 1)

                def o_high(n):
                    for jj in range(2):
                        j = 2 * (n % 2) + jj
                        act.wait_ge(S["o_transposed"], at(g, "o_transposed", 2 * n + jj + 1))
                        if n % STEPS < 2:
                            act.wait_ge(S["ao_done"], at(g, "ao_done", j + 1 - GROUP))
                        nc.scalar.activation(oth[:, o_rows(n), j * TOK:(j + 1) * TOK],
                                             o_t_view(jj), ACT.Copy).then_inc(S["oth_ready"], 1)

                def p_evac(n):
                    for jj in range(2):
                        act.wait_ge(S["p_transposed"], at(g, "p_transposed", 2 * n + jj + 1))
                        act.wait_ge(S["pv_done"], at(g, "pv_done", 2 * n + jj - 1))
                        nc.scalar.activation(pt[0:TOK, jj, :, :],
                                             ps[0:TOK, BANK_PT + jj, 0:UHEADS * TOK].rearrange("p (h x) -> p h x", h=UHEADS),
                                             ACT.Copy).then_inc(S["pt_ready"], 1)

                def exps(n):
                    act.wait_ge(S["maxed"], at(g, "maxed", n + 1))
                    act.wait_ge(S["p_transposed"], at(g, "p_transposed", 2 * (n - 1)))
                    for i in range(2 * UHEADS):
                        last = nc.scalar.activation(pr[0:TOK, n % 2, i, :], s[0:TOK, n % 2, i, :], ACT.Exp,
                                                    bias=nmax[0:TOK, n % 2, i:i + 1], scale=1.0)
                    last.then_inc(S["exped"], 1)

                for n in range(STEPS):
                    if has(n - 2, now, prev):
                        o_high(n - 2)
                    for u, k in items_of(n, 0, now, nxt):
                        if k >= UHEADS:
                            v_item(u, k)
                    if has(n - 1, now, prev):
                        p_evac(n - 1)
                    for u, k in items_of(n, 1, now, nxt):
                        if k >= UHEADS:
                            v_item(u, k)
                    if has(n, now, prev):
                        exps(n)
                    if n == EARLY_SLOT and not now and prev:
                        high_weights(range(EARLY_FILLS))
                    if n == LATE_SLOT and not now and prev:
                        high_weights(range(EARLY_FILLS, WFILLS - 1))
                    if n == X2_SLOTS[1] and prev:
                        act.wait_ge(S["x2_transposed"], at(g - 1, "x2_transposed", 1))
                        nc.scalar.activation(ffn_x[:, :, bass.ts(g - 1, GTOK)], ps[:, BANK_PJ:BANK_PJ + 2, 0:GTOK],
                                             ACT.Copy).then_inc(S["x2_copied"], 1)
                    if n == X_SLOTS[1] and nxt:
                        act.wait_ge(S["x_transposed"], at(g + 1, "x_transposed", 1))
                        nc.scalar.activation(xh[:, :, :], ps[:, BANK_PJ:BANK_PJ + 2, 0:GTOK], ACT.Copy) \
                            .then_inc(S["xh_ready"], 1)

            turns(act, turn)
            high_weights(range(WFILLS - 1, WFILLS))

            act.wait_ge(S["scales_ready"], 1)
            for g in range(GROUPS):
                nc.scalar.activation(fxh[:, :, of(g)], ffn_x[:, :, of(g)], ACT.Copy, scale=scal[:, I_X:I_X + 1]) \
                    .then_inc(S["fx_high"], 1)

            def gu_copy(which, g, half):
                dst = (gate, up)[which][:, g, half * (FFN_T // 2) * GTOK:(half + 1) * (FFN_T // 2) * GTOK]
                act.wait_ge(S["gu_maxed"], 2 * g + (2 * GROUPS * which + half + 1))
                nc.scalar.activation(dst.rearrange("p (m x) -> p m x", m=FFN_T // 2),
                                     ps[:, 3 * half:3 * half + 3, 0:GTOK], ACT.Copy).then_inc(S["gu_copied"], 1)

            with nc.scalar.Fori(0, GROUPS, 1) as g:
                gu_copy(0, g, 0)
                gu_copy(0, g, 1)
            act.wait_ge(S["scales_ready"], 2)
            with nc.scalar.Fori(0, GROUPS, 1) as g:
                gu_copy(1, g, 0)
                apart(act)
                act.wait_ge(S["gate_rounded"], g + 1)
                act.wait_ge(S["g2_ready"], at(g, "g2_ready", -1))
                nc.scalar.activation(sig[:, bass.ds(g % 2, 1), :], gate_i[:, g, :], ACT.Sigmoid,
                                     scale=scal[:, S_GATE:S_GATE + 1]).then_inc(S["sig_done"], 1)
                gu_copy(1, g, 1)
            nc.scalar.activation(scal[:, 15:16], ones[:, 0:1], ACT.Copy, scale=scal[:, S_GATE:S_GATE + 1])
            act.wait_ge(S["scales_ready"], 4)
            with nc.scalar.Fori(0, GROUPS, 1) as g:
                nc.scalar.activation(gate_i[:, g, :], gate[:, g, :], ACT.Copy, scale=scal[:, K_G2:K_G2 + 1]) \
                    .then_inc(S["g2_rounded"], 1)
            act.wait_ge(S["scales_ready"], 5)
            for g in range(GROUPS):
                nc.scalar.activation(fo_h[:, g, :], gate[:, g, :], ACT.Copy, scale=scal[:, K_O:K_O + 1]) \
                    .then_inc(S["o_high"], 1)
            with nc.scalar.Fori(0, GROUPS, 1) as g:
                for mo in range(DM_T):
                    act.wait_ge(S["down_done"], at(g, "down_done", mo + 1))
                    act.wait_ge(S["yt_transposed"], at(g, "yt_transposed", 0))
                    nc.scalar.activation(yt[:, mo, :], ps[:, mo, 0:GTOK], ACT.Copy, scale=scal[:, S_O:S_O + 1]) \
                        .then_inc(S["yt_ready"], 1)

        @block.tensor
        def _(pe):
            def mm(o, lhsT, rhs, start=True, stop=True):
                return nc.tensor.matmul(o, lhsT, rhs, start=start, stop=stop)

            def three_pass(o, parts, first=True):
                n = 0
                for lh, ll, rh, rl in parts:
                    for a, b in ((lh, rl), (ll, rh), (lh, rh)):
                        n += 1
                        last = mm(o, a, b, start=(n == 1), stop=(n == 3 * len(parts)))
                return last

            pe.wait_ge(S["wp_in"], 16)
            pe.wait_ge(S["small_in"], 16 * SMALLS)
            for c in range(FEAT_T):
                last = mm(ps[0:1, 7, 0:DM], b1_sb[:, c:c + 1], wp_sb[:, c, :], start=(c == 0), stop=(c == FEAT_T - 1))
            last.then_inc(S["bias_product"], 1)

            pe.wait_ge(S["ident_ready"], 1)
            pe.wait_ge(S["tables_ready"], 1)
            with nc.tensor.Fori(0, TOK_TILES // 2, 1) as i:
                for t in range(2):
                    pe.wait_ge(S["tok_normed"], at(i, "tok_normed", t + 1))
                    pe.wait_ge(S["tok_evac"], at(i, "tok_evac", t - 1))
                    for c in range(FEAT_T):
                        o = ps[:, 2 * t + c // 4, (c % 4) * P:(c % 4 + 1) * P]
                        last = nc.tensor.transpose(o, xnorm[:, t, c * P:(c + 1) * P], ident[:, :])
                    last.then_inc(S["tok_transposed"], 1)
                for t in range(2):
                    pe.wait_ge(S["tok_evac"], at(i, "tok_evac", t + 1))
                    pe.wait_ge(S["tok_y"], at(i, "tok_y", t - 1))
                    o = ps[:, 4 + t, 0:DM]
                    for c in range(FEAT_T):
                        mm(o, xnt[:, t, c, :], wp_sb[:, c, :], start=(c == 0), stop=False)
                    mm(o, ones[0:1, :], bias_tok[:, :], start=False, stop=True).then_inc(S["tok_product"], 1)
            pe.wait_ge(S["low_ready"], TOK_TILES // 2)
            pe.wait_ge(S["prologue_a"], 1)

            def fill_weights(fills):
                pe.wait_ge(S["q_done"], GROUPS)
                for r in fills:
                    if r >= 4:
                        pe.wait_ge(S["fw_low"], r - 3)
                    for i in range(4):
                        if r < 2 * QT // 4:
                            c, t = r // (QT // 4), 4 * (r % (QT // 4)) + i
                            src = wq_gu[:, t, c * P:(c + 1) * P]
                        else:
                            m = 2 * (r - 2 * QT // 4) + i // 2
                            src = wq_dn[:, i % 2, m * P:(m + 1) * P]
                        last = nc.tensor.transpose(ps[:, r % 4, i * P:(i + 1) * P], src, ident[:, :])
                    last.then_inc(S["fw_transposed"], 1)

            def turn(g, now, prev, nxt):
                def freed(tenant):
                    what, a, k = tenant
                    if what == "ao":
                        pe.wait_ge(S["h_added"], at(g, "h_added", a + 1 - GROUP))
                    elif k < UHEADS:
                        pe.wait_ge(S["roped"], at(g, "roped", UHEADS * a + k + 1))
                    else:
                        pe.wait_ge(S["v_ready"], at(g, "v_ready", GROUP * a + k - UHEADS + 1))

                def item(u, k):
                    if k < UHEADS:
                        col = (k // 2) * INNER + (2 * (u % UNITS) + k % 2) * P
                        last = three_pass(ps[:, item_bank(u, k), 0:GTOK], [
                            (wqkv_h[:, c, col:col + P], wqkv_l[:, c, col:col + P], xh[:, c, :], xl[:, c, :])
                            for c in range(DM_T)])
                    else:
                        j = k - UHEADS
                        t0, col = j * TOK, 2 * INNER + u % UNITS * UHEADS * HD
                        last = three_pass(ps[0:TOK, item_bank(u, k), 0:UHEADS * HD], [
                            (xh[:, c, t0:t0 + TOK], xl[:, c, t0:t0 + TOK],
                             wqkv_h[:, c, col:col + UHEADS * HD], wqkv_l[:, c, col:col + UHEADS * HD])
                            for c in range(DM_T)])
                    last.then_inc(S["proj_done"], 1)

                def scores(n):
                    u = n // 2
                    pe.wait_ge(S["qk_ready"], at(g, "qk_ready", UHEADS * (u + 1)))
                    pe.wait_ge(S["biased"], at(g, "biased", n))
                    for jj in range(2):
                        t0 = (2 * (n % 2) + jj) * TOK
                        for pair in range(2):
                            for e in range(2):
                                rows = slice(HD * e, HD * e + HD)
                                c0 = (2 * jj + pair) * TOK
                                last = mm(ps[0:TOK, BANK_S + e, c0:c0 + TOK], qk[rows, u % 2, pair, t0:t0 + TOK],
                                          qk[rows, u % 2, 2 + pair, t0:t0 + TOK])
                    last.then_inc(S["scores_done"], 1)

                def p_transpose(n):
                    pe.wait_ge(S["exped"], at(g, "exped", n + 1))
                    for jj in range(2):
                        pe.wait_ge(S["pt_ready"], at(g, "pt_ready", 2 * n + jj - 1))
                        for hh in range(UHEADS):
                            i = 4 * (hh % 2) + 2 * jj + hh // 2
                            last = nc.tensor.transpose(ps[0:TOK, BANK_PT + jj, hh * TOK:(hh + 1) * TOK],
                                                       pr[0:TOK, n % 2, i, :], ident[0:TOK, 0:TOK])
                        last.then_inc(S["p_transposed"], 1)

                def values(n):
                    u = n // 2
                    pe.wait_ge(S["v_ready"], at(g, "v_ready", GROUP * (u + 1)))
                    for jj in range(2):
                        j = 2 * (n % 2) + jj
                        pe.wait_ge(S["pt_ready"], at(g, "pt_ready", 2 * n + jj + 1))
                        pe.wait_ge(S["otl_ready"], at(g, "otl_ready", 2 * n + jj - 1))
                        for hh in range(UHEADS):
                            last = mm(ps[0:TOK, BANK_O + jj, hh * (HD + 1):(hh + 1) * (HD + 1)], pt[0:TOK, jj, hh, :],
                                      v[0:TOK, u % 2, j, hh, :])
                        last.then_inc(S["pv_done"], 1)

                def o_transpose(n):
                    for jj in range(2):
                        pe.wait_ge(S["o_normed"], at(g, "o_normed", 2 * n + jj + 1))
                        for c in range(2):
                            o = ps[:, BANK_O + jj, OT_AT + c * TOK:OT_AT + (c + 1) * TOK]
                            last = nc.tensor.transpose(o, on[0:TOK, jj, c * P:(c + 1) * P], ident[0:TOK, 0:TOK])
                        last.then_inc(S["o_transposed"], 1)

                def transpose_group(src, ready, group):
                    for j in range(GROUP):
                        pe.wait_ge(S[ready], at(group, ready, j + 1))
                        for c in range(DM_T):
                            last = nc.tensor.transpose(ps[:, BANK_PJ + c, j * TOK:(j + 1) * TOK],
                                                       src[0:TOK, j, c * P:(c + 1) * P], ident[0:TOK, 0:TOK])
                    return last

                def output_projection(j):
                    t0 = j * TOK
                    pe.wait_ge(S["otl_ready"], at(g - 1, "otl_ready", 2 * (STEPS - 2) + j + 1))
                    three_pass(ps[0:TOK, ao_bank(j), 0:DM], [
                        (oth[:, c, t0:t0 + TOK], otl[:, c, t0:t0 + TOK], wo_h[:, c, :], wo_l[:, c, :])
                        for c in range(INNER_T)]).then_inc(S["ao_done"], 1)

                held = {}
                if now:
                    held = {item_bank(0, k): ("item", 0, k) for k in (ITEMS - 2, ITEMS - 1)}

                def take(tenant):
                    what, a, k = tenant
                    b = ao_bank(a) if what == "ao" else item_bank(a, k)
                    if b in held:
                        freed(held[b])
                    held[b] = tenant
                    output_projection(a) if what == "ao" else item(a, k)

                for n in range(STEPS):
                    line = tenants(n, now, prev, nxt)
                    half = len(line) // 2
                    if has(n, now, prev):
                        scores(n)
                    if has(n - 2, now, prev):
                        o_transpose(n - 2)
                    for tenant in line[:half]:
                        take(tenant)
                    if has(n - 1, now, prev):
                        p_transpose(n - 1)
                    for tenant in line[half:]:
                        take(tenant)
                    if has(n - 1, now, prev):
                        values(n - 1)
                    if n == EARLY_SLOT and not now and prev:
                        fill_weights(range(EARLY_FILLS))
                    if n == LATE_SLOT and not now and prev:
                        fill_weights(range(EARLY_FILLS, WFILLS - 1))
                    if n == X2_SLOTS[1] and prev:
                        for b in held:
                            freed(held[b])
                        transpose_group(xn2, "x2_normed", g - 1).then_inc(S["x2_transposed"], 1)
                        held = {}
                        pe.wait_ge(S["x2_copied"], at(g - 1, "x2_copied", 1))
                    if n == X_SLOTS[1] and nxt:
                        for b in held:
                            freed(held[b])
                        transpose_group(xn, "x_normed", g + 1).then_inc(S["x_transposed"], 1)
                        held = {}
                        pe.wait_ge(S["xl_ready"], at(g + 1, "xl_ready", 1))

            turns(pe, turn)

            fill_weights(range(WFILLS - 1, WFILLS))
            pe.wait_ge(S["fw_low"], WFILLS)

            for which in range(2):
                with nc.tensor.Fori(0, GROUPS, 1) as g:
                    if which == 0:
                        pe.wait_ge(S["fx_ready"], g + 1)
                    for half in range(2):
                        pe.wait_ge(S["gu_copied"], 2 * g + (2 * GROUPS * which + half - 1 + SEEDS["gu_copied"]))
                        for b in range(3):
                            col = (which * FFN_T + 3 * half + b) * P
                            last = three_pass(ps[:, 3 * half + b, 0:GTOK], [
                                (wgu_h[:, c, col:col + P], wgu_l[:, c, col:col + P],
                                 fxh[:, c, bass.ts(g, GTOK)], fxl[:, c, bass.ts(g, GTOK)]) for c in range(DM_T)])
                        last.then_inc(S["gu_done"], 1)
            with nc.tensor.Fori(0, GROUPS, 1) as g:
                pe.wait_ge(S["fo_ready"], g + 1)
                for mo in range(DM_T):
                    pe.wait_ge(S["yt_ready"], at(g, "yt_ready", mo + 1 - DM_T))
                    three_pass(ps[:, mo, 0:GTOK], [
                        (wdn_h[:, m, mo * P:(mo + 1) * P], wdn_l[:, m, mo * P:(mo + 1) * P],
                         fo_h[:, g, m * GTOK:(m + 1) * GTOK], fo_l[:, g, m * GTOK:(m + 1) * GTOK])
                        for m in range(FFN_T)]).then_inc(S["down_done"], 1)
                pe.wait_ge(S["y_added"], at(g, "y_added", 0))
                for mo in range(DM_T):
                    pe.wait_ge(S["yt_ready"], at(g, "yt_ready", mo + 1))
                    for j in range(GROUP):
                        c0 = (j % 2) * DM + mo * P
                        last = nc.tensor.transpose(ps[0:TOK, 2 + j // 2, c0:c0 + P], yt[:, mo, j * TOK:(j + 1) * TOK],
                                                   ident[:, :])
                last.then_inc(S["yt_transposed"], 1)

        @block.vector
        def _(dve):
            V = nc.vector
            count = [0]

            def link(ins):
                count[0] += 1
                ins.then_inc(S["vstep"], 1)
                dve.wait_ge(S["vstep"], count[0])

            dve.wait_ge(S["iotas"], 2)
            dve.wait_ge(S["consts"], 3)
            dve.wait_ge(S["small_in"], 16 * SMALLS)
            for q in range(4):
                V.memset(sign[32 * q:32 * q + 32, :], 1.0 if q % 2 == 0 else -1.0)
            V.memset(gred[:, :], 0.0)
            link(V.tensor_copy(ang[:, 1, :], pos_i[:, :]))
            link(V.tensor_scalar(ang[:, 0, :], ang[:, 1, :], freq[:, 0:1], None, ALU.mult))
            link(V.tensor_scalar(ang[:, 1, :], ang[:, 0, :], 1.0 / TWO_PI, RINT, ALU.mult, ALU.add))
            link(V.tensor_scalar(ang[:, 1, :], ang[:, 1, :], RINT, None, ALU.subtract))
            for part in (PI_A, PI_B, PI_C):
                link(V.scalar_tensor_tensor(out=ang[:, 0, :], in0=ang[:, 1, :], scalar=-part, in1=ang[:, 0, :],
                                            op0=ALU.mult, op1=ALU.add))
            link(V.tensor_scalar(ang[:, 2, :], ang[:, 0, :], PI, -PI, ALU.min, ALU.max))
            link(V.tensor_scalar(ang[:, 3, :], ang[:, 0, :], TWO_PI / 4, None, ALU.add))
            link(V.tensor_scalar(ang[:, 1, :], ang[:, 3, :], PI, -TWO_PI, ALU.is_gt, ALU.mult))
            link(V.tensor_tensor(ang[:, 3, :], ang[:, 3, :], ang[:, 1, :], ALU.add))
            V.tensor_scalar(ang[:, 3, :], ang[:, 3, :], PI, -PI, ALU.min, ALU.max).then_inc(S["angles_ready"], 1)
            V.tensor_scalar(bias_as[:, :], bias_as[:, :], 0.01, None, ALU.max)
            V.tensor_scalar(bias_ps[:, :], bias_ps[:, :], 0.01, -1.0, ALU.max, ALU.mult)
            V.scalar_tensor_tensor(out=dist[:, :], in0=dist_i[:, :], scalar=-1.0, in1=dist_i[:, :], op0=ALU.mult,
                                   op1=ALU.max).then_inc(S["angles_ready"], 1)

            dve.wait_ge(S["bias_product"], 1)
            V.tensor_tensor(bias_tok[:, :], ps[0:1, 7, 0:DM], bp_sb[0:1, :], ALU.add)
            for c in range(FEAT_T):
                last = V.tensor_scalar(wp_sb[:, c, :], wp_sb[:, c, :], g1_sb[:, c:c + 1], None, ALU.mult)
            last.then_inc(S["tables_ready"], 1)

            for t in range(TOK_TILES):
                dve.wait_ge(patches_in[t], 16 * (2 if t < TOK_TILES - 1 else 3))
                for c in range(2):
                    last = V.bn_stats(stat1[:, t, c, :], xin[:, t, c * FEAT // 2:(c + 1) * FEAT // 2])
            link(last)
            for t in range(TOK_TILES):
                last = V.bn_aggr(mv1[:, t, :], stat1[:, t, :, :].rearrange("p c s -> p (c s)"))
            link(last)
            V.tensor_scalar(mv1[:, :, 1], mv1[:, :, 1], EPS, None, ALU.add).then_inc(S["tok_stats"], 1)

            dve.wait_ge(S["sines_ready"], 1)
            link(V.tensor_scalar(ang[:, 2, :], ang[:, 2, :], sign[:, 0:1], None, ALU.mult))
            V.tensor_scalar(rope_s[:, 0, :], ang[:, 2, :], SCORE_SCALE, None, ALU.mult)
            V.tensor_copy(rope_s[:, 1, :], ang[:, 2, :])
            V.tensor_scalar(rope_c[:, 0, :], ang[:, 3, :], SCORE_SCALE, None, ALU.mult)
            V.tensor_copy(rope_c[:, 1, :], ang[:, 3, :])

            dve.wait_ge(S["tok_rstd"], 1)
            with V.Fori(0, TOK_TILES // 2, 1) as i:
                for t in range(2):
                    dve.wait_ge(S["tok_transposed"], at(i, "tok_transposed", t - 1))
                    V.tensor_scalar(xnorm[:, t, :], xin[:, 2 * i + t, :], mv1[:, 2 * i + t, 0:1],
                                    rstd1[:, bass.ds(2 * i + t, 1)], ALU.subtract, ALU.mult).then_inc(S["tok_normed"], 1)
                dve.wait_ge(S["high_ready"], i + 1)
                V.tensor_tensor(flat(wqkv_l)[:, bass.ts(i, WPART)], wraw[:, bass.ts(i, WPART)],
                                flat(wqkv_h).bitcast(F32)[:, bass.ts(i, WPART)], ALU.subtract) \
                    .then_inc(S["low_ready"], 1)
                for t in range(2):
                    dve.wait_ge(S["tok_y"], at(i, "tok_y", t + 1))
                    V.bn_stats(stat2[:, 2 * i + t, :], ytok[:, 2 * i + t, :]).then_inc(S["tok_stats2"], 1)
            dve.wait_ge(S["tok_stats2"], TOK_TILES)
            for t in range(TOK_TILES):
                last = V.bn_aggr(mv2[:, t, :], stat2[:, t, :])
            link(last)
            V.tensor_scalar(mv2[:, :, 1], mv2[:, :, 1], EPS, None, ALU.add).then_inc(S["tok_stats2"], 1)

            dve.wait_ge(S["logs_ready"], 1)
            V.tensor_tensor(kbias[0:TOK, :, :], kbias[0:TOK, :, :],
                            bias_ps[0:TOK, :].unsqueeze(2).broadcast_to([TOK, HEADS, TOK]), ALU.mult)
            V.memset(xmax[:, :], 0.0)
            dve.wait_ge(S["tok_rstd2"], 1)
            for t in range(TOK_TILES):
                last = V.tensor_scalar(ytok[:, t, :], ytok[:, t, :], mv2[:, t, 0:1], rstd2[:, t:t + 1],
                                       ALU.subtract, ALU.mult)
            link(last)
            link(V.tensor_tensor(ytok[:, :, :], ytok[:, :, :], over(g2_sb, TOK_TILES), ALU.mult))
            for half in range(2):
                rows_ = slice(SEAT * half, SEAT * half + IMG_TOK)
                V.tensor_tensor(h[0:IMG_TOK, half:BATCHES:2, :], ytok[rows_, :, :], over(b2_sb, TOK_TILES, rows_),
                                ALU.add).then_inc(S["tok_placed"], 1)
            dve.wait_ge(S["wo_ready"], 1)
            V.tensor_tensor(flat(wo_l), wraw[:, 0:INNER_T * DM], flat(wo_h).bitcast(F32), ALU.subtract) \
                .then_inc(S["prologue_v"], 1)
            dve.wait_ge(S["prologue_v"], 1)
            dve.wait_ge(S["prologue_a"], 1)
            dve.wait_ge(S["tok_placed"], 2)
            dve.wait_ge(S["txt_in"], 16)
            dve.wait_ge(S["ffnw_in"], 32)

            def low_weights(fills):
                for r in fills:
                    dve.wait_ge(S["fw_high"], r + 1)
                    V.tensor_tensor(weight_fill(wgu_l, wdn_l, r), fill_view(r),
                                    weight_fill(wgu_h, wdn_h, r).bitcast(F32), ALU.subtract).then_inc(S["fw_low"], 1)

            def turn(g, now, prev, nxt):
                def statistics(group, st, m, stats):
                    for j in range(GROUP):
                        V.bn_stats(st[0:TOK, j, :], h[0:TOK, GROUP * group + j, :]).then_inc(S[stats], 1)
                    dve.wait_ge(S[stats], at(group, stats, GROUP))
                    V.memset(scal[:, 14:15], 0.0)
                    for j in range(GROUP):
                        V.bn_aggr(m[0:TOK, j, :], st[0:TOK, j, :]).then_inc(S[stats], 1)
                    dve.wait_ge(S[stats], at(group, stats, 2 * GROUP))
                    V.tensor_scalar(m[0:TOK, :, 1], m[0:TOK, :, 1], EPS, None, ALU.add).then_inc(S[stats], 1)

                def norm(group, m, r, dst, rooted, normed):
                    dve.wait_ge(S[rooted], at(group, rooted, 1))
                    for j in range(GROUP):
                        V.tensor_scalar(dst[0:TOK, j, :], h[0:TOK, GROUP * group + j, :], m[0:TOK, j, 0:1],
                                        r[0:TOK, j:j + 1], ALU.subtract, ALU.mult).then_inc(S[normed], 1)

                def rope(u, k):
                    dve.wait_ge(S["proj_done"], at(g, "proj_done", ITEMS * u + k + 1))
                    swapped = f"swapped{u % 2}"
                    if k == 0:
                        dve.wait_ge(S[swapped], at(g, swapped, 64 * (u // 2)))
                        dve.wait_ge(S["scores_done"], at(g, "scores_done", 2 * (u - 1)))
                    src = steps_view(ps[:, item_bank(u, k), 0:GTOK], GROUP)
                    for table, dst in ((rope_s, rs), (rope_c, qk)):
                        t = table[:, k // 2, :].unsqueeze(1).broadcast_to([P, GROUP, TOK])
                        last = V.tensor_tensor(steps_view(dst[:, u % 2, k, :], GROUP), src, t, ALU.mult)
                    last.then_inc(S["roped"], 1)

                def bias_and_max(n):
                    dve.wait_ge(S["scores_done"], at(g, "scores_done", n + 1))
                    dve.wait_ge(S["exped"], at(g, "exped", n - 1))
                    u = n // 2
                    kb = kbias[0:TOK, UHEADS * u:UHEADS * (u + 1), :].rearrange("p (e q) x -> p e (q x)", e=2)
                    V.tensor_tensor(s[0:TOK, n % 2, :, :].rearrange("p (e j q) x -> p e j (q x)", e=2, j=2),
                                    ps[0:TOK, BANK_S:BANK_S + 2, 0:UHEADS * TOK].rearrange("p e (j x) -> p e j x", j=2),
                                    kb.unsqueeze(2).broadcast_to([TOK, 2, 2, 2 * TOK]), ALU.add) \
                        .then_inc(S["biased"], 1)
                    dve.wait_ge(S["biased"], at(g, "biased", n + 1))
                    V.tensor_reduce(nmax[0:TOK, n % 2, :], s[0:TOK, n % 2, :, :], axis=AXX, op=ALU.max, negate=True) \
                        .then_inc(S["maxed"], 1)

                def o_low(n):
                    for jj in range(2):
                        j = 2 * (n % 2) + jj
                        dve.wait_ge(S["oth_ready"], at(g, "oth_ready", 2 * n + jj + 1))
                        at_ = (slice(None), o_rows(n), slice(j * TOK, (j + 1) * TOK))
                        V.tensor_tensor(otl[at_], o_t_view(jj), oth[at_].bitcast(F32), ALU.subtract) \
                            .then_inc(S["otl_ready"], 1)

                def normalise(n):
                    for jj in range(2):
                        dve.wait_ge(S["pv_done"], at(g, "pv_done", 2 * n + jj + 1))
                        o = ps[0:TOK, BANK_O + jj, 0:UHEADS * (HD + 1)].rearrange("p (h x) -> p h x", h=UHEADS)
                        V.reciprocal(rsum[0:TOK, jj, :], o[:, :, HD]).then_inc(S["o_summed"], 1)
                        dve.wait_ge(S["o_summed"], at(g, "o_summed", 2 * n + jj + 1))
                        dve.wait_ge(S["o_transposed"], at(g, "o_transposed", 2 * n + jj - 1))
                        V.tensor_tensor(on[0:TOK, jj, :].rearrange("p (h x) -> p h x", h=UHEADS), o[:, :, 0:HD],
                                        rsum[0:TOK, jj, :].unsqueeze(2).broadcast_to([TOK, UHEADS, HD]), ALU.mult) \
                            .then_inc(S["o_normed"], 1)

                def residual(j):
                    b = GROUP * (g - 1) + j
                    dve.wait_ge(S["ao_done"], at(g - 1, "ao_done", j + 1))
                    V.tensor_tensor(h[0:TOK, b, :], h[0:TOK, b, :], ps[0:TOK, ao_bank(j), 0:DM], ALU.add) \
                        .then_inc(S["h_added"], 1)

                for n in range(STEPS):
                    if has(n, now, prev):
                        bias_and_max(n)
                    if has(n - 2, now, prev):
                        o_low(n - 2)
                    for u, k in items_of(n, 0, now, nxt):
                        if k < UHEADS:
                            rope(u, k)
                    if n in AO_SLOTS and prev:
                        residual(AO_SLOTS[n])
                    for u, k in items_of(n, 1, now, nxt):
                        if k < UHEADS:
                            rope(u, k)
                    if n in AO_SLOTS and prev:
                        residual(AO_SLOTS[n] + 1)
                    if has(n - 1, now, prev):
                        normalise(n - 1)
                    if n == EARLY_SLOT and not now and prev:
                        low_weights(range(EARLY_FILLS))
                    if n == X2_SLOTS[0] and prev:
                        dve.wait_ge(S["h_added"], at(g - 1, "h_added", GROUP))
                        V.memset(scal[:, 13:14], 0.0)
                        statistics(g - 1, stat_f, mv_f, "ln2_stats")
                    if n == X_SLOTS[0] - 1 and nxt:
                        statistics(g + 1, stat, mv, "ln_stats")
                    if n == X2_SLOTS[1] and prev:
                        norm(g - 1, mv_f, rstd_f, xn2, "ln2_rstd", "x2_normed")
                        dve.wait_ge(S["x2_normed"], at(g - 1, "x2_normed", GROUP))
                        V.tensor_reduce(xmax[0:TOK, bass.ds(g - 1, 1)], xn2[0:TOK, :, :].rearrange("p j d -> p (j d)"),
                                        axis=AXX, op=ALU.max, apply_absolute_value=True).then_inc(S["xmax_ready"], 1)
                    if n == X_SLOTS[0] and nxt:
                        norm(g + 1, mv, rstd, xn, "ln_rstd", "x_normed")
                    if n == X_SLOTS[1] and nxt:
                        dve.wait_ge(S["xh_ready"], at(g + 1, "xh_ready", 1))
                        V.tensor_tensor(xl[:, :, :], ps[:, BANK_PJ:BANK_PJ + 2, 0:GTOK], xh[:, :, :].bitcast(F32),
                                        ALU.subtract).then_inc(S["xl_ready"], 1)
                    if n == 1 and now:
                        V.tensor_reduce(qmax[:, :], q_blocks(g), axis=AXX, op=ALU.max, apply_absolute_value=True) \
                            .then_inc(S["q_max"], 1)
                        dve.wait_ge(S["q_max"], at(g, "q_max", 1))
                        V.tensor_scalar(qmax[:, :], qmax[:, :], 1.0 / WMAX, TINY, ALU.mult, ALU.max) \
                            .then_inc(S["q_max"], 1)
                        dve.wait_ge(S["q_max"], at(g, "q_max", 2))
                        V.reciprocal(qinv[:, :], qmax[:, :]).then_inc(S["q_max"], 1)
                    if n == 3 and now:
                        part = wq[:, bass.ts(g, QPART)]
                        dve.wait_ge(S["q_scaled"], at(g, "q_scaled", 1))
                        V.tensor_scalar(part, part, RINT, RINT, ALU.add, ALU.subtract).then_inc(S["q_rounded"], 1)
                        dve.wait_ge(S["q_rounded"], at(g, "q_rounded", 1))
                        V.tensor_scalar(part, part, WMAX, -WMAX - 1.0, ALU.min, ALU.max).then_inc(S["q_rounded"], 1)

            turns(dve, turn)

            def col(n):
                return scal[:, n:n + 1]

            def scale_of(n, unit, s_, k_):
                dve.wait_ge(S["max_shared"], n + 1)
                if unit is None:
                    link(V.tensor_scalar(col(s_), gall[:, n:n + 1], 1.0 / ACTMAX, TINY, ALU.mult, ALU.max))
                    V.reciprocal(col(k_), col(s_)).then_inc(S["scales_ready"], 1)
                else:
                    link(V.tensor_scalar(col(s_), gall[:, n:n + 1], col(unit), 1.0 / ACTMAX, ALU.mult, ALU.mult))
                    link(V.tensor_scalar(col(s_), col(s_), TINY, None, ALU.max))
                    link(V.reciprocal(col(SCRATCH), col(s_)))
                    V.tensor_scalar(col(k_), col(SCRATCH), col(unit), None, ALU.mult).then_inc(S["scales_ready"], 1)

            dve.wait_ge(S["xmax_ready"], GROUPS)
            V.tensor_reduce(gred[:, 0:1], xmax[:, :], axis=AXX, op=ALU.max).then_inc(S["max_ready"], 1)
            low_weights(range(EARLY_FILLS, WFILLS - 2))
            scale_of(0, None, S_X, I_X)
            low_weights(range(WFILLS - 2, WFILLS))
            for g in range(GROUPS):
                dve.wait_ge(S["fx_rounded"], g + 1)
                V.tensor_tensor(fxl[:, :, of(g)], x_i[:, :, of(g)], fxh[:, :, of(g)].bitcast(F32), ALU.subtract) \
                    .then_inc(S["fx_ready"], 1)

            def gu_max(which, g, half):
                dve.wait_ge(S["gu_done"], 2 * g + (2 * GROUPS * which + half + 1))
                V.tensor_reduce(maxes[:, which, bass.ds(2 * g + half, 1)], ps[:, 3 * half:3 * half + 3, 0:GTOK],
                                axis=mybir.AxisListType.XY, op=ALU.max, apply_absolute_value=True) \
                    .then_inc(S["gu_maxed"], 1)

            def all_max(n, cols):
                V.tensor_reduce(gred[:, n:n + 1], maxes[:, n - 1, 0:cols], axis=AXX, op=ALU.max) \
                    .then_inc(S["max_ready"], 1)

            with V.Fori(0, GROUPS, 1) as g:
                gu_max(0, g, 0)
                gu_max(0, g, 1)
            dve.wait_ge(S["gu_maxed"], 2 * GROUPS)
            all_max(1, 2 * GROUPS)
            scale_of(1, S_X, S_GATE, K_GATE)
            def gated(g):
                dve.wait_ge(S["sig_rounded"], g + 1)
                V.scalar_tensor_tensor(out=gate[:, g, :], in0=sig_i[:, bass.ds(g % 2, 1), :], scalar=SIGLEVELS - 1.0,
                                       in1=gate_i[:, g, :], op0=ALU.min, op1=ALU.mult).then_inc(S["g2_ready"], 1)
                dve.wait_ge(S["g2_ready"], at(g, "g2_ready", 1))
                V.tensor_reduce(maxes[:, 2, bass.ds(g, 1)], gate[:, g, :], axis=AXX, op=ALU.max,
                                apply_absolute_value=True).then_inc(S["g2_maxed"], 1)

            gu_max(1, 0, 0)
            gu_max(1, 0, 1)
            with V.Fori(1, GROUPS, 1) as g:
                gu_max(1, g, 0)
                gated(g - 1)
                gu_max(1, g, 1)
            dve.wait_ge(S["gu_maxed"], 4 * GROUPS)
            all_max(2, 2 * GROUPS)
            gated(GROUPS - 1)
            dve.wait_ge(S["g2_maxed"], GROUPS)
            all_max(3, GROUPS)
            scale_of(2, S_X, S_UP, K_UP)
            link(V.tensor_scalar(col(U_G2), col(S_GATE), 1.0 / SIGLEVELS, None, ALU.mult))
            scale_of(3, U_G2, S_G2, K_G2)
            with V.Fori(0, GROUPS, 1) as g:
                dve.wait_ge(S["g2_rounded"], g + 1)
                dve.wait_ge(S["up_rounded"], g + 1)
                V.tensor_tensor(gate[:, g, :], gate_i[:, g, :], up_i[:, g, :], ALU.mult).then_inc(S["o_ready"], 1)
                dve.wait_ge(S["o_ready"], g + 1)
                V.tensor_reduce(maxes[:, 3, bass.ds(g, 1)], gate[:, g, :], axis=AXX, op=ALU.max,
                                apply_absolute_value=True).then_inc(S["o_maxed"], 1)
            dve.wait_ge(S["o_maxed"], GROUPS)
            all_max(4, GROUPS)
            link(V.tensor_tensor(col(U_O), col(S_G2), col(S_UP), ALU.mult))
            scale_of(4, U_O, S_O, K_O)
            with V.Fori(0, GROUPS, 1) as g:
                dve.wait_ge(S["o_high"], g + 1)
                dve.wait_ge(S["o_rounded"], g + 1)
                V.tensor_tensor(fo_l[:, g, :], up_i[:, g, :], fo_h[:, g, :].bitcast(F32), ALU.subtract) \
                    .then_inc(S["fo_ready"], 1)
            with V.Fori(0, GROUPS, 1) as g:
                dve.wait_ge(S["yt_transposed"], at(g, "yt_transposed", 1))
                hg = h[0:TOK, bass.ts(g, GROUP), :].rearrange("p j d -> p (j d)").rearrange("p (b x) -> p b x", b=2)
                V.tensor_tensor(hg, hg, ps[0:TOK, 2:4, :], ALU.add).then_inc(S["y_added"], 1)


S_X, I_X, S_GATE, K_GATE, S_UP, K_UP, U_G2, S_G2, K_G2, U_O, S_O, K_O, SCRATCH = range(13)
SMALLS = 2
OT_AT = 264
WFILLS = 2 * QT // 4 + FFN_T // 2


def kernel(x, txt, L0_tok_Wp, L0_tok_bp, L0_tok_ln1_g, L0_tok_ln1_b, L0_tok_ln2_g, L0_tok_ln2_b, L0_attn_qkv_w,
           L0_attn_out_w, L0_attn_bias_p, L0_attn_bias_a, L0_attn_rope_freqs, L0_ffn_w_gate, L0_ffn_w_up,
           L0_ffn_w_down):
    import concourse.bacc as bacc
    from concourse.bass_utils import run_bass_kernel_spmd

    def lay(a, *shape):
        return np.ascontiguousarray(np.asarray(a).reshape(shape))

    patches = np.asarray(x).reshape(BATCHES, CHANNELS, SIDE, PATCH, SIDE, PATCH).transpose(0, 2, 4, 3, 5, 1)

    def by_unit(a):
        return lay(np.asarray(a).reshape(UNITS, 2, 2).transpose(0, 2, 1), 1, HEADS)

    arrays = dict(
        patches=lay(patches, BATCHES, IMG_TOK, FEAT),
        txt=lay(txt, BATCHES, TXT_TOK, DM),
        wp=lay(L0_tok_Wp, FEAT, DM),
        cols=np.concatenate([lay(L0_tok_ln1_g, FEAT_T, P).T, lay(L0_tok_ln1_b, FEAT_T, P).T,
                             np.tile(lay(L0_attn_rope_freqs, HALF, 1), (P // HALF, 1))], axis=1),
        rows=np.concatenate([lay(L0_tok_bp, 1, DM), lay(L0_tok_ln2_g, 1, DM), lay(L0_tok_ln2_b, 1, DM),
                             by_unit(L0_attn_bias_p), by_unit(L0_attn_bias_a)], axis=1),
        wqkv=np.ascontiguousarray(np.asarray(L0_attn_qkv_w).T),
        wo=np.ascontiguousarray(np.asarray(L0_attn_out_w).T),
        wgu=np.concatenate([np.asarray(L0_ffn_w_gate), np.asarray(L0_ffn_w_up)]),
        wdn=lay(L0_ffn_w_down, DM, FFN),
    )
    arrays = {name: np.ascontiguousarray(a) for name, a in arrays.items()}
    nc = bacc.Bacc("TRN2", target_bir_lowering=False, num_devices=1)
    args = [nc.dram_tensor(name, a.shape, mybir.dt.from_np(a.dtype), kind="ExternalInput").ap()
            for name, a in arrays.items()]
    args.append(nc.dram_tensor("out", (BATCHES, TOK, DM), F32, kind="ExternalOutput").ap())
    build(nc, *args)
    r = run_bass_kernel_spmd(nc, [arrays], core_ids=[0])
    return r.results[0]["out"]
```

```python
from contextlib import ExitStack

import numpy as np
import concourse.bass as bass
from concourse import mybir

F32 = mybir.dt.float32
F32R = mybir.dt.float32r
I32 = mybir.dt.int32
ACT = mybir.ActivationFunctionType
ALU = mybir.AluOpType
AXX = mybir.AxisListType.X

P = 128
BATCHES, CHANNELS, IMG, PATCH = 16, 3, 112, 16
SIDE = IMG // PATCH
IMG_TOK = SIDE * SIDE
TXT_TOK = 32
TOK = IMG_TOK + TXT_TOK
FEAT = PATCH * PATCH * CHANNELS
FEAT_T = FEAT // P
DM = 256
DM_T = DM // P
HEADS, HD = 16, 64
HALF = HD // 2
INNER = HEADS * HD
INNER_T = INNER // P
FFN = 768
FFN_T = FFN // P
GROUP = 4
GROUPS = BATCHES // GROUP
GTOK = GROUP * TOK
UNITS = 4
UHEADS = HEADS // UNITS
STEPS = 2 * UNITS
ITEMS = 8
TOK_TILES = BATCHES // 2
SEAT = 64
QBLOCK = 32
QT = 2 * FFN_T
QPART = (QT * DM + DM_T * FFN) // GROUPS

EPS = 1e-5
SCORE_SCALE = 1.0 / float(np.sqrt(HD))
TOK_TURNS = TOK_TILES // 2
WPART = DM_T * 3 * INNER // TOK_TURNS
OPART = INNER_T * DM // TOK_TURNS
STAT_PARTS = ((0, 1), (1, 2), (2, 4), (4, TOK_TILES))
LOADS = ((0, 1), (1, 2), (2, 4), (4, TOK_TILES))
WMAX = 7.0
ACTMAX = 32767.0
SIGLEVELS = 65536.0
TINY = 1e-12
RINT = 12582912.0
AO_PLACES = {(1, 1): ("project", 0), (2, 0): ("project", 1), (2, 1): ("return", 0), (3, 0): ("return", 1)}
X2_STATS, X2_NORM, X2_TURN, X2_MAX = 4, 6, 6, 6
X_STATS, X_NORM, X_TURN = 2, 4, 5
Q_SCALE, Q_ROUND = 0, 2
FIRST = 2
EARLY_SLOT, LATE_SLOT = 0, 3
EARLY_FILLS = 6
PI = 3.1415925
TWO_PI = 2.0 * float(np.pi)
PI_A = 6.28125
PI_B = float(np.float32(np.round((TWO_PI - PI_A) * 2.0**21) / 2.0**21))
PI_C = float(np.float32(TWO_PI - PI_A - PI_B))

BANK_S = 0
BANK_PT = 2
BANK_O = 4
BANK_PJ = 6


def build(nc, patches, txt, wp, cols, rows, wqkv, wo, wgu, wdn, out):
    ctx = ExitStack()
    with ctx:
        def sb(name, shape, dt=F32, where=ctx):
            return where.enter_context(nc.sbuf_tensor(name, shape, dt))

        ident = sb("ident", [P, P])
        ones = sb("ones", [P, P])
        neg_half = sb("neg_half", [P, BATCHES])
        h = sb("h", [P, BATCHES, DM])
        ffn_x = sb("ffn_x", [P, DM_T, BATCHES * TOK])
        wq = sb("wq", [P, QT * DM + DM_T * FFN])
        xmax = sb("xmax", [P, GROUPS])
        gred = sb("gred", [P, 5])
        gall = sb("gall", [P, 5])
        idle = sb("idle", [P, 2])
        scal = sb("scal", [P, 16])

        wq_gu = wq[:, 0:QT * DM].rearrange("p (t i) -> p t i", t=QT)
        wq_dn = wq[:, QT * DM:].rearrange("p (t i) -> p t i", t=DM_T)

        att = ExitStack()
        wqkv_h = sb("wqkv_h", [P, DM_T, 3 * INNER], F32R, att)
        raw = ExitStack()
        wqkv_raw = sb("wqkv_raw", [P, DM_T, 3 * INNER], where=raw)
        raw.close()
        wqkv_l = sb("wqkv_l", [P, DM_T, 3 * INNER], F32R, att)
        wo_h = sb("wo_h", [P, INNER_T, DM], F32R, att)
        wo_raw = sb("wo_raw", [P, INNER_T, DM], where=raw)
        raw.close()
        wo_l = sb("wo_l", [P, INNER_T, DM], F32R, att)
        rope_c = sb("rope_c", [P, 2, TOK], where=att)
        rope_s = sb("rope_s", [P, 2, TOK], where=att)
        kbias = sb("kbias", [P, HEADS, TOK], where=att)
        xh = sb("xh", [P, DM_T, GTOK], F32R, att)
        xl = sb("xl", [P, DM_T, GTOK], F32R, att)
        xn = sb("xn", [P, GROUP, DM], where=att)
        stat = sb("stat", [P, GROUP, 6], where=att)
        mv = sb("mv", [P, GROUP, 2], where=att)
        rstd = sb("rstd", [P, GROUP], where=att)
        v = sb("v", [P, 2, GROUP, UHEADS, HD + 1], where=att)

        pro = ExitStack()
        xin = sb("xin", [P, TOK_TILES, FEAT], where=pro)
        xnt = sb("xnt", [P, 2, FEAT_T, P], where=pro)
        xnorm = sb("xnorm", [P, 2, FEAT], where=pro)
        ytok = sb("ytok", [P, 2, DM], where=pro)
        wp_sb = sb("wp_sb", [P, FEAT_T, DM], where=pro)
        wp_g = sb("wp_g", [P, FEAT_T, DM], where=pro)
        bias_tok = sb("bias_tok", [1, DM], where=pro)
        cols_sb = sb("cols_sb", [P, 2 * FEAT_T + 1], where=pro)
        rows_sb = sb("rows_sb", [P, 3 * DM + 2 * HEADS], where=pro)
        stat1 = sb("stat1", [P, TOK_TILES, 2, 6], where=pro)
        mv1 = sb("mv1", [P, TOK_TILES, 2], where=pro)
        rstd1 = sb("rstd1", [P, TOK_TILES], where=pro)
        stat2 = sb("stat2", [P, 2, 6], where=pro)
        mv2 = sb("mv2", [P, 2, 2], where=pro)
        rstd2 = sb("rstd2", [P, 2], where=pro)
        sign = sb("sign", [P, 1], where=pro)
        pos_i = sb("pos_i", [P, TOK], I32, pro)
        dist_i = sb("dist_i", [P, TOK], I32, pro)
        dist = sb("dist", [P, TOK], where=pro)
        ang = sb("ang", [P, 4, TOK], where=pro)
        pro.close()

        g1_sb, b1_sb, freq = cols_sb[:, 0:FEAT_T], cols_sb[:, FEAT_T:2 * FEAT_T], cols_sb[:, 2 * FEAT_T:2 * FEAT_T + 1]
        bp_sb, g2_sb, b2_sb = (rows_sb[:, DM * i:DM * (i + 1)] for i in range(3))
        bias_ps, bias_as = (rows_sb[:, 3 * DM + HEADS * i:3 * DM + HEADS * (i + 1)] for i in range(2))

        xn2 = sb("xn2", [P, GROUP, DM], where=att)
        qmax = sb("qmax", [P, QPART // QBLOCK], where=att)
        qinv = sb("qinv", [P, QPART // QBLOCK], where=att)
        stat_f = sb("stat_f", [P, GROUP, 6], where=att)
        mv_f = sb("mv_f", [P, GROUP, 2], where=att)
        rstd_f = sb("rstd_f", [P, GROUP], where=att)
        rs = sb("rs", [P, 2, UHEADS, GTOK], where=att)
        rsx = sb("rsx", [P, 2, UHEADS, GTOK], where=att)
        qk = sb("qk", [P, 2, UHEADS, GTOK], where=att)
        s = sb("s", [P, 2, 2 * UHEADS, TOK], where=att)
        nmax = sb("nmax", [P, 2, 2 * UHEADS], where=att)
        pr = sb("pr", [P, 2, 2 * UHEADS, TOK], where=att)
        pt = sb("pt", [P, 2, UHEADS, TOK], where=att)
        rsum = sb("rsum", [P, 2, UHEADS], where=att)
        on = sb("on", [P, 2, UHEADS * HD], where=att)
        ot = sb("ot", [P, DM_T, GTOK], where=att)
        oth = sb("oth", [P, INNER_T, GTOK], F32R, att)
        otl = sb("otl", [P, INNER_T, GTOK], F32R, att)
        att.close()

        wgu_h = sb("wgu_h", [P, DM_T, QT * P], F32R)
        wgu_l = sb("wgu_l", [P, DM_T, QT * P], F32R)
        wdn_h = sb("wdn_h", [P, FFN_T, DM], F32R)
        wdn_l = sb("wdn_l", [P, FFN_T, DM], F32R)
        yt = sb("yt", [P, DM_T, GTOK])
        maxes = sb("maxes", [P, 4, 2 * GROUPS])
        gate = sb("gate", [P, GROUPS, FFN_T * GTOK])
        fu = ExitStack()
        up = sb("up", [P, GROUPS, FFN_T * GTOK], where=fu)
        fu.close()
        fo_l = sb("fo_l", [P, GROUPS, FFN_T * GTOK], F32R)
        fx = ExitStack()
        fxh = sb("fxh", [P, DM_T, BATCHES * TOK], F32R, fx)
        fxl = sb("fxl", [P, DM_T, BATCHES * TOK], F32R, fx)
        sig = sb("sig", [P, 2, FFN_T * GTOK], where=fx)
        x_i = sb("x_i", [P, DM_T, BATCHES * TOK], I32, fx)
        fx.close()
        fo_h = sb("fo_h", [P, GROUPS, FFN_T * GTOK], F32R)
        gate_i, up_i, sig_i = (t[:, :, :].bitcast(I32) for t in (gate, up, sig))

        ps = ctx.enter_context(nc.psum_tensor("ps", [P, 8, 512], F32))

        names = (
            "txt_in wp_in cols_in rows_in wqkv_in wo_in ffnw_in out_stored "
            "consts iotas ident_ready tok_stats tok_rstd tok_normed tok_transposed tok_evac tok_product "
            "tok_y tok_stats2 tok_rstd2 tok_scaled tok_placed bias_product angles_ready sines_ready "
            "logs_ready tables_ready high_ready low_ready vstep prologue_v prologue_a "
            "ln_stats ln_rstd x_normed x_transposed xh_ready xl_ready proj_done roped swapped0 swapped1 "
            "qk_ready v_ready scores_done biased maxed exped p_transposed pt_ready pv_done "
            "o_summed o_normed o_transposed oth_ready otl_ready ao_done ot_ready ao_returned h_added ln2_stats ln2_rstd x2_normed "
            "x2_transposed x2_copied xmax_ready q_max q_scaled q_rounded q_done "
            "fw_transposed fw_high fw_low max_ready max_shared scales_ready fx_high fx_rounded fx_ready gu_done gu_maxed "
            "gu_copied gate_rounded sig_done sig_rounded g2_ready g2_maxed up_rounded g2_rounded last_floats o_ready last_product o_maxed "
            "o_high o_rounded fo_ready down_done yt_ready yt_transposed y_added"
        ).split()
        S = {n: ctx.enter_context(nc.semaphore(n)) for n in names}
        patches_in = [ctx.enter_context(nc.semaphore(f"patches_in{n}")) for n in range(len(LOADS))]
        block = ctx.enter_context(nc.Block())

        PER = dict(
            ln_stats=2 * GROUP + 1, ln_rstd=1, x_normed=GROUP, x_transposed=1, xh_ready=1, xl_ready=1,
            proj_done=UNITS * ITEMS, roped=UNITS * UHEADS, swapped0=UNITS // 2 * 64, swapped1=UNITS // 2 * 64,
            qk_ready=UNITS * UHEADS, v_ready=UNITS * GROUP, scores_done=STEPS, biased=STEPS, maxed=STEPS,
            exped=STEPS, p_transposed=2 * STEPS, pt_ready=2 * STEPS, pv_done=2 * STEPS,
            o_summed=2 * STEPS, o_normed=2 * STEPS, o_transposed=2 * STEPS, oth_ready=2 * STEPS,
            otl_ready=2 * STEPS, ao_done=2, ot_ready=2, ao_returned=2, h_added=2, ln2_stats=2 * GROUP + 1, ln2_rstd=1,
            x2_normed=GROUP, x2_transposed=1, x2_copied=1, xmax_ready=1, q_max=3, q_scaled=1, q_rounded=2, q_done=1,
            down_done=DM_T, yt_ready=DM_T,
            tok_normed=2, tok_transposed=2, tok_evac=2, tok_product=2, tok_y=2, tok_stats2=5,
            tok_rstd2=1, tok_scaled=2, tok_placed=4)
        SEEDS = dict(tok_transposed=2, tok_product=2, tok_evac=2, tok_y=2, tok_placed=4, biased=1, exped=2, p_transposed=4,
                     pt_ready=2, pv_done=8, o_transposed=2, otl_ready=2, qk_ready=8,
                     scores_done=4, yt_ready=DM_T, g2_ready=2, swapped0=16, swapped1=16, x2_copied=1, ao_done=2, ao_returned=2, gu_copied=2, yt_transposed=1,
                     y_added=1)

        def at(i, name, n):
            return i * PER.get(name, 1) + (SEEDS.get(name, 0) + n)

        def turns(eng, turn):
            turn(-1, False, False, True)
            turn(0, True, False, True)
            with eng.Fori(1, GROUPS - 1, 1) as g:
                turn(g, True, True, True)
            turn(GROUPS - 1, True, True, False)
            turn(GROUPS, False, True, False)

        def has(n, now, prev):
            return (now if n >= 0 else prev) and n < STEPS

        def items_of(n, half, now, nxt):
            unit, pair = divmod(2 * n + half + 1, ITEMS // 2)
            unit += 1
            if not (nxt if unit >= UNITS else now):
                return []
            return [(unit, 2 * pair), (unit, 2 * pair + 1)]

        def tenants(n, now, prev, nxt):
            out = []
            for half in range(2):
                out.append([("item", u, k) for u, k in items_of(n, half, now, nxt)])
                if (n, half) in AO_PLACES and prev:
                    out[half].append(AO_PLACES[n, half] + (0,))
            return out

        def item_bank(u, k):
            n, half = divmod(ITEMS // 2 * (u - 1) - 1 + k // 2, 2)
            return BANK_PJ + (k + (half == 0 and (n, half) in AO_PLACES)) % 2

        def ao_bank(j):
            return BANK_PJ + j

        def steps_view(ap, cols):
            return ap.rearrange("p (j x) -> p j x", j=cols)

        def o_t_view(jj):
            return ps[:, BANK_O + jj, OT_AT:OT_AT + 2 * TOK].rearrange("p (c x) -> p c x", c=2)

        def o_rows(n):
            u = n % STEPS // 2
            return slice(2 * u, 2 * u + 2)

        def fill_view(r):
            return ps[:, r % 4 if r < EARLY_FILLS else r - 3, :]

        def weight_fill(gu, dn, r):
            if r < 2 * QT // 4:
                c, q = r // (QT // 4), r % (QT // 4)
                return gu[:, c, 512 * q:512 * q + 512]
            m = 2 * (r - 2 * QT // 4)
            return dn[:, m:m + 2, :].rearrange("p m d -> p (m d)")

        def of(g):
            return slice(g * GTOK, (g + 1) * GTOK)

        def pieces(t):
            return t[:, :, :].rearrange("p g (a x) -> p (g a) x", a=2)

        def flat(t):
            return t[:, :, :].rearrange("p c d -> p (c d)")

        def q_blocks(g):
            return wq[:, bass.ts(g, QPART)].rearrange("p (b i) -> p b i", i=QBLOCK)

        def by_block(ap):
            return ap[:, :].unsqueeze(2).broadcast_to([P, QPART // QBLOCK, QBLOCK])

        def over(ap, n, rows=slice(0, P)):
            return ap[rows, :].unsqueeze(1).broadcast_to([rows.stop - rows.start, n, DM])

        def split_low(eng, raw, high, low, i, n, part):
            at_ = slice(i * part, (i + 1) * part)
            eng.wait_ge(S["high_ready"], 2 * i + n)
            eng.tensor_tensor(flat(low)[:, at_], flat(raw)[:, at_], flat(high).bitcast(F32)[:, at_], ALU.subtract) \
                .then_inc(S["low_ready"], 1)

        def finish_rotation(eng, g, u):
            swapped = f"swapped{u % 2}"
            eng.wait_ge(S[swapped], at(g, swapped, 64 * (u // 2 + 1)))
            for i in range(UHEADS):
                eng.tensor_tensor(qk[:, u % 2, i, :], qk[:, u % 2, i, :], rsx[:, u % 2, i, :], ALU.add) \
                    .then_inc(S["qk_ready"], 1)

        @block.sync
        def _(sp):
            for n, (a, b) in enumerate(LOADS):
                if a == 2:
                    sp.dma_start(wp_sb[:, :, :], wp.rearrange("(c p) d -> p c d", p=P)).then_inc(S["wp_in"], 16)
                for half in range(2):
                    whole = b - a - (1 if half and b == TOK_TILES else 0)
                    start = (2 * a + half) * IMG_TOK * FEAT
                    src = bass.AP(patches.tensor, patches.offset + start,
                                  [[FEAT, SEAT], [2 * IMG_TOK * FEAT, whole], [1, FEAT]])
                    sp.dma_start(xin[SEAT * half:SEAT * half + SEAT, a:a + whole, :], src).then_inc(patches_in[n], 16)
            sp.dma_start(xin[SEAT:SEAT + IMG_TOK, TOK_TILES - 1, :], patches[BATCHES - 1]) \
                .then_inc(patches_in[-1], 16)
            sp.dma_start(xin[SEAT + IMG_TOK:2 * SEAT, TOK_TILES - 1, :], patches[0, 0:SEAT - IMG_TOK, :]) \
                .then_inc(patches_in[-1], 16)
            sp.dma_start(wqkv_raw[:, :, :], wqkv.rearrange("(c p) n -> p c n", p=P)) \
                .then_inc(S["wqkv_in"], 16)
            sp.dma_start(h[IMG_TOK:TOK, :, :], txt.rearrange("b t d -> t b d")).then_inc(S["txt_in"], 16)
            sp.dma_start(wo_raw[:, :, :], wo.rearrange("(c p) d -> p c d", p=P)).then_inc(S["wo_in"], 16)
            sp.dma_start(wq_gu, wgu.rearrange("(t p) i -> p t i", p=P)).then_inc(S["ffnw_in"], 16)
            sp.dma_start(wq_dn, wdn.rearrange("(t p) i -> p t i", p=P)).then_inc(S["ffnw_in"], 16)

            sp.wait_ge(S["prologue_v"], 1)
            sp.wait_ge(S["prologue_a"], 1)

            def turn(g, now, prev, nxt):
                for n in range(0, STEPS, 2):
                    for u, _ in items_of(n, 0, now, nxt)[:1]:
                        swapped = f"swapped{u % 2}"
                        sp.wait_ge(S["roped"], at(g, "roped", UHEADS * (u + 1)))
                        sp.wait_ge(S["qk_ready"], at(g, "qk_ready", UHEADS * (u - 1)))
                        for q in range(4):
                            sp.dma_start(rsx[32 * q:32 * q + 32, u % 2], rs[32 * (q ^ 1):32 * (q ^ 1) + 32, u % 2]) \
                                .then_inc(S[swapped], 16)

            turns(sp, turn)

            out_g = out.rearrange("(g j) t d -> g t j d", g=GROUPS)
            with sp.Fori(0, GROUPS, 1) as g:
                sp.wait_ge(S["y_added"], at(g, "y_added", 1))
                sp.dma_start(out_g[g], h[0:TOK, bass.ts(g, GROUP), :]).then_inc(S["out_stored"], 16)
            sp.wait_ge(S["out_stored"], 16 * GROUPS)

        @block.gpsimd
        def _(pool):
            for name, n in SEEDS.items():
                pool.sem_inc(S[name], n)
            nc.gpsimd.memset(neg_half[:, :], -0.5).then_inc(S["consts"], 1)
            nc.gpsimd.memset(ones[:, :], 1.0).then_inc(S["consts"], 1)
            nc.gpsimd.memset(v[:, :, :, :, HD:HD + 1].rearrange("p a j h c -> p (a j h) c"), 1.0) \
                .then_inc(S["consts"], 1)
            nc.gpsimd.iota(pos_i[:, :], [[1, TOK]], base=0, channel_multiplier=0).then_inc(S["iotas"], 1)
            nc.gpsimd.iota(dist_i[:, :], [[1, TOK]], base=0, channel_multiplier=-1).then_inc(S["iotas"], 1)
            pool.wait_ge(S["consts"], 3)
            nc.gpsimd.affine_select(out=ident[:, :], in_=ones[:, :], compare_op=ALU.is_equal, fill=0.0, base=0,
                                    pattern=[[-1, P]], channel_multiplier=1).then_inc(S["ident_ready"], 1)
            for n, (a, b) in enumerate(STAT_PARTS):
                pool.wait_ge(S["tok_stats"], n + 1)
                nc.gpsimd.tensor_tensor(rstd1[:, a:b], mv1[:, a:b, 1], neg_half[:, a:b], ALU.pow) \
                    .then_inc(S["tok_rstd"], 1)
            def root(of, rooted, group, m, r):
                pool.wait_ge(S[of], at(group, of, PER[of]))
                nc.gpsimd.tensor_tensor(r[0:TOK, :], m[0:TOK, :, 1], neg_half[0:TOK, 0:GROUP], ALU.pow) \
                    .then_inc(S[rooted], 1)

            for i in range(TOK_TURNS):
                if i == TOK_TURNS - 2:
                    root("ln_stats", "ln_rstd", 0, mv, rstd)
                pool.wait_ge(S["tok_stats2"], at(i, "tok_stats2", 5))
                nc.gpsimd.tensor_tensor(rstd2[:, :], mv2[:, :, 1], neg_half[:, 0:2], ALU.pow) \
                    .then_inc(S["tok_rstd2"], 1)
                if i < TOK_TURNS - 1:
                    split_low(nc.gpsimd, wqkv_raw, wqkv_h, wqkv_l, i, 1, WPART)
                split_low(nc.gpsimd, wo_raw, wo_h, wo_l, i, 2, OPART)

            def turn(g, now, prev, nxt):
                def carry(n):
                    nc.gpsimd.tensor_tensor(idle[:, n:n + 1], neg_half[:, 0:1], neg_half[:, 0:1], ALU.mult)

                for n in range(STEPS):
                    if n == X2_STATS + 1 and prev:
                        root("ln2_stats", "ln2_rstd", g - 1, mv_f, rstd_f)
                    if n % 2 == 0 and now:
                        for u, _ in items_of(n, 0, now, nxt)[:1]:
                            finish_rotation(nc.gpsimd, g, u)
                    if n == X_STATS and now and nxt:
                        root("ln_stats", "ln_rstd", g + 1, mv, rstd)
                    if n == Q_SCALE and now:
                        pool.wait_ge(S["q_max"], at(g, "q_max", 3))
                        carry(0)
                        nc.gpsimd.tensor_tensor(q_blocks(g), q_blocks(g), by_block(qinv), ALU.mult) \
                            .then_inc(S["q_scaled"], 1)
                    if n == Q_ROUND + 1 and now:
                        pool.wait_ge(S["q_rounded"], at(g, "q_rounded", 2))
                        carry(1)
                        nc.gpsimd.tensor_tensor(q_blocks(g), q_blocks(g), by_block(qmax), ALU.mult) \
                            .then_inc(S["q_done"], 1)

            turns(pool, turn)

            def share_max(n):
                pool.wait_ge(S["max_ready"], n + 1)
                nc.gpsimd.partition_all_reduce(gall[:, n:n + 1], gred[:, n:n + 1], P, bass.bass_isa.ReduceOp.max) \
                    .then_inc(S["max_shared"], 1)

            def to_integers(dst, src, factor):
                return nc.gpsimd.tensor_scalar(dst, src, factor, 0.0, ALU.mult, ALU.add)

            share_max(0)
            pool.wait_ge(S["scales_ready"], 1)
            pool.wait_ge(S["x2_copied"], at(GROUPS - 1, "x2_copied", 1))
            for g in range(GROUPS):
                to_integers(x_i[:, :, of(g)], ffn_x[:, :, of(g)], scal[:, I_X:I_X + 1]).then_inc(S["fx_rounded"], 1)
            share_max(1)

            def round_gate(g):
                to_integers(gate_i[:, g, :], gate[:, g, :], scal[:, K_GATE:K_GATE + 1]).then_inc(S["gate_rounded"], 1)

            pool.wait_ge(S["scales_ready"], 2)
            pool.wait_ge(S["gu_copied"], 2 * GROUPS + SEEDS["gu_copied"])
            round_gate(0)
            for g in range(GROUPS):
                if g + 1 < GROUPS:
                    round_gate(g + 1)
                pool.wait_ge(S["sig_done"], g + 1)
                to_integers(sig_i[:, g % 2, :], sig[:, g % 2, :], SIGLEVELS) \
                    .then_inc(S["sig_rounded"], 1)
            share_max(2)
            pool.wait_ge(S["scales_ready"], 3)
            pool.wait_ge(S["gu_copied"], 4 * GROUPS + SEEDS["gu_copied"])
            for g in range(GROUPS):
                if g == 1:
                    share_max(3)
                to_integers(up_i[:, g, :], up[:, g, :], scal[:, K_UP:K_UP + 1]).then_inc(S["up_rounded"], 1)
            pool.wait_ge(S["last_floats"], 2)
            nc.gpsimd.tensor_tensor(gate[:, GROUPS - 1, :], gate[:, GROUPS - 1, :], up[:, GROUPS - 1, :], ALU.mult) \
                .then_inc(S["last_product"], 1)
            share_max(4)
            pool.wait_ge(S["scales_ready"], 5)
            for n in range(2 * GROUPS):
                to_integers(pieces(up_i)[:, n, :], pieces(gate)[:, n, :], scal[:, K_O:K_O + 1]) \
                    .then_inc(S["o_rounded"], 1)

        @block.scalar
        def _(act):
            act.dma_start(cols_sb[:, :], cols).then_inc(S["cols_in"], 16)
            act.dma_start(rows_sb[:, :], rows.broadcast_to([P, 3 * DM + 2 * HEADS])).then_inc(S["rows_in"], 16)

            def evacuate(i, t):
                act.wait_ge(S["tok_transposed"], at(i, "tok_transposed", t + 1))
                act.wait_ge(S["tok_product"], at(i, "tok_product", t - 1))
                nc.scalar.activation(xnt[:, t, 0:4, :], ps[:, 2 * t, 0:4 * P].rearrange("p (c x) -> p c x", c=4),
                                     ACT.Copy)
                nc.scalar.activation(xnt[:, t, 4:6, :],
                                     ps[:, 2 * t + 1, 0:2 * P].rearrange("p (c x) -> p c x", c=2), ACT.Copy) \
                    .then_inc(S["tok_evac"], 1)

            def x_high(group):
                act.wait_ge(S["x_transposed"], at(group, "x_transposed", 1))
                nc.scalar.activation(xh[:, :, :], ps[:, BANK_PJ:BANK_PJ + 2, 0:GTOK], ACT.Copy) \
                    .then_inc(S["xh_ready"], 1)

            def tok_turn(i, more):
                def split_high(into, raw, part):
                    nc.scalar.activation(flat(into)[:, bass.ts(i, part)], flat(raw)[:, bass.ts(i, part)], ACT.Copy) \
                        .then_inc(S["high_ready"], 1)

                if not more:
                    split_high(wqkv_h, wqkv_raw, WPART)
                for t in range(2):
                    act.wait_ge(S["tok_product"], at(i, "tok_product", t + 1))
                    act.wait_ge(S["tok_placed"], at(i, "tok_placed", 0))
                    nc.scalar.activation(ytok[:, t, :], ps[:, 4 + t, 0:DM], ACT.Copy).then_inc(S["tok_y"], 1)
                    if more:
                        evacuate(i + 1, t)
                    elif t == 0:
                        x_high(0)
                if more:
                    act.wait_ge(S["wqkv_in"], 16)
                    split_high(wqkv_h, wqkv_raw, WPART)
                act.wait_ge(S["wo_in"], 16)
                split_high(wo_h, wo_raw, OPART)

            evacuate(0, 0)
            evacuate(0, 1)
            act.wait_ge(S["angles_ready"], 1)
            nc.scalar.activation(ang[:, 2:4, :], ang[:, 2:4, :], ACT.Sin).then_inc(S["sines_ready"], 1)
            act.wait_ge(S["angles_ready"], 2)
            for i in range(HEADS):
                last = nc.scalar.activation(kbias[0:TOK, i, :], dist[0:TOK, :], ACT.Ln, bias=1.0,
                                            scale=bias_as[0:TOK, i:i + 1])
            last.then_inc(S["logs_ready"], 1)
            with nc.scalar.Fori(0, TOK_TURNS - 1, 1) as i:
                tok_turn(i, True)
            tok_turn(TOK_TURNS - 1, False)
            act.wait_ge(S["prologue_v"], 1)
            nc.scalar.activation(scal[:, 15:16], ones[:, 0:1], ACT.Copy).then_inc(S["prologue_a"], 1)

            def high_weights(fills):
                for r in fills:
                    act.wait_ge(S["fw_transposed"], r + 1)
                    nc.scalar.activation(weight_fill(wgu_h, wdn_h, r), fill_view(r), ACT.Copy) \
                        .then_inc(S["fw_high"], 1)

            def turn(g, now, prev, nxt):
                def v_item(u, k):
                    j = k - UHEADS
                    act.wait_ge(S["proj_done"], at(g, "proj_done", ITEMS * u + k + 1))
                    act.wait_ge(S["pv_done"], at(g, "pv_done", 4 * (u - 1) - (2 if j < 2 else 0)))
                    nc.scalar.activation(v[0:TOK, u % 2, j, :, 0:HD],
                                         ps[0:TOK, item_bank(u, k), 0:UHEADS * HD].rearrange("p (h d) -> p h d", h=UHEADS),
                                         ACT.Copy).then_inc(S["v_ready"], 1)

                def o_high(n):
                    for jj in range(2):
                        j = 2 * (n % 2) + jj
                        act.wait_ge(S["o_transposed"], at(g, "o_transposed", 2 * n + jj + 1))
                        if n % STEPS < 2:
                            act.wait_ge(S["ao_done"], at(g, "ao_done", 0))
                        nc.scalar.activation(oth[:, o_rows(n), j * TOK:(j + 1) * TOK],
                                             o_t_view(jj), ACT.Copy).then_inc(S["oth_ready"], 1)

                def p_evac(n):
                    for jj in range(2):
                        act.wait_ge(S["p_transposed"], at(g, "p_transposed", 2 * n + jj + 1))
                        act.wait_ge(S["pv_done"], at(g, "pv_done", 2 * n + jj - 1))
                        nc.scalar.activation(pt[0:TOK, jj, :, :],
                                             ps[0:TOK, BANK_PT + jj, 0:UHEADS * TOK].rearrange("p (h x) -> p h x", h=UHEADS),
                                             ACT.Copy).then_inc(S["pt_ready"], 1)

                def exps(n):
                    act.wait_ge(S["maxed"], at(g, "maxed", n + 1))
                    act.wait_ge(S["p_transposed"], at(g, "p_transposed", 2 * (n - 1)))
                    for i in range(2 * UHEADS):
                        last = nc.scalar.activation(pr[0:TOK, n % 2, i, :], s[0:TOK, n % 2, i, :], ACT.Exp,
                                                    bias=nmax[0:TOK, n % 2, i:i + 1], scale=1.0)
                    last.then_inc(S["exped"], 1)

                def projected(n, half):
                    what, mo = AO_PLACES.get((n, half), ("", 0))
                    if what == "project" and prev:
                        act.wait_ge(S["ao_done"], at(g - 1, "ao_done", mo + 1))
                        act.wait_ge(S["ao_returned"], at(g - 1, "ao_returned", 0))
                        nc.scalar.activation(ot[:, mo, :], ps[:, ao_bank(mo), 0:GTOK], ACT.Copy) \
                            .then_inc(S["ot_ready"], 1)

                for n in range(STEPS):
                    for u, k in items_of(n, 0, now, nxt):
                        if k >= UHEADS:
                            v_item(u, k)
                    projected(n, 0)
                    if has(n - 2, now, prev):
                        o_high(n - 2)
                    if n == EARLY_SLOT + 1 and not now and prev:
                        high_weights(range(EARLY_FILLS // 2, EARLY_FILLS))
                    if n == X_TURN and now and nxt:
                        x_high(g + 1)
                    if has(n - 1, now, prev):
                        p_evac(n - 1)
                    for u, k in items_of(n, 1, now, nxt):
                        if k >= UHEADS:
                            v_item(u, k)
                    if has(n, now, prev):
                        exps(n)
                    projected(n, 1)
                    if n == EARLY_SLOT and not now and prev:
                        high_weights(range(EARLY_FILLS // 2))
                    if n == LATE_SLOT and not now and prev:
                        high_weights(range(EARLY_FILLS, WFILLS))
                    if n == X2_TURN and prev:
                        act.wait_ge(S["x2_transposed"], at(g - 1, "x2_transposed", 1))
                        nc.scalar.activation(ffn_x[:, :, bass.ts(g - 1, GTOK)], ps[:, BANK_PJ:BANK_PJ + 2, 0:GTOK],
                                             ACT.Copy).then_inc(S["x2_copied"], 1)

            turns(act, turn)

            act.wait_ge(S["x2_copied"], at(GROUPS - 1, "x2_copied", 1))
            act.wait_ge(S["scales_ready"], 1)
            for g in range(GROUPS):
                nc.scalar.activation(fxh[:, :, of(g)], ffn_x[:, :, of(g)], ACT.Copy, scale=scal[:, I_X:I_X + 1]) \
                    .then_inc(S["fx_high"], 1)

            def gu_copy(which, g, half):
                dst = (gate, up)[which][:, g, half * (FFN_T // 2) * GTOK:(half + 1) * (FFN_T // 2) * GTOK]
                act.wait_ge(S["gu_maxed"], 2 * g + (2 * GROUPS * which + half + 1))
                nc.scalar.activation(dst.rearrange("p (m x) -> p m x", m=FFN_T // 2),
                                     ps[:, 3 * half:3 * half + 3, 0:GTOK], ACT.Copy).then_inc(S["gu_copied"], 1)

            with nc.scalar.Fori(0, GROUPS, 1) as g:
                gu_copy(0, g, 0)
                gu_copy(0, g, 1)
            act.wait_ge(S["scales_ready"], 2)
            nc.scalar.activation(scal[:, 15:16], ones[:, 0:1], ACT.Sigmoid)
            for g in range(GROUPS):
                gu_copy(1, g, 0)
                act.wait_ge(S["gate_rounded"], g + 1)
                act.wait_ge(S["g2_ready"], at(g, "g2_ready", -1))
                nc.scalar.activation(sig[:, g % 2, :], gate_i[:, g, :], ACT.Sigmoid,
                                     scale=scal[:, S_GATE:S_GATE + 1]).then_inc(S["sig_done"], 1)
                gu_copy(1, g, 1)
            nc.scalar.activation(scal[:, 15:16], ones[:, 0:1], ACT.Copy, scale=scal[:, S_GATE:S_GATE + 1])
            act.wait_ge(S["scales_ready"], 4)
            with nc.scalar.Fori(1, GROUPS, 1) as g:
                nc.scalar.activation(gate_i[:, g, :], gate[:, g, :], ACT.Copy, scale=scal[:, K_G2:K_G2 + 1]) \
                    .then_inc(S["g2_rounded"], 1)
            act.wait_ge(S["g2_rounded"], GROUPS - 1)
            nc.scalar.activation(gate[:, GROUPS - 1, :], gate_i[:, GROUPS - 1, :], ACT.Copy).then_inc(S["last_floats"], 1)
            act.wait_ge(S["up_rounded"], GROUPS)
            nc.scalar.activation(up[:, GROUPS - 1, :], up_i[:, GROUPS - 1, :], ACT.Copy).then_inc(S["last_floats"], 1)
            act.wait_ge(S["scales_ready"], 5)
            for n in range(2 * GROUPS):
                nc.scalar.activation(pieces(fo_h)[:, n, :], pieces(gate)[:, n, :], ACT.Copy, scale=scal[:, K_O:K_O + 1]) \
                    .then_inc(S["o_high"], 1)
            with nc.scalar.Fori(0, GROUPS, 1) as g:
                for mo in range(DM_T):
                    act.wait_ge(S["down_done"], at(g, "down_done", mo + 1))
                    act.wait_ge(S["yt_transposed"], at(g, "yt_transposed", 0))
                    nc.scalar.activation(yt[:, mo, :], ps[:, mo, 0:GTOK], ACT.Copy, scale=scal[:, S_O:S_O + 1]) \
                        .then_inc(S["yt_ready"], 1)

        @block.tensor
        def _(pe):
            def mm(o, lhsT, rhs, start=True, stop=True):
                return nc.tensor.matmul(o, lhsT, rhs, start=start, stop=stop)

            def three_pass(o, parts, before=None):
                n = 0
                for m, (lh, ll, rh, rl) in enumerate(parts):
                    if before is not None:
                        before(m)
                    for a, b in ((lh, rl), (ll, rh), (lh, rh)):
                        n += 1
                        last = mm(o, a, b, start=(n == 1), stop=(n == 3 * len(parts)))
                return last

            def transpose_group(src, ready, group):
                for j in range(GROUP):
                    pe.wait_ge(S[ready], at(group, ready, j + 1))
                    for c in range(DM_T):
                        last = nc.tensor.transpose(ps[:, BANK_PJ + c, j * TOK:(j + 1) * TOK],
                                                   src[0:TOK, j, c * P:(c + 1) * P], ident[0:TOK, 0:TOK])
                return last

            def tok_transpose(i, t):
                pe.wait_ge(S["tok_normed"], at(i, "tok_normed", t + 1))
                pe.wait_ge(S["tok_evac"], at(i, "tok_evac", t - 1))
                for c in range(FEAT_T):
                    o = ps[:, 2 * t + c // 4, (c % 4) * P:(c % 4 + 1) * P]
                    last = nc.tensor.transpose(o, xnorm[:, t, c * P:(c + 1) * P], ident[:, :])
                last.then_inc(S["tok_transposed"], 1)

            def tok_turn(i, more):
                for t in range(2):
                    pe.wait_ge(S["tok_evac"], at(i, "tok_evac", t + 1))
                    pe.wait_ge(S["tok_y"], at(i, "tok_y", t - 1))
                    o = ps[:, 4 + t, 0:DM]
                    for c in range(FEAT_T):
                        mm(o, xnt[:, t, c, :], wp_g[:, c, :], start=(c == 0), stop=False)
                    mm(o, ones[0:1, :], bias_tok[:, :], start=False, stop=True).then_inc(S["tok_product"], 1)
                    if more:
                        tok_transpose(i + 1, t)
                    elif t == 0:
                        transpose_group(xn, "x_normed", 0).then_inc(S["x_transposed"], 1)

            pe.wait_ge(S["ident_ready"], 1)
            tok_transpose(0, 0)
            tok_transpose(0, 1)
            pe.wait_ge(S["wp_in"], 16)
            pe.wait_ge(S["cols_in"], 16)
            for c in range(FEAT_T):
                last = mm(ps[0:1, 7, 0:DM], b1_sb[:, c:c + 1], wp_sb[:, c, :], start=(c == 0), stop=(c == FEAT_T - 1))
            last.then_inc(S["bias_product"], 1)
            pe.wait_ge(S["tables_ready"], 2)
            with nc.tensor.Fori(0, TOK_TURNS - 1, 1) as i:
                tok_turn(i, True)
            tok_turn(TOK_TURNS - 1, False)
            pe.wait_ge(S["low_ready"], 2 * TOK_TURNS - 1)

            def fill_weights(fills):
                pe.wait_ge(S["q_done"], GROUPS)
                for r in fills:
                    if r >= 4:
                        pe.wait_ge(S["fw_low"], r - 3 if r < EARLY_FILLS else EARLY_FILLS)
                    for i in range(4):
                        if r < 2 * QT // 4:
                            c, t = r // (QT // 4), 4 * (r % (QT // 4)) + i
                            src = wq_gu[:, t, c * P:(c + 1) * P]
                        else:
                            m = 2 * (r - 2 * QT // 4) + i // 2
                            src = wq_dn[:, i % 2, m * P:(m + 1) * P]
                        last = nc.tensor.transpose(fill_view(r)[:, i * P:(i + 1) * P], src, ident[:, :])
                    last.then_inc(S["fw_transposed"], 1)

            def turn(g, now, prev, nxt):
                def freed(tenant):
                    what, a, k = tenant
                    if what == "x":
                        pe.wait_ge(S["xl_ready"], at(g + 1, "xl_ready", 1))
                    elif what == "x2":
                        pe.wait_ge(S["x2_copied"], at(g - 1, "x2_copied", 1))
                    elif what == "project":
                        pe.wait_ge(S["ot_ready"], at(g - 1, "ot_ready", a + 1))
                    elif what == "return":
                        pe.wait_ge(S["h_added"], at(g - 1, "h_added", a + 1))
                    elif k < UHEADS:
                        pe.wait_ge(S["roped"], at(g, "roped", UHEADS * a + k + 1))
                    else:
                        pe.wait_ge(S["v_ready"], at(g, "v_ready", GROUP * a + k - UHEADS + 1))

                def item(u, k):
                    if k < UHEADS:
                        col = (k // 2) * INNER + (2 * (u % UNITS) + k % 2) * P
                        last = three_pass(ps[:, item_bank(u, k), 0:GTOK], [
                            (wqkv_h[:, c, col:col + P], wqkv_l[:, c, col:col + P], xh[:, c, :], xl[:, c, :])
                            for c in range(DM_T)])
                    else:
                        j = k - UHEADS
                        t0, col = j * TOK, 2 * INNER + u % UNITS * UHEADS * HD
                        last = three_pass(ps[0:TOK, item_bank(u, k), 0:UHEADS * HD], [
                            (xh[:, c, t0:t0 + TOK], xl[:, c, t0:t0 + TOK],
                             wqkv_h[:, c, col:col + UHEADS * HD], wqkv_l[:, c, col:col + UHEADS * HD])
                            for c in range(DM_T)])
                    last.then_inc(S["proj_done"], 1)

                def scores(n):
                    u = n // 2
                    pe.wait_ge(S["qk_ready"], at(g, "qk_ready", UHEADS * (u + 1)))
                    pe.wait_ge(S["biased"], at(g, "biased", n))
                    for jj in range(2):
                        t0 = (2 * (n % 2) + jj) * TOK
                        for pair in range(2):
                            for e in range(2):
                                rows = slice(HD * e, HD * e + HD)
                                c0 = (2 * jj + pair) * TOK
                                last = mm(ps[0:TOK, BANK_S + e, c0:c0 + TOK], qk[rows, u % 2, pair, t0:t0 + TOK],
                                          qk[rows, u % 2, 2 + pair, t0:t0 + TOK])
                    last.then_inc(S["scores_done"], 1)

                def p_transpose(n):
                    pe.wait_ge(S["exped"], at(g, "exped", n + 1))
                    for jj in range(2):
                        pe.wait_ge(S["pt_ready"], at(g, "pt_ready", 2 * n + jj - 1))
                        for hh in range(UHEADS):
                            i = 4 * (hh % 2) + 2 * jj + hh // 2
                            last = nc.tensor.transpose(ps[0:TOK, BANK_PT + jj, hh * TOK:(hh + 1) * TOK],
                                                       pr[0:TOK, n % 2, i, :], ident[0:TOK, 0:TOK])
                        last.then_inc(S["p_transposed"], 1)

                def values(n):
                    u = n // 2
                    pe.wait_ge(S["v_ready"], at(g, "v_ready", GROUP * (u + 1)))
                    for jj in range(2):
                        j = 2 * (n % 2) + jj
                        pe.wait_ge(S["pt_ready"], at(g, "pt_ready", 2 * n + jj + 1))
                        pe.wait_ge(S["otl_ready"], at(g, "otl_ready", 2 * n + jj - 1))
                        for hh in range(UHEADS):
                            last = mm(ps[0:TOK, BANK_O + jj, hh * (HD + 1):(hh + 1) * (HD + 1)], pt[0:TOK, jj, hh, :],
                                      v[0:TOK, u % 2, j, hh, :])
                        last.then_inc(S["pv_done"], 1)

                def o_transpose(n):
                    for jj in range(2):
                        pe.wait_ge(S["o_normed"], at(g, "o_normed", 2 * n + jj + 1))
                        for c in range(2):
                            o = ps[:, BANK_O + jj, OT_AT + c * TOK:OT_AT + (c + 1) * TOK]
                            last = nc.tensor.transpose(o, on[0:TOK, jj, c * P:(c + 1) * P], ident[0:TOK, 0:TOK])
                        last.then_inc(S["o_transposed"], 1)

                def project(mo):
                    pe.wait_ge(S["low_ready"], 2 * TOK_TURNS)
                    pe.wait_ge(S["otl_ready"], at(g - 1, "otl_ready", 2 * STEPS))
                    three_pass(ps[:, ao_bank(mo), 0:GTOK], [
                        (wo_h[:, c, mo * P:(mo + 1) * P], wo_l[:, c, mo * P:(mo + 1) * P], oth[:, c, :], otl[:, c, :])
                        for c in range(INNER_T)]).then_inc(S["ao_done"], 1)

                def turn_back(b):
                    pe.wait_ge(S["ot_ready"], at(g - 1, "ot_ready", DM_T))
                    for jj in range(2):
                        for mo in range(DM_T):
                            c0, t0 = jj * DM + mo * P, (2 * b + jj) * TOK
                            last = nc.tensor.transpose(ps[0:TOK, ao_bank(b), c0:c0 + P], ot[:, mo, t0:t0 + TOK],
                                                       ident[:, :])
                    last.then_inc(S["ao_returned"], 1)

                both = (BANK_PJ, BANK_PJ + 1)
                held = {}
                if not now and nxt:
                    held = {b: ("x", 0, 0) for b in both}
                if now:
                    held = {item_bank(1, k): ("item", 1, k) for k in (0, 1)}

                def take(tenant):
                    what, a, k = tenant
                    b = item_bank(a, k) if what == "item" else ao_bank(a)
                    if b in held:
                        freed(held[b])
                    held[b] = tenant
                    if what == "item":
                        item(a, k)
                    else:
                        (project if what == "project" else turn_back)(a)

                for n in range(STEPS):
                    first_half, second_half = tenants(n, now, prev, nxt)
                    if has(n, now, prev):
                        scores(n)
                    for tenant in first_half[:FIRST]:
                        take(tenant)
                    if has(n - 2, now, prev):
                        o_transpose(n - 2)
                    if n == EARLY_SLOT + 1 and not now and prev:
                        fill_weights(range(EARLY_FILLS // 2, EARLY_FILLS))
                    for tenant in first_half[FIRST:]:
                        take(tenant)
                    if n == X_TURN and now and nxt:
                        for b in held:
                            freed(held[b])
                        transpose_group(xn, "x_normed", g + 1).then_inc(S["x_transposed"], 1)
                        held = {b: ("x", 0, 0) for b in both}
                    if has(n - 1, now, prev):
                        p_transpose(n - 1)
                    if has(n - 1, now, prev) and n == X_TURN:
                        values(n - 1)
                    for tenant in second_half:
                        take(tenant)
                    if has(n - 1, now, prev) and n != X_TURN:
                        values(n - 1)
                    if n == EARLY_SLOT and not now and prev:
                        fill_weights(range(EARLY_FILLS // 2))
                    if n == LATE_SLOT and not now and prev:
                        fill_weights(range(EARLY_FILLS, WFILLS))
                    if n == X2_TURN and prev:
                        for b in held:
                            freed(held[b])
                        transpose_group(xn2, "x2_normed", g - 1).then_inc(S["x2_transposed"], 1)
                        held = {b: ("x2", 0, 0) for b in both}

            turns(pe, turn)

            pe.wait_ge(S["fw_low"], EARLY_FILLS)

            for which in range(2):
                with nc.tensor.Fori(0, GROUPS, 1) as g:
                    if which == 0:
                        pe.wait_ge(S["fx_ready"], g + 1)
                    for half in range(2):
                        if which == 0 and half == 1:
                            pe.wait_ge(S["fw_low"], WFILLS)
                        pe.wait_ge(S["gu_copied"], 2 * g + (2 * GROUPS * which + half - 1 + SEEDS["gu_copied"]))
                        for b in range(3):
                            col = (which * FFN_T + 3 * half + b) * P
                            last = three_pass(ps[:, 3 * half + b, 0:GTOK], [
                                (wgu_h[:, c, col:col + P], wgu_l[:, c, col:col + P],
                                 fxh[:, c, bass.ts(g, GTOK)], fxl[:, c, bass.ts(g, GTOK)]) for c in range(DM_T)])
                        last.then_inc(S["gu_done"], 1)
            with nc.tensor.Fori(0, GROUPS, 1) as g:
                def half_ready(m):
                    if m % (FFN_T // 2) == 0:
                        pe.wait_ge(S["fo_ready"], 2 * g + (1 + m // (FFN_T // 2)))

                for mo in range(DM_T):
                    pe.wait_ge(S["yt_ready"], at(g, "yt_ready", mo + 1 - DM_T))
                    three_pass(ps[:, mo, 0:GTOK], [
                        (wdn_h[:, m, mo * P:(mo + 1) * P], wdn_l[:, m, mo * P:(mo + 1) * P],
                         fo_h[:, g, m * GTOK:(m + 1) * GTOK], fo_l[:, g, m * GTOK:(m + 1) * GTOK])
                        for m in range(FFN_T)], half_ready if mo == 0 else None).then_inc(S["down_done"], 1)
                pe.wait_ge(S["y_added"], at(g, "y_added", 0))
                for mo in range(DM_T):
                    pe.wait_ge(S["yt_ready"], at(g, "yt_ready", mo + 1))
                    for j in range(GROUP):
                        c0 = (j % 2) * DM + mo * P
                        last = nc.tensor.transpose(ps[0:TOK, 2 + j // 2, c0:c0 + P], yt[:, mo, j * TOK:(j + 1) * TOK],
                                                   ident[:, :])
                last.then_inc(S["yt_transposed"], 1)

        @block.vector
        def _(dve):
            V = nc.vector
            count = [0]

            def link(ins):
                count[0] += 1
                ins.then_inc(S["vstep"], 1)
                dve.wait_ge(S["vstep"], count[0])

            def patch_stats(a, b):
                for t in range(a, b):
                    for n, (first, _) in enumerate(LOADS):
                        if t == first:
                            dve.wait_ge(patches_in[n], 16 * (2 if n < len(LOADS) - 1 else 4))
                    for c in range(2):
                        last = V.bn_stats(stat1[:, t, c, :], xin[:, t, c * FEAT // 2:(c + 1) * FEAT // 2])
                link(last)
                for t in range(a, b):
                    last = V.bn_aggr(mv1[:, t, :], stat1[:, t, :, :].rearrange("p c s -> p (c s)"))
                link(last)
                V.tensor_scalar(mv1[:, a:b, 1], mv1[:, a:b, 1], EPS, None, ALU.add).then_inc(S["tok_stats"], 1)

            def patch_norm(i, t):
                dve.wait_ge(S["tok_transposed"], at(i, "tok_transposed", t - 1))
                V.tensor_scalar(xnorm[:, t, :], xin[:, 2 * i + t, :], mv1[:, bass.ds(2 * i + t, 1), 0],
                                rstd1[:, bass.ds(2 * i + t, 1)], ALU.subtract, ALU.mult).then_inc(S["tok_normed"], 1)

            patch_stats(0, 1)
            patch_stats(1, 2)
            for t in range(2):
                dve.wait_ge(S["tok_rstd"], t + 1)
                patch_norm(0, t)
            dve.wait_ge(S["cols_in"], 16)
            dve.wait_ge(S["wp_in"], 16)
            for c in range(FEAT_T):
                last = V.tensor_scalar(wp_g[:, c, :], wp_sb[:, c, :], g1_sb[:, c:c + 1], None, ALU.mult)
            last.then_inc(S["tables_ready"], 1)
            dve.wait_ge(S["iotas"], 2)
            dve.wait_ge(S["consts"], 3)
            for q in range(4):
                V.memset(sign[32 * q:32 * q + 32, :], 1.0 if q % 2 == 0 else -1.0)
            V.memset(gred[:, :], 0.0)
            link(V.tensor_copy(ang[:, 1, :], pos_i[:, :]))
            link(V.tensor_scalar(ang[:, 0, :], ang[:, 1, :], freq[:, 0:1], None, ALU.mult))
            link(V.tensor_scalar(ang[:, 1, :], ang[:, 0, :], 1.0 / TWO_PI, RINT, ALU.mult, ALU.add))
            link(V.tensor_scalar(ang[:, 1, :], ang[:, 1, :], RINT, None, ALU.subtract))
            for part in (PI_A, PI_B, PI_C):
                link(V.scalar_tensor_tensor(out=ang[:, 0, :], in0=ang[:, 1, :], scalar=-part, in1=ang[:, 0, :],
                                            op0=ALU.mult, op1=ALU.add))
            link(V.tensor_scalar(ang[:, 2, :], ang[:, 0, :], PI, -PI, ALU.min, ALU.max))
            link(V.tensor_scalar(ang[:, 3, :], ang[:, 0, :], TWO_PI / 4, None, ALU.add))
            link(V.tensor_scalar(ang[:, 1, :], ang[:, 3, :], PI, -TWO_PI, ALU.is_gt, ALU.mult))
            link(V.tensor_tensor(ang[:, 3, :], ang[:, 3, :], ang[:, 1, :], ALU.add))
            V.tensor_scalar(ang[:, 3, :], ang[:, 3, :], PI, -PI, ALU.min, ALU.max).then_inc(S["angles_ready"], 1)
            dve.wait_ge(S["rows_in"], 16)
            V.tensor_scalar(bias_as[:, :], bias_as[:, :], 0.01, None, ALU.max)
            V.tensor_scalar(bias_ps[:, :], bias_ps[:, :], 0.01, -1.0, ALU.max, ALU.mult)
            V.scalar_tensor_tensor(out=dist[:, :], in0=dist_i[:, :], scalar=-1.0, in1=dist_i[:, :], op0=ALU.mult,
                                   op1=ALU.max).then_inc(S["angles_ready"], 1)
            dve.wait_ge(S["bias_product"], 1)
            V.tensor_tensor(bias_tok[:, :], ps[0:1, 7, 0:DM], bp_sb[0:1, :], ALU.add).then_inc(S["tables_ready"], 1)
            patch_stats(2, 4)
            dve.wait_ge(S["tok_rstd"], 3)
            patch_norm(1, 0)
            patch_norm(1, 1)
            patch_stats(4, TOK_TILES)
            dve.wait_ge(S["sines_ready"], 1)
            link(V.tensor_scalar(ang[:, 2, :], ang[:, 2, :], sign[:, 0:1], None, ALU.mult))
            V.tensor_scalar(rope_s[:, 0, :], ang[:, 2, :], SCORE_SCALE, None, ALU.mult)
            V.tensor_copy(rope_s[:, 1, :], ang[:, 2, :])
            V.tensor_scalar(rope_c[:, 0, :], ang[:, 3, :], SCORE_SCALE, None, ALU.mult)
            V.tensor_copy(rope_c[:, 1, :], ang[:, 3, :])
            dve.wait_ge(S["logs_ready"], 1)
            V.tensor_tensor(kbias[0:TOK, :, :], kbias[0:TOK, :, :],
                            bias_ps[0:TOK, :].unsqueeze(2).broadcast_to([TOK, HEADS, TOK]), ALU.mult)
            dve.wait_ge(S["tok_rstd"], len(STAT_PARTS))

            def statistics(group, st, m, stats, first=0):
                for j in range(first, GROUP):
                    V.bn_stats(st[0:TOK, j, :], h[0:TOK, GROUP * group + j, :]).then_inc(S[stats], 1)
                dve.wait_ge(S[stats], at(group, stats, GROUP))
                V.memset(scal[:, 14:15], 0.0)
                for j in range(GROUP):
                    V.bn_aggr(m[0:TOK, j, :], st[0:TOK, j, :]).then_inc(S[stats], 1)
                dve.wait_ge(S[stats], at(group, stats, 2 * GROUP))
                V.tensor_scalar(m[0:TOK, :, 1], m[0:TOK, :, 1], EPS, None, ALU.add).then_inc(S[stats], 1)

            def norm(group, m, r, dst, rooted, normed):
                dve.wait_ge(S[rooted], at(group, rooted, 1))
                for j in range(GROUP):
                    V.tensor_scalar(dst[0:TOK, j, :], h[0:TOK, GROUP * group + j, :], m[0:TOK, j, 0:1],
                                    r[0:TOK, j:j + 1], ALU.subtract, ALU.mult).then_inc(S[normed], 1)

            def x_low(group):
                dve.wait_ge(S["xh_ready"], at(group, "xh_ready", 1))
                V.tensor_tensor(xl[:, :, :], ps[:, BANK_PJ:BANK_PJ + 2, 0:GTOK], xh[:, :, :].bitcast(F32),
                                ALU.subtract).then_inc(S["xl_ready"], 1)

            def tok_turn(i, more, ahead=False):
                for t in range(2):
                    if t == 1 and not more:
                        x_low(0)
                        split_low(V, wqkv_raw, wqkv_h, wqkv_l, TOK_TURNS - 1, 1, WPART)
                    dve.wait_ge(S["tok_y"], at(i, "tok_y", t + 1))
                    V.bn_stats(stat2[:, t, :], ytok[:, t, :]).then_inc(S["tok_stats2"], 1)
                    if ahead and t == 0:
                        patch_norm(i + 2, 0)
                dve.wait_ge(S["tok_stats2"], at(i, "tok_stats2", 2))
                V.memset(scal[:, 14:15], 0.0)
                for t in range(2):
                    V.bn_aggr(mv2[:, t, :], stat2[:, t, :]).then_inc(S["tok_stats2"], 1)
                dve.wait_ge(S["tok_stats2"], at(i, "tok_stats2", 4))
                V.tensor_scalar(mv2[:, :, 1], mv2[:, :, 1], EPS, None, ALU.add).then_inc(S["tok_stats2"], 1)
                for t in range(2):
                    V.scalar_tensor_tensor(out=ytok[:, t, :], in0=ytok[:, t, :], scalar=mv2[:, t, 0:1], in1=g2_sb,
                                           op0=ALU.subtract, op1=ALU.mult).then_inc(S["tok_scaled"], 1)
                dve.wait_ge(S["tok_rstd2"], at(i, "tok_rstd2", 1))
                dve.wait_ge(S["tok_scaled"], at(i, "tok_scaled", 2))
                hg = h[0:IMG_TOK, bass.ts(i, GROUP), :]
                for t in range(2):
                    for half in range(2):
                        rows_ = slice(SEAT * half, SEAT * half + IMG_TOK)
                        V.scalar_tensor_tensor(out=hg[:, 2 * t + half, :], in0=ytok[rows_, t, :],
                                               scalar=rstd2[rows_, t:t + 1], in1=b2_sb[rows_, :],
                                               op0=ALU.mult, op1=ALU.add).then_inc(S["tok_placed"], 1)
                if ahead:
                    patch_norm(i + 2, 1)

            with V.Fori(0, TOK_TURNS - 2, 1) as i:
                tok_turn(i, True, ahead=True)
            dve.wait_ge(S["txt_in"], 16)
            dve.wait_ge(S["tok_placed"], at(0, "tok_placed", 4))
            statistics(0, stat, mv, "ln_stats")
            tok_turn(TOK_TURNS - 2, True)
            norm(0, mv, rstd, xn, "ln_rstd", "x_normed")
            tok_turn(TOK_TURNS - 1, False)
            V.memset(xmax[:, :], 0.0).then_inc(S["prologue_v"], 1)
            dve.wait_ge(S["prologue_v"], 1)
            dve.wait_ge(S["prologue_a"], 1)
            dve.wait_ge(S["tok_placed"], at(TOK_TURNS, "tok_placed", 0))
            dve.wait_ge(S["ffnw_in"], 32)

            def low_weights(fills):
                for r in fills:
                    dve.wait_ge(S["fw_high"], r + 1)
                    V.tensor_tensor(weight_fill(wgu_l, wdn_l, r), fill_view(r),
                                    weight_fill(wgu_h, wdn_h, r).bitcast(F32), ALU.subtract).then_inc(S["fw_low"], 1)

            def turn(g, now, prev, nxt):
                def rope(u, k):
                    dve.wait_ge(S["proj_done"], at(g, "proj_done", ITEMS * u + k + 1))
                    swapped = f"swapped{u % 2}"
                    if k == 0:
                        dve.wait_ge(S[swapped], at(g, swapped, 64 * (u // 2)))
                        dve.wait_ge(S["scores_done"], at(g, "scores_done", 2 * (u - 1)))
                    src = steps_view(ps[:, item_bank(u, k), 0:GTOK], GROUP)
                    for table, dst in ((rope_s, rs), (rope_c, qk)):
                        t = table[:, k // 2, :].unsqueeze(1).broadcast_to([P, GROUP, TOK])
                        last = V.tensor_tensor(steps_view(dst[:, u % 2, k, :], GROUP), src, t, ALU.mult)
                    last.then_inc(S["roped"], 1)

                def bias_and_max(n):
                    dve.wait_ge(S["scores_done"], at(g, "scores_done", n + 1))
                    dve.wait_ge(S["exped"], at(g, "exped", n - 1))
                    u = n // 2
                    kb = kbias[0:TOK, UHEADS * u:UHEADS * (u + 1), :].rearrange("p (e q) x -> p e (q x)", e=2)
                    V.tensor_tensor(s[0:TOK, n % 2, :, :].rearrange("p (e j q) x -> p e j (q x)", e=2, j=2),
                                    ps[0:TOK, BANK_S:BANK_S + 2, 0:UHEADS * TOK].rearrange("p e (j x) -> p e j x", j=2),
                                    kb.unsqueeze(2).broadcast_to([TOK, 2, 2, 2 * TOK]), ALU.add) \
                        .then_inc(S["biased"], 1)
                    dve.wait_ge(S["biased"], at(g, "biased", n + 1))
                    V.tensor_reduce(nmax[0:TOK, n % 2, :], s[0:TOK, n % 2, :, :], axis=AXX, op=ALU.max, negate=True) \
                        .then_inc(S["maxed"], 1)

                def o_low(n):
                    for jj in range(2):
                        j = 2 * (n % 2) + jj
                        dve.wait_ge(S["oth_ready"], at(g, "oth_ready", 2 * n + jj + 1))
                        at_ = (slice(None), o_rows(n), slice(j * TOK, (j + 1) * TOK))
                        V.tensor_tensor(otl[at_], o_t_view(jj), oth[at_].bitcast(F32), ALU.subtract) \
                            .then_inc(S["otl_ready"], 1)

                def normalise(n):
                    for jj in range(2):
                        dve.wait_ge(S["pv_done"], at(g, "pv_done", 2 * n + jj + 1))
                        o = ps[0:TOK, BANK_O + jj, 0:UHEADS * (HD + 1)].rearrange("p (h x) -> p h x", h=UHEADS)
                        V.reciprocal(rsum[0:TOK, jj, :], o[:, :, HD]).then_inc(S["o_summed"], 1)
                        dve.wait_ge(S["o_summed"], at(g, "o_summed", 2 * n + jj + 1))
                        dve.wait_ge(S["o_transposed"], at(g, "o_transposed", 2 * n + jj - 1))
                        V.tensor_tensor(on[0:TOK, jj, :].rearrange("p (h x) -> p h x", h=UHEADS), o[:, :, 0:HD],
                                        rsum[0:TOK, jj, :].unsqueeze(2).broadcast_to([TOK, UHEADS, HD]), ALU.mult) \
                            .then_inc(S["o_normed"], 1)

                def residual(n, half):
                    what, b = AO_PLACES.get((n, half), ("", 0))
                    if what != "return" or not prev:
                        return
                    dve.wait_ge(S["ao_returned"], at(g - 1, "ao_returned", b + 1))
                    hb = h[0:TOK, bass.ds(GROUP * (g - 1) + 2 * b, 2), :].rearrange("p j d -> p (j d)")
                    V.tensor_tensor(hb, hb, ps[0:TOK, ao_bank(b), :], ALU.add).then_inc(S["h_added"], 1)
                    if not now and b == 0:
                        dve.wait_ge(S["h_added"], at(g - 1, "h_added", 1))
                        for j in range(2):
                            V.bn_stats(stat_f[0:TOK, j, :], h[0:TOK, GROUP * (g - 1) + j, :]) \
                                .then_inc(S["ln2_stats"], 1)

                def weight_scales():
                    V.tensor_reduce(qmax[:, :], q_blocks(g), axis=AXX, op=ALU.max, apply_absolute_value=True) \
                        .then_inc(S["q_max"], 1)
                    dve.wait_ge(S["q_max"], at(g, "q_max", 1))
                    V.tensor_scalar(qmax[:, :], qmax[:, :], 1.0 / WMAX, TINY, ALU.mult, ALU.max) \
                        .then_inc(S["q_max"], 1)
                    dve.wait_ge(S["q_max"], at(g, "q_max", 2))
                    V.reciprocal(qinv[:, :], qmax[:, :]).then_inc(S["q_max"], 1)

                def weight_integers():
                    part = wq[:, bass.ts(g, QPART)]
                    dve.wait_ge(S["q_scaled"], at(g, "q_scaled", 1))
                    V.tensor_scalar(part, part, RINT, RINT, ALU.add, ALU.subtract).then_inc(S["q_rounded"], 1)
                    dve.wait_ge(S["q_rounded"], at(g, "q_rounded", 1))
                    V.tensor_scalar(part, part, WMAX, -WMAX - 1.0, ALU.min, ALU.max).then_inc(S["q_rounded"], 1)

                def ropes(n, half):
                    for u, k in items_of(n, half, now, nxt):
                        if k < UHEADS:
                            rope(u, k)

                for n in range(STEPS):
                    if has(n, now, prev):
                        bias_and_max(n)
                    ropes(n, 0)
                    if has(n - 2, now, prev):
                        o_low(n - 2)
                    if n == EARLY_SLOT + 1 and not now and prev:
                        low_weights(range(EARLY_FILLS // 2, EARLY_FILLS))
                    residual(n, 0)
                    if n == X_NORM and now and nxt:
                        norm(g + 1, mv, rstd, xn, "ln_rstd", "x_normed")
                    if n == X2_NORM and prev:
                        norm(g - 1, mv_f, rstd_f, xn2, "ln2_rstd", "x2_normed")
                    if n == X2_MAX and prev:
                        dve.wait_ge(S["x2_normed"], at(g - 1, "x2_normed", GROUP))
                        V.tensor_reduce(xmax[0:TOK, bass.ds(g - 1, 1)], xn2[0:TOK, :, :].rearrange("p j d -> p (j d)"),
                                        axis=AXX, op=ALU.max, apply_absolute_value=True).then_inc(S["xmax_ready"], 1)
                    if n == X_TURN and now and nxt:
                        x_low(g + 1)
                    if n == X_TURN and has(n - 1, now, prev):
                        normalise(n - 1)
                    ropes(n, 1)
                    if n == Q_SCALE and now:
                        weight_scales()
                    if n == Q_ROUND and now:
                        weight_integers()
                    if n == X_STATS and now and nxt:
                        statistics(g + 1, stat, mv, "ln_stats")
                    residual(n, 1)
                    if has(n - 1, now, prev) and n != X_TURN:
                        normalise(n - 1)
                    if n == EARLY_SLOT and not now and prev:
                        low_weights(range(EARLY_FILLS // 2))
                    if n == X2_STATS and prev:
                        dve.wait_ge(S["h_added"], at(g - 1, "h_added", 2))
                        V.memset(scal[:, 13:14], 0.0)
                        statistics(g - 1, stat_f, mv_f, "ln2_stats", 0 if now else 2)

                if not now and nxt:
                    dve.wait_ge(S["roped"], at(g, "roped", UHEADS * (UNITS + 1)))
                    finish_rotation(V, g, UNITS)

            turns(dve, turn)

            def col(n):
                return scal[:, n:n + 1]

            def scale_of(n, unit, s_, k_):
                dve.wait_ge(S["max_shared"], n + 1)
                if unit is None:
                    link(V.tensor_scalar(col(s_), gall[:, n:n + 1], 1.0 / ACTMAX, TINY, ALU.mult, ALU.max))
                    V.reciprocal(col(k_), col(s_)).then_inc(S["scales_ready"], 1)
                else:
                    link(V.tensor_scalar(col(s_), gall[:, n:n + 1], col(unit), 1.0 / ACTMAX, ALU.mult, ALU.mult))
                    link(V.tensor_scalar(col(s_), col(s_), TINY, None, ALU.max))
                    link(V.reciprocal(col(SCRATCH), col(s_)))
                    V.tensor_scalar(col(k_), col(SCRATCH), col(unit), None, ALU.mult).then_inc(S["scales_ready"], 1)

            dve.wait_ge(S["xmax_ready"], GROUPS)
            V.tensor_reduce(gred[:, 0:1], xmax[:, :], axis=AXX, op=ALU.max).then_inc(S["max_ready"], 1)
            scale_of(0, None, S_X, I_X)
            for g in range(GROUPS):
                if g == 1:
                    low_weights(range(EARLY_FILLS, WFILLS))
                dve.wait_ge(S["fx_high"], g + 1)
                dve.wait_ge(S["fx_rounded"], g + 1)
                V.tensor_tensor(fxl[:, :, of(g)], x_i[:, :, of(g)], fxh[:, :, of(g)].bitcast(F32), ALU.subtract) \
                    .then_inc(S["fx_ready"], 1)

            def gu_max(which, g, half):
                dve.wait_ge(S["gu_done"], 2 * g + (2 * GROUPS * which + half + 1))
                V.tensor_reduce(maxes[:, which, bass.ds(2 * g + half, 1)], ps[:, 3 * half:3 * half + 3, 0:GTOK],
                                axis=mybir.AxisListType.XY, op=ALU.max, apply_absolute_value=True) \
                    .then_inc(S["gu_maxed"], 1)

            def all_max(n, cols):
                V.tensor_reduce(gred[:, n:n + 1], maxes[:, n - 1, 0:cols], axis=AXX, op=ALU.max) \
                    .then_inc(S["max_ready"], 1)

            with V.Fori(0, GROUPS, 1) as g:
                gu_max(0, g, 0)
                gu_max(0, g, 1)
            dve.wait_ge(S["gu_maxed"], 2 * GROUPS)
            all_max(1, 2 * GROUPS)
            scale_of(1, S_X, S_GATE, K_GATE)
            def gated(g):
                dve.wait_ge(S["sig_rounded"], g + 1)
                V.scalar_tensor_tensor(out=gate[:, g, :], in0=sig_i[:, bass.ds(g % 2, 1), :], scalar=SIGLEVELS - 1.0,
                                       in1=gate_i[:, g, :], op0=ALU.min, op1=ALU.mult).then_inc(S["g2_ready"], 1)

            def gated_max(g):
                dve.wait_ge(S["g2_ready"], at(g, "g2_ready", 1))
                V.tensor_reduce(maxes[:, 2, bass.ds(g, 1)], gate[:, g, :], axis=AXX, op=ALU.max,
                                apply_absolute_value=True).then_inc(S["g2_maxed"], 1)

            link(V.tensor_scalar(col(U_G2), col(S_GATE), 1.0 / SIGLEVELS, None, ALU.mult))
            gu_max(1, 0, 0)
            gu_max(1, 0, 1)
            with V.Fori(1, GROUPS, 1) as g:
                gu_max(1, g, 0)
                gated(g - 1)
                gu_max(1, g, 1)
                gated_max(g - 1)
            dve.wait_ge(S["gu_maxed"], 4 * GROUPS)
            all_max(2, 2 * GROUPS)
            gated(GROUPS - 1)
            scale_of(2, S_X, S_UP, K_UP)
            gated_max(GROUPS - 1)
            dve.wait_ge(S["g2_maxed"], GROUPS)
            all_max(3, GROUPS)
            scale_of(3, U_G2, S_G2, K_G2)
            dve.wait_ge(S["scales_ready"], 4)
            link(V.tensor_scalar(gate_i[:, 0, :], gate[:, 0, :], col(K_G2), None, ALU.mult))

            def product(g):
                dve.wait_ge(S["up_rounded"], g + 1)
                V.tensor_tensor(gate[:, g, :], gate_i[:, g, :], up_i[:, g, :], ALU.mult).then_inc(S["o_ready"], 1)
                dve.wait_ge(S["o_ready"], g + 1)
                V.tensor_reduce(maxes[:, 3, bass.ds(g, 1)], gate[:, g, :], axis=AXX, op=ALU.max,
                                apply_absolute_value=True).then_inc(S["o_maxed"], 1)

            product(0)
            with V.Fori(1, GROUPS - 1, 1) as g:
                dve.wait_ge(S["g2_rounded"], g)
                product(g)
            dve.wait_ge(S["last_product"], 1)
            V.tensor_reduce(maxes[:, 3, GROUPS - 1:GROUPS], gate[:, GROUPS - 1, :], axis=AXX, op=ALU.max,
                            apply_absolute_value=True).then_inc(S["o_maxed"], 1)
            dve.wait_ge(S["o_maxed"], GROUPS)
            all_max(4, GROUPS)
            link(V.tensor_tensor(col(U_O), col(S_G2), col(S_UP), ALU.mult))
            scale_of(4, U_O, S_O, K_O)
            with V.Fori(0, 2 * GROUPS, 1) as n:
                dve.wait_ge(S["o_high"], n + 1)
                dve.wait_ge(S["o_rounded"], n + 1)
                V.tensor_tensor(pieces(fo_l)[:, n, :], pieces(up_i)[:, n, :], pieces(fo_h)[:, n, :].bitcast(F32),
                                ALU.subtract) \
                    .then_inc(S["fo_ready"], 1)
            with V.Fori(0, GROUPS, 1) as g:
                dve.wait_ge(S["yt_transposed"], at(g, "yt_transposed", 1))
                hg = h[0:TOK, bass.ts(g, GROUP), :].rearrange("p j d -> p (j d)").rearrange("p (b x) -> p b x", b=2)
                V.tensor_tensor(hg, hg, ps[0:TOK, 2:4, :], ALU.add).then_inc(S["y_added"], 1)


S_X, I_X, S_GATE, K_GATE, S_UP, K_UP, U_G2, S_G2, K_G2, U_O, S_O, K_O, SCRATCH = range(13)
OT_AT = 264
WFILLS = 2 * QT // 4 + FFN_T // 2


def kernel(x, txt, L0_tok_Wp, L0_tok_bp, L0_tok_ln1_g, L0_tok_ln1_b, L0_tok_ln2_g, L0_tok_ln2_b, L0_attn_qkv_w,
           L0_attn_out_w, L0_attn_bias_p, L0_attn_bias_a, L0_attn_rope_freqs, L0_ffn_w_gate, L0_ffn_w_up,
           L0_ffn_w_down):
    import concourse.bacc as bacc
    from concourse.bass_utils import run_bass_kernel_spmd

    def lay(a, *shape):
        return np.ascontiguousarray(np.asarray(a).reshape(shape))

    patches = np.asarray(x).reshape(BATCHES, CHANNELS, SIDE, PATCH, SIDE, PATCH).transpose(0, 2, 4, 3, 5, 1)

    def by_unit(a):
        return lay(np.asarray(a).reshape(UNITS, 2, 2).transpose(0, 2, 1), 1, HEADS)

    arrays = dict(
        patches=lay(patches, BATCHES, IMG_TOK, FEAT),
        txt=lay(txt, BATCHES, TXT_TOK, DM),
        wp=lay(L0_tok_Wp, FEAT, DM),
        cols=np.concatenate([lay(L0_tok_ln1_g, FEAT_T, P).T, lay(L0_tok_ln1_b, FEAT_T, P).T,
                             np.tile(lay(L0_attn_rope_freqs, HALF, 1), (P // HALF, 1))], axis=1),
        rows=np.concatenate([lay(L0_tok_bp, 1, DM), lay(L0_tok_ln2_g, 1, DM), lay(L0_tok_ln2_b, 1, DM),
                             by_unit(L0_attn_bias_p), by_unit(L0_attn_bias_a)], axis=1),
        wqkv=np.ascontiguousarray(np.asarray(L0_attn_qkv_w).T),
        wo=np.ascontiguousarray(np.asarray(L0_attn_out_w).T),
        wgu=np.concatenate([np.asarray(L0_ffn_w_gate), np.asarray(L0_ffn_w_up)]),
        wdn=lay(L0_ffn_w_down, DM, FFN),
    )
    arrays = {name: np.ascontiguousarray(a) for name, a in arrays.items()}
    nc = bacc.Bacc("TRN2", target_bir_lowering=False, num_devices=1)
    args = [nc.dram_tensor(name, a.shape, mybir.dt.from_np(a.dtype), kind="ExternalInput").ap()
            for name, a in arrays.items()]
    args.append(nc.dram_tensor("out", (BATCHES, TOK, DM), F32, kind="ExternalOutput").ap())
    build(nc, *args)
    r = run_bass_kernel_spmd(nc, [arrays], core_ids=[0])
    return r.results[0]["out"]
```
